# Optimizing a Trainium2 kernel written in Bass

```python
import numpy as np
import jax
import jax.numpy as jnp

def _softmax(x, axis=-1):
    return jax.nn.softmax(x, axis=axis)

def _gelu(x):
    return jax.nn.gelu(x, approximate=True)

def _silu(x):
    return jax.nn.silu(x)

def _sigmoid(x):
    return jax.nn.sigmoid(x)

def _layernorm(x, axis=-1, eps=1e-05):
    m = jnp.mean(x, axis=axis, keepdims=True)
    v = jnp.var(x, axis=axis, keepdims=True)
    return (x - m) / jnp.sqrt(v + eps)

def _scatter_add(tgt, idx, src, axis=0):
    return tgt.at[idx].add(src)

def _segment_sum(src, seg, n):
    return jax.ops.segment_sum(src, seg, n)
kernel_name = 'mk_hybrid_d1_jaxref_r4_a2e620'

def setup_inputs(seed: int=0):
    np.random.seed(seed)
    _w = jnp.asarray

    def _L0_attn_a_setup():
        import jax, jax.numpy as jnp
        import numpy as np
        N_HEADS = 16
        EPS = 1e-06

        def _feature_map(x):
            return jax.nn.elu(x) + 1.0
        key = jax.random.key(seed)
        k1, k2, k3 = jax.random.split(key, 3)
        B, S, D = (1, 512, 256)
        x = jax.random.normal(k1, (B, S, D), dtype=jnp.float32)
        causal_mask = jnp.tril(jnp.ones((S, S), dtype=bool))[None, None]
        W_qkv = jax.random.normal(k2, (D, 3 * D), dtype=jnp.float32) / np.sqrt(D)
        W_out = jax.random.normal(k3, (D, D), dtype=jnp.float32) / np.sqrt(D)
        return {'x': x, 'causal_mask': causal_mask, 'W_qkv': W_qkv, 'W_out': W_out}
    _L0_attn_a_in = _L0_attn_a_setup()

    def _L0_attn_b_setup():
        import jax, jax.numpy as jnp
        import numpy as np
        import math
        B, S, DIM = (2, 512, 256)
        H, KVH = (16, 4)
        HD = DIM // H
        WINDOW = 64
        ROPE_BASE = 10000.0
        EPS = 1e-06

        def _rms_norm(v):
            return v * jax.lax.rsqrt(jnp.mean(v * v, axis=-1, keepdims=True) + EPS)

        def _rope_tables(seqlen, dtype):
            inv_freq = 1.0 / ROPE_BASE ** (jnp.arange(0, HD, 2, dtype=jnp.float32) / HD)
            t = jnp.arange(seqlen, dtype=jnp.float32)
            freqs = jnp.outer(t, inv_freq)
            return (jnp.cos(freqs).astype(dtype)[None, None], jnp.sin(freqs).astype(dtype)[None, None])

        def _apply_rotary(v, cos, sin):
            half = v.shape[-1] // 2
            v1, v2 = (v[..., :half], v[..., half:])
            return jnp.concatenate((v1 * cos + v2 * sin, -v1 * sin + v2 * cos), axis=-1)
        key = jax.random.key(seed)
        ks = jax.random.split(key, 6)
        s = 0.02
        return {'x': jax.random.normal(ks[0], (B, S, DIM), jnp.float32), 'Wq': jax.random.normal(ks[1], (DIM, DIM), jnp.float32) * s, 'Wk': jax.random.normal(ks[2], (KVH * HD, DIM), jnp.float32) * s, 'Wv': jax.random.normal(ks[3], (KVH * HD, DIM), jnp.float32) * s, 'Wo': jax.random.normal(ks[4], (DIM, DIM), jnp.float32) * s, 'q_gain': jnp.ones((H,), jnp.float32), 'pair_mix': jnp.tile(jnp.eye(2, dtype=jnp.float32), (H // 2, 1, 1)) + 0.01 * jax.random.normal(ks[5], (H // 2, 2, 2), jnp.float32)}
    _L0_attn_b_in = _L0_attn_b_setup()

    def _L0_ffn_setup():
        import jax, jax.numpy as jnp
        import numpy as np
        EPS = 1e-05

        def _quantize(W):
            gamma = jnp.mean(jnp.abs(W))
            return jnp.clip(jnp.round(W / (gamma + EPS)), -1.0, 1.0)
        key = jax.random.key(seed)
        k_x, k_w1, k_b1, k_w2, k_b2 = jax.random.split(key, 5)
        n_embd = 256
        d_ff = 4 * n_embd
        B, S = (4, 1024)
        bound1 = 1.0 / np.sqrt(n_embd)
        bound2 = 1.0 / np.sqrt(d_ff)
        x = jax.random.normal(k_x, (B, S, n_embd), dtype=jnp.float32)
        W1 = jax.random.uniform(k_w1, (d_ff, n_embd), jnp.float32, -bound1, bound1)
        b1 = jax.random.uniform(k_b1, (d_ff,), jnp.float32, -bound1, bound1)
        W2 = jax.random.uniform(k_w2, (n_embd, d_ff), jnp.float32, -bound2, bound2)
        b2 = jax.random.uniform(k_b2, (n_embd,), jnp.float32, -bound2, bound2)
        return {'x': x, 'W1': W1, 'b1': b1, 'W2': W2, 'b2': b2}
    _L0_ffn_in = _L0_ffn_setup()
    _d = {'L0_attn_a_x': _L0_attn_a_in['x'], 'L0_attn_a_causal_mask': _L0_attn_a_in['causal_mask'], 'L0_attn_a_W_qkv': _L0_attn_a_in['W_qkv'], 'L0_attn_a_W_out': _L0_attn_a_in['W_out'], 'L0_attn_b_Wq': _L0_attn_b_in['Wq'], 'L0_attn_b_Wk': _L0_attn_b_in['Wk'], 'L0_attn_b_Wv': _L0_attn_b_in['Wv'], 'L0_attn_b_Wo': _L0_attn_b_in['Wo'], 'L0_attn_b_q_gain': _L0_attn_b_in['q_gain'], 'L0_attn_b_pair_mix': _L0_attn_b_in['pair_mix'], 'L0_ffn_W1': _L0_ffn_in['W1'], 'L0_ffn_b1': _L0_ffn_in['b1'], 'L0_ffn_W2': _L0_ffn_in['W2'], 'L0_ffn_b2': _L0_ffn_in['b2']}
    _x0 = _d['L0_attn_a_x']
    _d['L0_attn_a_x'] = jax.random.normal(jax.random.fold_in(jax.random.key(seed), 1), (32, 512, 256), dtype=_x0.dtype)
    del _x0
    return _d

def reference(L0_attn_a_x, L0_attn_a_causal_mask, L0_attn_a_W_qkv, L0_attn_a_W_out, L0_attn_b_Wq, L0_attn_b_Wk, L0_attn_b_Wv, L0_attn_b_Wo, L0_attn_b_q_gain, L0_attn_b_pair_mix, L0_ffn_W1, L0_ffn_b1, L0_ffn_W2, L0_ffn_b2):

    def _L0_attn_a_ref(x, causal_mask, W_qkv, W_out):
        import jax, jax.numpy as jnp
        import numpy as np
        N_HEADS = 16
        EPS = 1e-06

        def _feature_map(x):
            return jax.nn.elu(x) + 1.0
        B, S, D = x.shape
        H = N_HEADS
        hd = D // H
        qkv = x @ W_qkv
        q, k, v = jnp.split(qkv, 3, axis=-1)

        def to_heads(t):
            return t.reshape(B, S, H, hd).transpose(0, 2, 1, 3)
        q, k, v = (to_heads(q), to_heads(k), to_heads(v))
        phi_q = _feature_map(q)
        phi_k = _feature_map(k)
        k_cum = jnp.cumsum(phi_k, axis=2)
        kv = jnp.einsum('bhsi,bhsj->bhsij', phi_k, v)
        kv_cum = jnp.cumsum(kv, axis=2)
        numer = jnp.einsum('bhsi,bhsij->bhsj', phi_q, kv_cum)
        denom = jnp.einsum('bhsi,bhsi->bhs', phi_q, k_cum) + EPS
        attn_out = numer / denom[..., None]
        attn_out = attn_out.transpose(0, 2, 1, 3).reshape(B, S, D)
        return attn_out @ W_out

    def _L0_attn_b_ref(x, Wq, Wk, Wv, Wo, q_gain, pair_mix):
        import jax, jax.numpy as jnp
        import numpy as np
        import math
        B, S, DIM = (2, 512, 256)
        H, KVH = (16, 4)
        HD = DIM // H
        WINDOW = 64
        ROPE_BASE = 10000.0
        EPS = 1e-06

        def _rms_norm(v):
            return v * jax.lax.rsqrt(jnp.mean(v * v, axis=-1, keepdims=True) + EPS)

        def _rope_tables(seqlen, dtype):
            inv_freq = 1.0 / ROPE_BASE ** (jnp.arange(0, HD, 2, dtype=jnp.float32) / HD)
            t = jnp.arange(seqlen, dtype=jnp.float32)
            freqs = jnp.outer(t, inv_freq)
            return (jnp.cos(freqs).astype(dtype)[None, None], jnp.sin(freqs).astype(dtype)[None, None])

        def _apply_rotary(v, cos, sin):
            half = v.shape[-1] // 2
            v1, v2 = (v[..., :half], v[..., half:])
            return jnp.concatenate((v1 * cos + v2 * sin, -v1 * sin + v2 * cos), axis=-1)
        bsz, seqlen, dim = x.shape
        q = (x @ Wq.T).reshape(bsz, seqlen, H, HD).transpose(0, 2, 1, 3)
        k = (x @ Wk.T).reshape(bsz, seqlen, KVH, HD).transpose(0, 2, 1, 3)
        v = (x @ Wv.T).reshape(bsz, seqlen, KVH, HD).transpose(0, 2, 1, 3)
        q = _rms_norm(q)
        k = _rms_norm(k)
        cos, sin = _rope_tables(seqlen, q.dtype)
        q = _apply_rotary(q, cos, sin)
        k = _apply_rotary(k, cos, sin)
        q = q * q_gain.astype(q.dtype)[None, :, None, None]
        rep = H // KVH
        k_full = jnp.repeat(k, rep, axis=1)
        v_full = jnp.repeat(v, rep, axis=1)
        pos = jnp.arange(seqlen)
        mask = (pos[:, None] >= pos[None, :]) & (pos[:, None] - pos[None, :] < WINDOW)
        scale = 1.0 / math.sqrt(HD)
        scores = jnp.einsum('bhqd,bhkd->bhqk', q, k_full) * scale
        scores = jnp.where(mask[None, None], scores, jnp.finfo(scores.dtype).min)
        att = jax.nn.softmax(scores, axis=-1)
        y = jnp.einsum('bhqk,bhkd->bhqd', att, v_full)
        yp = y.reshape(bsz, H // 2, 2, seqlen, HD)
        y = jnp.einsum('bpitd,poi->bpotd', yp, pair_mix.astype(y.dtype)).reshape(bsz, H, seqlen, HD)
        out = y.transpose(0, 2, 1, 3).reshape(bsz, seqlen, dim) @ Wo.T
        return out

    def _L0_ffn_ref(x, W1, b1, W2, b2):
        import jax, jax.numpy as jnp
        import numpy as np
        EPS = 1e-05

        def _quantize(W):
            gamma = jnp.mean(jnp.abs(W))
            return jnp.clip(jnp.round(W / (gamma + EPS)), -1.0, 1.0)
        Wq1 = _quantize(W1)
        Wq2 = _quantize(W2)
        h = jax.nn.relu(jnp.einsum('bsd,fd->bsf', x, Wq1) + b1)
        out = jnp.einsum('bsf,df->bsd', h, Wq2) + b2
        return out
    x = L0_attn_a_x
    x = x + _L0_attn_a_ref(_layernorm(x, axis=-1), L0_attn_a_causal_mask, L0_attn_a_W_qkv, L0_attn_a_W_out)
    x = x + _L0_ffn_ref(_layernorm(x, axis=-1), L0_ffn_W1, L0_ffn_b1, L0_ffn_W2, L0_ffn_b2)
    x = x + _L0_attn_b_ref(_layernorm(x, axis=-1), L0_attn_b_Wq, L0_attn_b_Wk, L0_attn_b_Wv, L0_attn_b_Wo, L0_attn_b_q_gain, L0_attn_b_pair_mix)
    x = x + _L0_ffn_ref(_layernorm(x, axis=-1), L0_ffn_W1, L0_ffn_b1, L0_ffn_W2, L0_ffn_b2)
    return x

_drawn_inputs = setup_inputs


def setup_inputs(seed=0):
    import zlib

    import numpy as np

    out = dict(_drawn_inputs(seed))
    spreads = {'L0_attn_b_q_gain': (1.0, 0.6)}
    factors = {'L0_attn_b_Wq': 8.0,
     'L0_attn_b_Wk': 8.0,
     'L0_attn_b_Wv': 8.0,
     'L0_attn_b_Wo': 8.0,
     'L0_attn_b_pair_mix': 8.0,
     'L0_ffn_b1': 8.0,
     'L0_ffn_b2': 8.0}
    for name, (base, spread) in spreads.items():
        noise = np.random.default_rng([zlib.crc32(name.encode()), seed]).standard_normal(out[name].shape)
        drawn = base * np.exp(spread * noise) if base else spread * noise
        out[name] = jnp.asarray(drawn.astype(out[name].dtype))
    for name, factor in factors.items():
        out[name] = (out[name] * factor).astype(out[name].dtype)
    return out
```

```python
from contextlib import ExitStack

import numpy as np

import concourse.bass as bass
from concourse import mybir

ALU = mybir.AluOpType
ACT = mybir.ActivationFunctionType
X = mybir.AxisListType.X
F32 = mybir.dt.float32
F32R = mybir.dt.float32r
BF16 = mybir.dt.bfloat16

P = 128
NSEQ, S, D = 32, 512, 256
NT = S // P
KB = D // P
H, HD = 16, 16
HB = H // KB
HV = HD + 1
FF = 4 * D
FB = FF // P
KVH = 4
REP = H // KVH
W = 64
NBL = S // W
QK = (H + KVH) * HD
NB = QK + KVH * HD
SLOT = 4 * HD
LN_EPS, A_EPS, RMS_EPS, Q_EPS = 1e-5, 1e-6, 1e-6, 1e-5
MASKED = -1e30

_WIDTHS = dict(ident=P, causal=P, heads=HB * HV, parity=2, kodd=W, keven=W, qodd=P, qeven=P,
               cos=NT * HD, sin=NT * HD)
COL, _at = {}, 0
for _name, _w in _WIDTHS.items():
    COL[_name] = (_at, _at + _w)
    _at += _w
NCONST = _at


def constants():
    c = np.zeros((P, NCONST), np.float32)

    def put(name, value):
        c[:, COL[name][0]:COL[name][1]] = np.asarray(value, np.float32).reshape(P, -1)

    p, q = np.arange(P)[:, None], np.arange(P)[None, :]
    put("ident", p == q)
    put("causal", p <= q)
    head = np.repeat(np.arange(HB), HV)[None, :]
    put("heads", p // HD == head)
    put("parity", (p // HD) % 2 == np.arange(2)[None, :])
    k, qq = np.arange(P)[:, None], np.arange(W)[None, :]
    odd = np.where(k < W, qq < k, k - W <= qq)
    even = np.where(k < W, k <= qq, qq < k - W)
    put("kodd", np.where(odd, 0.0, MASKED))
    put("keven", np.where(even, 0.0, MASKED))
    put("qodd", np.where(np.tile(odd.T, (2, 1)), 0.0, MASKED))
    put("qeven", np.where(np.tile(even.T, (2, 1)), 0.0, MASKED))
    inv = (1.0 / np.float32(10000.0) ** (np.arange(0, HD, 2, dtype=np.float32) / HD)).astype(np.float32)
    ang = np.outer(np.arange(S, dtype=np.float32), inv)
    cos, sin = np.cos(ang).astype(np.float32), np.sin(ang).astype(np.float32)
    table = lambda a, b: np.concatenate([a, b], 1).reshape(NT, P, HD).transpose(1, 0, 2)
    put("cos", table(cos, cos))
    put("sin", table(sin, -sin))
    return c


def needed(value):
    return not isinstance(value, int) or value > 0


def build(nc, x, w_qkv, w_out, w_b, wo_b, gain, mix, w1, b1, w2, b2, const, out):
    with ExitStack() as ctx:
        def sb(name, shape, dt=F32):
            return ctx.enter_context(nc.sbuf_tensor(name, shape, dt))

        def sem(name):
            return ctx.enter_context(nc.semaphore(name))

        cst = sb("cst", [P, NCONST])
        C = {n: cst[:, a:b] for n, (a, b) in COL.items()}
        ident, causal = C["ident"], C["causal"]
        ident_b = sb("ident_b", [P, P], BF16)
        neg_ident = sb("neg_ident", [P, P], F32R)
        ident_r = sb("ident_r", [P, P], F32R)
        kmask = sb("kmask", [P, 2, W], BF16)
        qmask = sb("qmask", [P, 2, P], BF16)
        wqkv_h, wqkv_l = (sb(f"wqkv_{n}", [P, KB, 3 * D], F32R) for n in "hl")
        wout_h, wout_l = (sb(f"wout_{n}", [P, KB, D], F32R) for n in "hl")
        wb_h, wb_l = (sb(f"wb_{n}", [P, KB, NB], F32R) for n in "hl")
        wob_h, wob_l = (sb(f"wob_{n}", [P, 2, D], F32R) for n in "hl")
        w1t = sb("w1t", [P, KB, FF], F32R)
        w2t = sb("w2t", [P, FB, D], F32R)
        b1c = sb("b1c", [P, FB])
        b2f = sb("b2f", [1, D])
        b2_h, b2_l = sb("b2_h", [1, D], F32R), sb("b2_l", [1, D], F32R)
        ones_f = sb("ones_f", [P, P])
        ones_r = sb("ones_r", [1, P], F32R)
        gains = sb("gains", [P, H + KVH])
        mixc = sb("mixc", [P, 4])
        mhalf = sb("mhalf", [P, H + KVH])
        gsum = sb("gsum", [P, 2])
        thr = sb("thr", [P, 4])

        x0, x1, x2, x3 = (sb(f"x{n}", [P, NT, D]) for n in range(4))

        class Norm:
            def __init__(self, n):
                self.st = sb(n + "st", [P, NT, 6])
                self.mv = sb(n + "mv", [P, NT, 2])
                self.tmp = sb(n + "tmp", [P, 3, NT])
                self.rstd = sb(n + "rstd", [P, NT])
                self.xn = sb(n + "xn", [P, NT, D])
                self.xh = sb(n + "xh", [P, KB, S], F32R)
                self.xl = sb(n + "xl", [P, KB, S], F32R)
                self.bn = sem(n + "bn_stats_done")
                self.stats = sem(n + "mean_var_ready")
                self.chain = sem(n + "rstd_steps")
                self.ready = sem(n + "rstd_ready")
                self.normed = sem(n + "normed")
                self.turned = sem(n + "transposed")
                self.hi = sem(n + "hi_ready")
                self.lo = sem(n + "lo_ready")

        at, ff = Norm("at_"), Norm("ff_")

        f_r = sb("f_r", [P, 2, S])
        f_hh = sb("f_hh", [P, 2, S], F32R)
        f_hl = sb("f_hl", [P, 2, S], F32R)

        a_ek = sb("a_ek", [P, 2, D])
        a_eq = sb("a_eq", [P, 2, S])
        a_kt = sb("a_kt", [P, NT - 1, D])
        a_v = sb("a_v", [P, NT, H, HV])
        a_qT = sb("a_qT", [P, KB, S])
        a_kT = sb("a_kT", [P, KB, S])
        a_qz = sb("a_qz", [P, KB, 2, S])
        a_s = sb("a_s", [P, 2, 4, S])
        a_state = sb("a_state", [P, 2, KB * HB * HV])
        a_den = sb("a_den", [P, 2, H])
        a_y = sb("a_y", [P, D])
        a_yh, a_yl = sb("a_yh", [P, KB, P], F32R), sb("a_yl", [P, KB, P], F32R)

        b_sq = sb("b_sq", [P, QK])
        b_ss = sb("b_ss", [P, H + KVH])
        b_tmp = sb("b_tmp", [P, 3, H + KVH])
        b_rs = sb("b_rs", [P, H + KVH])
        b_qn = sb("b_qn", [P, 2, H + KVH, HD])
        b_rc = sb("b_rc", [P, H + KVH, HD])
        b_rsn = sb("b_rsn", [P, H + KVH, HD])
        b_qr = sb("b_qr", [P, 2, H + KVH, HD])
        b_qs = sb("b_qs", [P, H, 4, HD], F32R)
        b_ks = sb("b_ks", [P, KVH, 4, HD], F32R)
        b_qT = sb("b_qT", [P, 2, NBL, REP * W], F32R)
        b_kT = sb("b_kT", [P, 2, S], F32R)
        b_kTm = sb("b_kTm", [P, 2, NT, P], F32R)
        b_v = sb("b_v", [P, NT, KVH, HV])
        b_vm = sb("b_vm", [P, NT, KVH, HV])
        b_m = sb("b_m", [P, 2, 2 * 4], F32R)
        b_p = sb("b_p", [P, 2, 2, S])
        b_den = sb("b_den", [P, 2 * KVH])
        b_y = sb("b_y", [P, 2, P])
        b_yh, b_yl = sb("b_yh", [P, 2, P], F32R), sb("b_yl", [P, 2, P], F32R)

        Q = [ctx.enter_context(nc.psum_tensor(f"Q{n}", [P, S], F32)) for n in range(4)]
        HID = [ctx.enter_context(nc.psum_tensor(f"HID{n}", [P, S], F32)) for n in range(2)]
        Y = [ctx.enter_context(nc.psum_tensor(f"Y{n}", [P, S], F32)) for n in range(2)]

        st_a = a_s[:, 0].rearrange("p a n -> p (a n)")
        st_w1 = a_s[:, 1].rearrange("p a n -> p (a n)")
        st_w2 = a_qz[:, :].rearrange("p a b n -> p (a b n)")
        st_b = b_p[:, :].rearrange("p a b n -> p (a b n)")

        loaded, setup, setup_pe, prepared, ones_set = (sem(n) for n in (
            "weights_loaded", "setup_steps", "abs_sum_ready", "weights_prepared", "constants_set"))
        pool_gate, dve_gate = sem("pool_gate"), sem("dve_gate")
        x_in, stored = sem("x_loaded"), sem("x_stored")
        f_h, f_rr, f_act, f_lo, f_w2, f_out = (sem(n) for n in (
            "f_hidden_ready", "f_relu_ready", "f_hi_ready", "f_lo_ready", "f_down_done", "f_added"))
        (a_kv, a_ek_s, a_v_s, a_mk, a_kt_s, a_qk, a_eq_s, a_mq, a_ph, a_qz_s, a_sc, a_sm, a_u, a_st, a_o, a_dn,
         a_yn, a_t, a_h, a_l, a_p, a_out) = (sem("a_" + n) for n in (
             "kv_projected", "k_exp", "v_ready", "k_exp_capped", "k_ready", "qk_projected", "q_exp", "q_exp_capped",
             "phi_ready", "q_split_by_parity", "scores", "scores_masked", "state_summed", "state_ready", "numerators",
             "denominator_steps", "normalised", "y_transposed", "y_hi", "y_lo", "projected", "added"))
        (b_qkv, b_sq_s, b_v_s, b_ss_s, b_ch, b_rs_s, b_vm_s, b_qn_s, b_ro, b_qr_s, b_hi, b_lo, b_t, b_te, b_km, b_mm,
         b_mx, b_s, b_ex, b_o, b_dn, b_yn, b_t2, b_h2, b_l2, b_pp, b_out) = (sem("b_" + n) for n in (
             "projected", "squares", "v_ready", "sums_of_squares", "rstd_steps", "rstd_ready", "even_v_ready",
             "qk_normed", "rotary_steps", "rotated", "stack_hi", "stack_lo", "qk_transposed", "qk_evacuated", "even_keys_ready",
             "scores_for_max", "max_ready", "scores", "exp_ready", "numerators", "denominators", "normalised",
             "y_transposed", "y_hi", "y_lo", "out_projected", "added"))

        block = ctx.enter_context(nc.Block())

        def steps(engine, phase1, phase2):
            phase1(0, 0, None, None, 0)
            phase2(None, None, 0, 0, 1)
            phase1(1, 1, None, None, 0)
            phase2(0, 2, 1, 1, 2)
            with engine.Fori(2, NSEQ) as i:
                phase1(i, i * 2 - 1, i - 2, i * 2 - 2, i - 1)
                phase2(i - 1, i * 2, i, i * 2 - 1, i + 1)
            phase1(None, None, NSEQ - 2, 2 * NSEQ - 2, NSEQ - 1)
            phase2(NSEQ - 1, 2 * NSEQ - 1, None, None, NSEQ)
            phase1(None, None, NSEQ - 1, 2 * NSEQ - 1, NSEQ)

        @block.sync
        def _(sp):
            sp.dma_start(st_a[:, 0:KB * 3 * D].rearrange("p (k n) -> p k n", k=KB),
                         w_qkv.rearrange("(k p) n -> p k n", p=P)).then_inc(loaded, 16)
            sp.dma_start(st_a[:, KB * 3 * D:KB * 4 * D].rearrange("p (k n) -> p k n", k=KB),
                         w_out.rearrange("(k p) n -> p k n", p=P)).then_inc(loaded, 16)
            sp.dma_start(cst[:], const).then_inc(loaded, 16)
            sp.dma_start(st_b[:, 0:KB * NB].rearrange("p (k n) -> p k n", k=KB),
                         w_b.rearrange("(k p) n -> p k n", p=P)).then_inc(loaded, 16)
            sp.dma_start(st_b[:, KB * NB:KB * NB + 2 * D].rearrange("p (k n) -> p k n", k=2),
                         wo_b.rearrange("o p n -> p o n")).then_inc(loaded, 16)
            sp.dma_start(st_w1.rearrange("p (k n) -> p k n", k=KB),
                         w1.rearrange("(k p) n -> p k n", p=P)).then_inc(loaded, 16)
            sp.dma_start(st_w2.rearrange("p (k n) -> p k n", k=FB),
                         w2.rearrange("(k p) n -> p k n", p=P)).then_inc(loaded, 16)
            sp.dma_start(b1c[:], b1).then_inc(loaded, 16)
            sp.dma_start(b2f[:], b2).then_inc(loaded, 16)
            sp.dma_start(gains[:, 0:H], gain.partition_broadcast(P)).then_inc(loaded, 16)
            sp.dma_start(mixc[:], mix).then_inc(loaded, 16)

            def phase1(a, at_turn, c, f_turn, b_done):
                if a is not None:
                    if needed(a * NT):
                        sp.wait_ge(a_out, a * NT)
                    src = x[a] if isinstance(a, int) else x[bass.ds(a, 1)].rearrange("o s d -> (o s) d")
                    sp.dma_start(x0[:], src.rearrange("(t p) d -> p t d", p=P)).then_inc(x_in, 16)
                if c is not None:
                    sp.wait_ge(f_out, (f_turn + 1) * 2)
                    dst = out[c] if isinstance(c, int) else out[bass.ds(c, 1)].rearrange("o s d -> (o s) d")
                    sp.dma_start(dst.rearrange("(t p) d -> p t d", p=P), x3[:]).then_inc(stored, 16)

            steps(sp, phase1, lambda *_: None)
            sp.wait_ge(stored, 16 * NSEQ)

        N_LOADS = 11
        N_PREPARED = 23

        @block.tensor
        def _(pe):
            pe.wait_ge(ones_set, 5)
            pe.wait_ge(setup, 2)
            pe.matmul(Q[0][:, 0:2], ones_f[:], gsum[:], start=True, stop=True).then_inc(setup_pe, 1)
            pe.wait_ge(prepared, N_PREPARED)

            def three(dst, lhs, rhs, n, start=True, last=True):
                mm = None
                for k in range(n):
                    (lh, ll), (rh, rl) = lhs(k), rhs(k)
                    for j, (a, b) in enumerate(((lh, rh), (lh, rl), (ll, rh))):
                        mm = pe.matmul(dst, a, b, start=(start and k == 0 and j == 0), stop=(last and k == n - 1 and j == 2))
                return mm

            def norm_transpose(n, turn, banks):
                for hf in range(2):
                    pe.wait_ge(n.normed, turn * NT + 2 * hf + 2)
                    for k in range(KB):
                        for t in range(2):
                            mm = pe.transpose(banks[hf][:, k * D + t * P:k * D + (t + 1) * P],
                                              n.xn[:, 2 * hf + t, k * P:(k + 1) * P], ident)
                    mm.then_inc(n.turned, 1)

            def f_norm(turn):
                if needed(turn * FB):
                    pe.wait_ge(f_act, turn * FB)
                norm_transpose(ff, turn, HID)

            def f_up(turn, fb):
                if fb == 0:
                    pe.wait_ge(ff.lo, turn * 2 + 2)
                if fb >= 2:
                    pe.wait_ge(f_act, turn * FB + fb - 1)
                for k in range(KB):
                    for j, src in enumerate((ff.xh, ff.xl)):
                        mm = pe.matmul(HID[fb % 2][:], w1t[:, k, fb * P:(fb + 1) * P], src[:, k, :],
                                       start=(k == 0 and j == 0), stop=(k == KB - 1 and j == 1))
                mm.then_inc(f_h, 1)

            def f_down(turn, fb):
                pe.wait_ge(f_lo, turn * FB + fb + 1)
                if fb == 0:
                    if needed(turn * 2):
                        pe.wait_ge(f_out, turn * 2)
                    for t in range(NT):
                        for j, b in enumerate((b2_h, b2_l)):
                            pe.matmul(Y[t // 2][:, (t % 2) * D:(t % 2 + 1) * D], ones_r[:], b[:],
                                      start=(t % 2 == 0 and j == 0), stop=False, skip_group_check=True)
                for t in range(NT):
                    for j, h in enumerate((f_hh, f_hl)):
                        mm = pe.matmul(Y[t // 2][:, (t % 2) * D:(t % 2 + 1) * D], h[:, fb % 2, t * P:(t + 1) * P],
                                       w2t[:, fb, :], start=False, stop=(fb == FB - 1 and j == 1), skip_group_check=True)
                mm.then_inc(f_w2, 1)

            def f_unit(turn, k):
                if turn is None:
                    return
                if k + 1 < FB:
                    f_up(turn, k + 1)
                if k >= 0:
                    f_down(turn, k)

            def phase1(a, n, c, fn, b_done):
                def unit(k):
                    f_unit(fn, k)

                def kv(t):
                    pe.wait_ge(at.lo, n * 2 + t // 2 + 1)
                    if t < 2 and needed(b_done * NT):
                        pe.wait_ge(b_out, b_done * NT)
                        pe.wait_ge(b_ex, b_done * 2 * NBL)
                    if t >= 2:
                        pe.wait_ge(a_kt_s, a * (NT - 1) + t - 1)
                    lo, width = (D, 2 * D) if t < NT - 1 else (2 * D, D)
                    three(Q[2 + t % 2][:, 0:width],
                          lambda k: (at.xh[:, k, t * P:(t + 1) * P], at.xl[:, k, t * P:(t + 1) * P]),
                          lambda k: (wqkv_h[:, k, lo:lo + width], wqkv_l[:, k, lo:lo + width]), KB).then_inc(a_kv, 1)

                def qk(m):
                    if m == 0:
                        pe.wait_ge(at.lo, n * 2 + 2)
                    if m >= 2:
                        pe.wait_ge(a_ph, a * 4 + m - 1)
                    three(Q[m % 2][:], lambda k: (wqkv_h[:, k, m * P:(m + 1) * P], wqkv_l[:, k, m * P:(m + 1) * P]),
                          lambda k: (at.xh[:, k, :], at.xl[:, k, :]), KB).then_inc(a_qk, 1)

                def scores(ch):
                    if ch == 0:
                        pe.wait_ge(a_qz_s, (a + 1) * 4)
                        pe.wait_ge(a_ph, (a + 1) * 4)
                    for r in range(4):
                        if 4 * ch + r >= 2:
                            pe.wait_ge(a_sm, a * 16 + 4 * ch + r - 1)
                        rows = slice(32 * r, 32 * r + 32)
                        for k in range(KB):
                            mm = pe.matmul(Q[r % 2][:, k * 2 * P:(k + 1) * 2 * P].rearrange("p (e q) -> p e q", e=2),
                                           a_kT[rows, k, ch * P:(ch + 1) * P], a_qz[rows, k, :, ch * P:(ch + 1) * P],
                                           start=(k == 0), stop=(k == KB - 1), skip_group_check=True)
                        mm.then_inc(a_sc, 1)

                def state(ch):
                    pe.wait_ge(a_v_s, a * NT + (NT if ch == 0 else ch + 1))
                    pe.wait_ge(a_kt_s, a * (NT - 1) + ch + 1)
                    if ch:
                        pe.wait_ge(a_st, a * 3 + ch)
                    for k in range(KB):
                        mm = pe.matmul(Q[3][:, k * HB * HV:(k + 1) * HB * HV].rearrange("p (h j) -> p h j", h=HB),
                                       a_kt[:, ch, k * P:(k + 1) * P], a_v[:, ch, k * HB:(k + 1) * HB, :],
                                       start=(ch == 0 and k == 0), stop=True, skip_group_check=True)
                    mm.then_inc(a_u, 1)

                def numer(ch):
                    pe.wait_ge(a_sm, a * 16 + 4 * ch + 4)
                    pe.wait_ge(a_v_s, a * NT + ch + 1)
                    if ch:
                        pe.wait_ge(a_st, a * 3 + ch)
                        pe.wait_ge(a_out, a * NT + ch)
                    else:
                        pe.wait_ge(a_kt_s, (a + 1) * (NT - 1))
                    first = True
                    if ch:
                        for k in range(KB):
                            pe.matmul(Q[2][:, k * HB * HV:(k + 1) * HB * HV], a_qT[:, k, ch * P:(ch + 1) * P],
                                      a_state[:, (ch - 1) % 2, k * HB * HV:(k + 1) * HB * HV],
                                      start=first, stop=False, skip_group_check=True)
                            first = False
                    for r in range(4):
                        for j in range(4):
                            k, e = divmod(j, 2)
                            h = k * HB + 2 * r + e
                            mm = pe.matmul(Q[2][:, h * HV:(h + 1) * HV], a_s[:, ch % 2, r, j * P:(j + 1) * P],
                                           a_v[:, ch, h, :], start=first, stop=True, skip_group_check=True)
                            first = False
                    mm.then_inc(a_o, 1)

                def turn_y(ch):
                    pe.wait_ge(a_yn, a * NT + ch + 1)
                    for k in range(KB):
                        mm = pe.transpose(Q[2][:, k * P:(k + 1) * P], a_y[:, k * P:(k + 1) * P], ident)
                    mm.then_inc(a_t, 1)

                def project(ch):
                    pe.wait_ge(a_l, a * NT + ch + 1)
                    three(Q[2][:, 0:D], lambda k: (a_yh[:, k, :], a_yl[:, k, :]),
                          lambda k: (wout_h[:, k, :], wout_l[:, k, :]), KB).then_inc(a_p, 1)

                if a is None:
                    f_norm(fn)
                    for k in range(-1, FB):
                        unit(k)
                    return
                if needed(b_done * 2 * NBL):
                    pe.wait_ge(b_mx, b_done * 2 * NBL)
                norm_transpose(at, n, Q)
                kv(0)
                kv(1)
                if fn is not None:
                    f_norm(fn)
                unit(-1)
                kv(2)
                kv(3)
                qk(0)
                qk(1)
                unit(0)
                qk(2)
                qk(3)
                unit(1)
                scores(0)
                state(0)
                numer(0)
                unit(2)
                for ch in range(NT):
                    if ch + 1 < NT:
                        scores(ch + 1)
                    turn_y(ch)
                    if ch < 3:
                        unit(3 + 2 * ch)
                    project(ch)
                    if ch + 1 < NT:
                        if ch + 1 < NT - 1:
                            state(ch + 1)
                        numer(ch + 1)
                        if ch < 2:
                            unit(4 + 2 * ch)

            def phase2(b, n, f, fn, a_done):
                def unit(k):
                    f_unit(fn, k)

                def qkv(t):
                    pe.wait_ge(at.lo, n * 2 + t // 2 + 1)
                    if t == 0:
                        pe.wait_ge(a_out, a_done * NT)
                        pe.wait_ge(a_st, a_done * 3)
                    if t >= 2:
                        pe.wait_ge(b_qn_s, b * NT + t - 1)
                    three(Q[2 + t % 2][:, 0:NB],
                          lambda k: (at.xh[:, k, t * P:(t + 1) * P], at.xl[:, k, t * P:(t + 1) * P]),
                          lambda k: (wb_h[:, k, :], wb_l[:, k, :]), KB).then_inc(b_qkv, 1)

                def turn_qk(t):
                    pe.wait_ge(b_lo, b * NT + t + 1)
                    for j in range(3):
                        free = b * 12 + 3 * t + (0, 0, 1)[j]
                        if (t or j == 2) and needed(free):
                            pe.wait_ge(b_te, free)
                        src = b_ks[:] if j == 2 else b_qs[:, 8 * j:8 * j + 8]
                        src = src.rearrange("p h s d -> p (h s d)")
                        for r in range(2 if j == 2 else REP):
                            mm = pe.transpose(Q[j % 2][:, r * P:(r + 1) * P].bitcast(F32R),
                                              src[:, r * P:(r + 1) * P], ident_r[:])
                        mm.then_inc(b_t, 1)

                def keys(bl, g2, gp):
                    rows = slice(64 * g2, 64 * g2 + 64)
                    if bl % 2:
                        return b_kT[rows, gp, (bl - 1) * W:(bl + 1) * W]
                    return b_kTm[rows, gp, bl // 2, 0:(P if bl else W)]

                def for_max(bl):
                    nk = W if bl == 0 else P
                    j = b * NBL + bl
                    if bl == 0:
                        pe.wait_ge(b_te, (b + 1) * 12)
                        pe.wait_ge(b_km, (b + 1) * 7)
                    for g2 in range(2):
                        if bl:
                            pe.wait_ge(b_mx, j * 2 - 2 + g2 + 1)
                        dst = Q[g2][:, 0:4 * nk].rearrange("p (u k) -> p u k", u=4)
                        pe.matmul(dst, ident_b[:], qmask[:, 1 - bl % 2, 0:nk].unsqueeze(1).broadcast_to([P, 4, nk]),
                                  start=True, stop=False, skip_group_check=True)
                        for gp in range(2):
                            for rp in range(2):
                                mm = pe.matmul(dst[:, 2 * gp + rp, :],
                                               b_qT[64 * g2:64 * g2 + 64, gp, bl, rp * P:(rp + 1) * P],
                                               keys(bl, g2, gp), start=False, stop=True, skip_group_check=True)
                        mm.then_inc(b_mm, 1)

                def scores(bl):
                    nk = W if bl == 0 else P
                    j = b * NBL + bl
                    if bl == 0:
                        pe.wait_ge(b_qn_s, (b + 1) * NT)
                    for g2 in range(2):
                        pe.wait_ge(b_mx, j * 2 + g2 + 1)
                        if bl:
                            if g2 == 0 and bl % 2:
                                pe.wait_ge(b_yn, j)
                            if g2 == 0 and bl % 2 == 0:
                                pe.wait_ge(b_out, b * NT + bl // 2)
                            if g2 == 1:
                                pe.wait_ge(b_ex, j * 2)
                        dst = Q[2 + g2][0:nk, :]
                        pe.matmul(dst.rearrange("p (u q) -> p u q", u=8), ident_b[:, 0:nk],
                                  kmask[:, 1 - bl % 2, :].unsqueeze(1).broadcast_to([P, 8, W]),
                                  start=True, stop=False, skip_group_check=True)
                        for gp in range(2):
                            pe.matmul(dst[:, gp * REP * W:(gp + 1) * REP * W], keys(bl, g2, gp),
                                      b_qT[64 * g2:64 * g2 + 64, gp, bl, :],
                                      start=False, stop=False, skip_group_check=True)
                        for u in range(4):
                            mm = pe.matmul(dst[:, u * P:(u + 1) * P],
                                           b_m[:, bl % 2, 4 * g2 + u:4 * g2 + u + 1].broadcast_to([P, nk]),
                                           neg_ident[:], start=False, stop=True, skip_group_check=True)
                        mm.then_inc(b_s, 1)

                def numer(bl):
                    nk = W if bl == 0 else P
                    pe.wait_ge(b_ex, (b * NBL + bl + 1) * 2)
                    if bl == 0:
                        pe.wait_ge(b_vm_s, (b + 1) * 7)
                    v = (b_v[:, (bl - 1) // 2] if bl % 2 else b_vm[:, bl // 2])
                    first = True
                    for g in range(KVH):
                        gp, g2 = divmod(g, 2)
                        for rp in range(2):
                            u = 2 * g + rp
                            mm = pe.matmul(Q[2][:, u * HV:(u + 1) * HV],
                                           b_p[0:nk, bl % 2, g2, gp * 256 + rp * P:gp * 256 + (rp + 1) * P],
                                           v[0:nk, g, :], start=first, stop=True, skip_group_check=True)
                            first = False
                    mm.then_inc(b_o, 1)

                def turn_y(t):
                    pe.wait_ge(b_yn, b * NBL + 2 * t + 2)
                    for e in range(2):
                        mm = pe.transpose(Q[2][:, e * P:(e + 1) * P], b_y[:, e, :], ident)
                    mm.then_inc(b_t2, 1)

                def project(t):
                    pe.wait_ge(b_l2, b * NT + t + 1)
                    three(Q[2][:, 0:D], lambda k: (b_yh[:, k, :], b_yl[:, k, :]),
                          lambda k: (wob_h[:, k, :], wob_l[:, k, :]), 2).then_inc(b_pp, 1)

                if b is None:
                    f_norm(fn)
                    for k in range(-1, FB):
                        unit(k)
                    return
                pe.wait_ge(a_sm, a_done * 16)
                norm_transpose(at, n, Q)
                qkv(0)
                qkv(1)
                if fn is not None:
                    f_norm(fn)
                unit(-1)
                qkv(2)
                unit(0)
                turn_qk(0)
                qkv(3)
                unit(1)
                turn_qk(1)
                turn_qk(2)
                unit(2)
                turn_qk(3)
                for_max(0)
                scores(0)
                for_max(1)
                unit(3)
                for bl in range(NBL):
                    numer(bl)
                    if bl % 2:
                        unit(4 + bl // 2)
                        turn_y(bl // 2)
                    if bl + 2 < NBL:
                        for_max(bl + 2)
                    if bl % 2:
                        project(bl // 2)
                    if bl + 1 < NBL:
                        scores(bl + 1)

            steps(pe, phase1, phase2)

        @block.scalar
        def _(act):
            act.wait_ge(prepared, N_PREPARED)

            def norm_hi(n, turn, banks):
                for hf in range(2):
                    act.wait_ge(n.turned, turn * 2 + hf + 1)
                    act.activation(n.xh[:, :, hf * D:(hf + 1) * D],
                                   banks[hf][:, :].rearrange("p (k n) -> p k n", k=KB), ACT.Copy).then_inc(n.hi, 1)

            def f_norm(turn):
                if needed(turn * FB):
                    act.wait_ge(f_h, turn * FB)
                norm_hi(ff, turn, HID)

            def f_relu(turn, fb):
                act.wait_ge(f_h, turn * FB + fb + 1)
                if needed(turn * FB + fb - 1):
                    act.wait_ge(f_lo, turn * FB + fb - 1)
                    act.wait_ge(f_w2, turn * FB + fb - 1)
                act.activation(f_r[:, fb % 2, :], HID[fb % 2][:], ACT.Relu, bias=b1c[:, fb:fb + 1]).then_inc(f_rr, 1)
                act.activation(f_hh[:, fb % 2, :], HID[fb % 2][:], ACT.Relu, bias=b1c[:, fb:fb + 1]).then_inc(f_act, 1)

            def phase1(a, n, c, fn, b_done):
                def relu(fb):
                    if fn is not None:
                        f_relu(fn, fb)

                def kv(t):
                    act.wait_ge(a_kv, a * NT + t + 1)
                    src, v_at = Q[2 + t % 2], D
                    if t < NT - 1:
                        if needed(a * (NT - 1) + t - 1):
                            act.wait_ge(a_kt_s, a * (NT - 1) + t - 1)
                        act.activation(a_ek[:, t % 2, :], src[:, 0:D], ACT.Exp).then_inc(a_ek_s, 1)
                    else:
                        v_at = 0
                    if t == 0 and needed(a * NT):
                        act.wait_ge(a_o, a * NT)
                    act.activation(a_v[:, t, :, 0:HD], src[:, v_at:v_at + D].rearrange("p (h j) -> p h j", h=H),
                                   ACT.Copy).then_inc(a_v_s, 1)

                def q_exp(m):
                    act.wait_ge(a_qk, a * 4 + m + 1)
                    if needed(a * 4 + m - 1):
                        act.wait_ge(a_ph, a * 4 + m - 1)
                    act.activation(a_eq[:, m % 2, :], Q[m % 2][:], ACT.Exp).then_inc(a_eq_s, 1)

                def y_hi(ch):
                    act.wait_ge(a_t, a * NT + ch + 1)
                    if needed(a * NT + ch):
                        act.wait_ge(a_p, a * NT + ch)
                    act.activation(a_yh[:], Q[2][:, 0:D].rearrange("p (k n) -> p k n", k=KB), ACT.Copy).then_inc(a_h, 1)

                if a is None:
                    f_norm(fn)
                    for k in range(FB):
                        relu(k)
                    return
                if needed(b_done * NT):
                    act.wait_ge(b_qkv, b_done * NT)
                norm_hi(at, n, Q)
                kv(0)
                kv(1)
                if fn is not None:
                    f_norm(fn)
                relu(0)
                kv(2)
                kv(3)
                q_exp(0)
                q_exp(1)
                relu(1)
                q_exp(2)
                q_exp(3)
                relu(2)
                relu(3)
                for ch in range(NT):
                    y_hi(ch)
                    if ch < 2:
                        relu(4 + 2 * ch)
                        relu(5 + 2 * ch)

            def phase2(b, n, f, fn, a_done):
                def relu(fb):
                    if fn is not None:
                        f_relu(fn, fb)

                def squares(t):
                    act.wait_ge(b_qkv, b * NT + t + 1)
                    if needed(b * NT + t):
                        act.wait_ge(b_ss_s, b * NT + t)
                    act.activation(b_sq[:], Q[2 + t % 2][:, 0:QK], ACT.Square).then_inc(b_sq_s, 1)
                    if t == 0 and needed(b * NBL):
                        act.wait_ge(b_o, b * NBL)
                    act.activation(b_v[:, t, :, 0:HD], Q[2 + t % 2][:, QK:NB].rearrange("p (h j) -> p h j", h=KVH),
                                   ACT.Copy).then_inc(b_v_s, 1)

                def stack_hi(t):
                    act.wait_ge(b_qr_s, b * NT + t + 1)
                    if needed(b * 12 + 3 * t):
                        act.wait_ge(b_t, b * 12 + 3 * t)
                    act.activation(b_qs[:, :, 0:2, :], b_qr[:, t % 2, 0:H, :].unsqueeze(2).broadcast_to([P, H, 2, HD]),
                                   ACT.Copy).then_inc(b_hi, 1)
                    act.activation(b_ks[:, :, 0::2, :], b_qr[:, t % 2, H:, :].unsqueeze(2).broadcast_to([P, KVH, 2, HD]),
                                   ACT.Copy).then_inc(b_hi, 1)

                def evacuate(t):
                    if t == 0 and needed(b * 2 * NBL):
                        act.wait_ge(b_s, b * 2 * NBL)
                    for j in range(3):
                        act.wait_ge(b_t, b * 12 + 3 * t + j + 1)
                        if j < 2:
                            act.activation(b_qT[:, j, 2 * t:2 * t + 2, :].rearrange("p e (r q) -> p r e q", r=REP),
                                           Q[j][:, :].rearrange("p (r e q) -> p r e q", r=REP, e=2), ACT.Copy).then_inc(b_te, 1)
                        else:
                            act.activation(b_kT[:, :, t * P:(t + 1) * P],
                                           Q[0][:, 0:2 * P].rearrange("p (r n) -> p r n", r=2), ACT.Copy).then_inc(b_te, 1)

                def exps(bl):
                    nk = W if bl == 0 else P
                    j = b * NBL + bl
                    if needed(j - 1):
                        act.wait_ge(b_o, j - 1)
                    for g2 in range(2):
                        act.wait_ge(b_s, j * 2 + g2 + 1)
                        act.activation(b_p[0:nk, bl % 2, g2, :], Q[2 + g2][0:nk, :], ACT.Exp).then_inc(b_ex, 1)

                def y_hi(t):
                    act.wait_ge(b_t2, b * NT + t + 1)
                    if needed(b * NT + t):
                        act.wait_ge(b_pp, b * NT + t)
                    act.activation(b_yh[:].rearrange("p r (e q) -> p r e q", e=2),
                                   Q[2][:, 0:D].rearrange("p (e r q) -> p r e q", e=2, r=2), ACT.Copy).then_inc(b_h2, 1)

                if b is None:
                    f_norm(fn)
                    for k in range(FB):
                        relu(k)
                    return
                act.wait_ge(a_qk, a_done * 4)
                act.wait_ge(a_kv, a_done * NT)
                norm_hi(at, n, Q)
                squares(0)
                squares(1)
                if fn is not None:
                    f_norm(fn)
                relu(0)
                squares(2)
                relu(1)
                stack_hi(0)
                evacuate(0)
                squares(3)
                relu(2)
                stack_hi(1)
                evacuate(1)
                stack_hi(2)
                evacuate(2)
                relu(3)
                stack_hi(3)
                evacuate(3)
                exps(0)
                relu(4)
                for bl in range(NBL):
                    if bl % 2:
                        if bl // 2 < 3:
                            relu(5 + bl // 2)
                        y_hi(bl // 2)
                    if bl + 1 < NBL:
                        exps(bl + 1)

            steps(act, phase1, phase2)

        @block.vector
        def _(dve):
            dve.wait_ge(loaded, 16 * N_LOADS)
            dve.tensor_reduce(gsum[:, 0:1], st_w1, X, ALU.add, apply_absolute_value=True).then_inc(setup, 1)
            dve.tensor_reduce(gsum[:, 1:2], st_w2, X, ALU.add, apply_absolute_value=True).then_inc(setup, 1)
            n = 0
            pairs = [(wqkv_h, wqkv_l, st_a[:, 0:KB * 3 * D], KB), (wout_h, wout_l, st_a[:, KB * 3 * D:KB * 4 * D], KB),
                     (wb_h, wb_l, st_b[:, 0:KB * NB], KB)]
            for hi, _, src, k in pairs:
                dve.tensor_copy(hi[:], src.rearrange("p (k n) -> p k n", k=k)).then_inc(prepared, 1)
                n += 1
            dve.tensor_copy(b2_h[:], b2f[:]).then_inc(prepared, 1)
            n += 1
            dve.wait_ge(prepared, n)
            for hi, lo, src, k in pairs:
                dve.tensor_tensor(lo[:], src.rearrange("p (k n) -> p k n", k=k), hi[:], ALU.subtract).then_inc(prepared, 1)
                n += 1
            dve.tensor_tensor(b2_l[:], b2f[:], b2_h[:], ALU.subtract).then_inc(prepared, 1)
            n += 1
            wo = st_b[:, KB * NB:KB * NB + 2 * D].rearrange("p (o n) -> p o n", o=2)
            mixed = x3[:, 0:2, :]
            for i in range(2):
                dve.tensor_scalar(mixed[:, i, :], wo[:, 0, :], mixc[:, i:i + 1], None, ALU.mult).then_inc(setup, 1)
            dve.wait_ge(setup, 4)
            for i in range(2):
                dve.scalar_tensor_tensor(out=mixed[:, i, :], in0=wo[:, 1, :], scalar=mixc[:, 2 + i:3 + i],
                                         in1=mixed[:, i, :], op0=ALU.mult, op1=ALU.add).then_inc(setup, 1)
            dve.wait_ge(setup, 6)
            dve.tensor_copy(wob_h[:], mixed).then_inc(prepared, 1)
            n += 1
            dve.wait_ge(prepared, n)
            dve.tensor_tensor(wob_l[:], mixed, wob_h[:], ALU.subtract).then_inc(prepared, 1)
            n += 1
            dve.wait_ge(setup_pe, 1)
            dve.tensor_scalar(thr[:, 0:2], Q[0][:, 0:2], 1.0 / (FF * D), Q_EPS, ALU.mult, ALU.add).then_inc(setup, 1)
            dve.wait_ge(setup, 7)
            dve.tensor_scalar(thr[:, 2:4], thr[:, 0:2], -0.5, None, ALU.mult).then_inc(setup, 1)
            dve.wait_ge(setup, 8)
            dve.tensor_scalar(thr[:, 0:2], thr[:, 0:2], 0.5, None, ALU.mult).then_inc(setup, 1)
            dve.wait_ge(setup, 9)
            below = [t[:].rearrange("p k n -> p (k n)") for t in (x1, x2, at.xn, ff.xn)]
            m = 9
            for j, (dst, src, k) in enumerate(((w1t, st_w1, KB), (w2t, st_w2, FB))):
                for half in range(2):
                    part = slice(half * 1024, (half + 1) * 1024)
                    dve.tensor_scalar(below[2 * j + half], src[:, part], thr[:, 2 + j:3 + j], None, ALU.is_lt).then_inc(setup, 1)
                m += 2
                dve.wait_ge(setup, m)
                flat = dst[:].rearrange("p k n -> p (k n)")
                for half in range(2):
                    part = slice(half * 1024, (half + 1) * 1024)
                    dve.scalar_tensor_tensor(out=flat[:, part], in0=src[:, part], scalar=thr[:, j:j + 1], in1=below[2 * j + half],
                                             op0=ALU.is_gt, op1=ALU.subtract).then_inc(prepared, 1)
                    n += 1
            dve.tensor_copy(ident_b[:], ident).then_inc(prepared, 1)
            dve.tensor_copy(ident_r[:], ident).then_inc(prepared, 1)
            dve.tensor_scalar(neg_ident[:], ident, -1.0, None, ALU.mult).then_inc(prepared, 1)
            dve.tensor_copy(kmask[:, 0, :], C["kodd"]).then_inc(prepared, 1)
            dve.tensor_copy(kmask[:, 1, :], C["keven"]).then_inc(prepared, 1)
            dve.tensor_copy(qmask[:, 0, :], C["qodd"]).then_inc(prepared, 1)
            dve.wait_ge(ones_set, 5)
            dve.tensor_copy(qmask[:, 1, :], C["qeven"]).then_inc(prepared, 1)
            dve.tensor_scalar(gains[:, 0:H], gains[:, 0:H], HD ** -0.5, None, ALU.mult).then_inc(prepared, 1)
            dve.tensor_copy(ones_r[:], ones_f[0:1, :]).then_inc(prepared, 1)
            assert n + 9 == N_PREPARED
            dve.wait_ge(prepared, N_PREPARED)

            def norm_stats(n, turn, src):
                for t in range(NT):
                    dve.bn_stats(n.st[:, t, :], src[:, t, :]).then_inc(n.bn, 1)
                for t in range(NT):
                    dve.wait_ge(n.bn, turn * NT + t + 1)
                    dve.sem_inc(dve_gate)
                    dve.bn_aggr(n.mv[:, t, :], n.st[:, t, :]).then_inc(n.stats, 1)

            def norm_apply(n, turn, src):
                dve.wait_ge(n.ready, turn + 1)
                if needed(turn * 2):
                    dve.wait_ge(n.turned, turn * 2)
                for t in range(NT):
                    dve.tensor_scalar(n.xn[:, t, :], src[:, t, :], n.mv[:, t, 0:1], n.rstd[:, t:t + 1],
                                      ALU.subtract, ALU.mult).then_inc(n.normed, 1)

            def norm_lo(n, turn, banks):
                for hf in range(2):
                    dve.wait_ge(n.hi, turn * 2 + hf + 1)
                    dve.tensor_tensor(n.xl[:, :, hf * D:(hf + 1) * D], banks[hf][:, :].rearrange("p (k n) -> p k n", k=KB),
                                      n.xh[:, :, hf * D:(hf + 1) * D], ALU.subtract).then_inc(n.lo, 1)

            def f_add(turn, src, dst):
                dve.wait_ge(f_w2, (turn + 1) * FB)
                for y in range(2):
                    dve.tensor_tensor(dst[:, 2 * y:2 * y + 2, :], Y[y][:, :].rearrange("p (t n) -> p t n", t=2),
                                      src[:, 2 * y:2 * y + 2, :], ALU.add).then_inc(f_out, 1)

            def phase1(a, n, c, fn, b_done):
                def f_stats():
                    if fn is not None:
                        dve.wait_ge(b_out, (c + 1) * NT)
                        norm_stats(ff, fn, x3)

                def f_apply():
                    if fn is not None:
                        norm_apply(ff, fn, x3)
                        norm_lo(ff, fn, HID)

                def f_finish():
                    if fn is not None:
                        dve.wait_ge(ff.normed, (fn + 1) * NT)
                        f_add(fn, x3, x3)

                def k_phi(t):
                    dve.wait_ge(a_mk, a * (NT - 1) + t + 1)
                    dve.wait_ge(a_v_s, a * NT + t + 1)
                    if t == 0 and needed(a * 3):
                        dve.wait_ge(a_u, a * 3)
                    dve.scalar_tensor_tensor(out=a_kt[:, t, :], in0=Q[2 + t % 2][:, 0:D], scalar=1.0, in1=a_ek[:, t % 2, :],
                                             op0=ALU.add, op1=ALU.max).then_inc(a_kt_s, 1)

                def phi(m):
                    dve.wait_ge(a_mq, a * 4 + m + 1)
                    if m == 0 and needed(a * NT):
                        dve.wait_ge(a_o, a * NT)
                    dst = (a_qT if m < 2 else a_kT)[:, m % 2, :]
                    dve.scalar_tensor_tensor(out=dst, in0=Q[m % 2][:], scalar=1.0, in1=a_eq[:, m % 2, :],
                                             op0=ALU.add, op1=ALU.max).then_inc(a_ph, 1)
                    if m < 2:
                        dve.wait_ge(a_ph, a * 4 + m + 1)
                        for e in range(2):
                            dve.tensor_scalar(a_qz[:, m, e, :], a_qT[:, m, :], C["parity"][:, e:e + 1], None,
                                              ALU.mult).then_inc(a_qz_s, 1)

                def mask(ch):
                    if needed(a * NT + ch - 1):
                        dve.wait_ge(a_o, a * NT + ch - 1)
                    for r in range(4):
                        dve.wait_ge(a_sc, a * 16 + 4 * ch + r + 1)
                        dve.tensor_tensor(a_s[:, ch % 2, r, :].rearrange("p (h q) -> p h q", h=4),
                                          Q[r % 2][:, :].rearrange("p (h q) -> p h q", h=4),
                                          causal.unsqueeze(1).broadcast_to([P, 4, P]), ALU.mult).then_inc(a_sm, 1)

                def state(ch):
                    dve.wait_ge(a_u, a * 3 + ch + 1)
                    if needed(a * NT + ch):
                        dve.wait_ge(a_o, a * NT + ch)
                    dve.tensor_tensor(a_state[:, ch % 2, :].rearrange("p (k n) -> p k n", k=KB),
                                      Q[3][:, 0:KB * HB * HV].rearrange("p (k n) -> p k n", k=KB),
                                      C["heads"].unsqueeze(1).broadcast_to([P, KB, HB * HV]), ALU.mult).then_inc(a_st, 1)

                def normalise(ch):
                    o = Q[2][:, 0:H * HV].rearrange("p (h j) -> p h j", h=H)
                    steps_before = a * 2 * NT + 2 * ch
                    dve.wait_ge(a_o, a * NT + ch + 1)
                    dve.tensor_scalar(a_den[:, 0, :], o[:, :, HD], A_EPS, None, ALU.add).then_inc(a_dn, 1)
                    dve.wait_ge(a_dn, steps_before + 1)
                    dve.reciprocal(a_den[:, 1, :], a_den[:, 0, :]).then_inc(a_dn, 1)
                    dve.wait_ge(a_dn, steps_before + 2)
                    if needed(a * NT + ch):
                        dve.wait_ge(a_t, a * NT + ch)
                    dve.tensor_tensor(a_y[:].rearrange("p (h j) -> p h j", h=H), o[:, :, 0:HD],
                                      a_den[:, 1, :].unsqueeze(2).broadcast_to([P, H, HD]), ALU.mult).then_inc(a_yn, 1)

                def y_lo(ch):
                    dve.wait_ge(a_h, a * NT + ch + 1)
                    dve.tensor_tensor(a_yl[:], Q[2][:, 0:D].rearrange("p (k n) -> p k n", k=KB), a_yh[:],
                                      ALU.subtract).then_inc(a_l, 1)

                def residual(ch):
                    dve.wait_ge(a_p, a * NT + ch + 1)
                    dve.tensor_tensor(x1[:, ch, :], Q[2][:, 0:D], x0[:, ch, :], ALU.add).then_inc(a_out, 1)

                if a is None:
                    f_stats()
                    f_apply()
                    f_finish()
                    return
                dve.wait_ge(x_in, (a + 1) * 16)
                norm_stats(at, n, x0)
                norm_apply(at, n, x0)
                norm_lo(at, n, Q)
                f_stats()
                k_phi(0)
                k_phi(1)
                f_apply()
                k_phi(2)
                for m in range(4):
                    phi(m)
                mask(0)
                state(0)
                normalise(0)
                for ch in range(NT):
                    if ch + 1 < NT:
                        mask(ch + 1)
                    y_lo(ch)
                    residual(ch)
                    if ch + 1 < NT:
                        if ch + 1 < NT - 1:
                            state(ch + 1)
                        normalise(ch + 1)
                    if ch == 2:
                        f_finish()

            def phase2(b, n, f, fn, a_done):
                def f_stats():
                    if fn is not None:
                        dve.wait_ge(a_out, (f + 1) * NT)
                        norm_stats(ff, fn, x1)

                def f_apply():
                    if fn is not None:
                        norm_apply(ff, fn, x1)
                        norm_lo(ff, fn, HID)

                def f_finish():
                    if fn is not None:
                        if b is not None:
                            dve.wait_ge(b_out, (b + 1) * NT)
                        f_add(fn, x1, x2)

                def sums(t):
                    dve.wait_ge(b_sq_s, b * NT + t + 1)
                    if needed(b * NT + t):
                        dve.wait_ge(b_rs_s, b * NT + t)
                    dve.tensor_reduce(b_ss[:], b_sq[:].rearrange("p (h j) -> p h j", j=HD), X, ALU.add).then_inc(b_ss_s, 1)

                def norm_qk(t):
                    dve.wait_ge(b_rs_s, b * NT + t + 1)
                    dve.wait_ge(b_v_s, b * NT + t + 1)
                    if needed(b * NT + t - 1):
                        dve.wait_ge(b_qr_s, b * NT + t - 1)
                    dve.tensor_tensor(b_qn[:, t % 2], Q[2 + t % 2][:, 0:QK].rearrange("p (h j) -> p h j", j=HD),
                                      b_rs[:].unsqueeze(2).broadcast_to([P, H + KVH, HD]), ALU.mult).then_inc(b_qn_s, 1)

                def even_v(t):
                    dve.tensor_copy(b_vm[0:W, t, :, 0:HD], b_v[0:W, t, :, 0:HD]).then_inc(b_vm_s, 1)
                    if t + 1 < NT:
                        dve.tensor_copy(b_vm[W:P, t + 1, :, 0:HD], b_v[W:P, t, :, 0:HD]).then_inc(b_vm_s, 1)

                def stack_lo(t):
                    dve.wait_ge(b_hi, (b * NT + t + 1) * 2)
                    dve.tensor_tensor(b_qs[:, :, 2:4, :], b_qr[:, t % 2, 0:H, :].unsqueeze(2).broadcast_to([P, H, 2, HD]),
                                      b_qs[:, :, 0:2, :], ALU.subtract)
                    dve.tensor_tensor(b_ks[:, :, 1::2, :], b_qr[:, t % 2, H:, :].unsqueeze(2).broadcast_to([P, KVH, 2, HD]),
                                      b_ks[:, :, 0::2, :], ALU.subtract).then_inc(b_lo, 1)

                def even_keys(t):
                    dve.wait_ge(b_te, b * 12 + 3 * t + 3)
                    if t == 0 and needed(b * 2 * NBL):
                        dve.wait_ge(b_s, b * 2 * NBL)
                    dve.tensor_copy(b_kTm[:, :, t, 0:W], b_kT[:, :, t * P:t * P + W]).then_inc(b_km, 1)
                    if t + 1 < NT:
                        dve.tensor_copy(b_kTm[:, :, t + 1, W:P], b_kT[:, :, t * P + W:(t + 1) * P]).then_inc(b_km, 1)

                def maxima(bl):
                    nk = W if bl == 0 else P
                    j = b * NBL + bl
                    if needed(j * 2 - 2):
                        dve.wait_ge(b_s, j * 2 - 2)
                    for g2 in range(2):
                        dve.wait_ge(b_mm, j * 2 + g2 + 1)
                        dve.tensor_reduce(b_m[:, bl % 2, 4 * g2:4 * g2 + 4],
                                          Q[g2][:, 0:4 * nk].rearrange("p (u k) -> p u k", u=4), X, ALU.max).then_inc(b_mx, 1)

                def normalise(bl):
                    j = b * NBL + bl
                    o = Q[2][:, 0:2 * KVH * HV].rearrange("p (h j) -> p h j", j=HV)
                    dve.wait_ge(b_o, j + 1)
                    dve.reciprocal(b_den[:], o[:, :, HD]).then_inc(b_dn, 1)
                    dve.wait_ge(b_dn, j + 1)
                    if needed(b * NT + bl // 2):
                        dve.wait_ge(b_t2, b * NT + bl // 2)
                    dve.tensor_tensor(b_y[:, bl % 2, :].rearrange("p (h j) -> p h j", j=HD), o[:, :, 0:HD],
                                      b_den[:].unsqueeze(2).broadcast_to([P, 2 * KVH, HD]), ALU.mult).then_inc(b_yn, 1)

                def y_lo(t):
                    dve.wait_ge(b_h2, b * NT + t + 1)
                    dve.tensor_tensor(b_yl[:].rearrange("p r (e q) -> p r e q", e=2),
                                      Q[2][:, 0:D].rearrange("p (e r q) -> p r e q", e=2, r=2),
                                      b_yh[:].rearrange("p r (e q) -> p r e q", e=2), ALU.subtract).then_inc(b_l2, 1)

                def residual(t):
                    dve.wait_ge(b_pp, b * NT + t + 1)
                    if t == 0 and needed(b * 16):
                        dve.wait_ge(stored, b * 16)
                    dve.tensor_tensor(x3[:, t, :], Q[2][:, 0:D], x2[:, t, :], ALU.add).then_inc(b_out, 1)

                if b is None:
                    f_stats()
                    f_apply()
                    f_finish()
                    return
                dve.wait_ge(f_out, 2 * (b if isinstance(b, int) and b == 0 else b * 2 - 1) + 2)
                norm_stats(at, n, x2)
                norm_apply(at, n, x2)
                norm_lo(at, n, Q)
                sums(0)
                f_stats()
                norm_qk(0)
                even_v(0)
                sums(1)
                norm_qk(1)
                even_v(1)
                f_apply()
                stack_lo(0)
                sums(2)
                norm_qk(2)
                even_v(2)
                stack_lo(1)
                sums(3)
                norm_qk(3)
                even_v(3)
                stack_lo(2)
                stack_lo(3)
                for t in range(NT):
                    even_keys(t)
                maxima(0)
                maxima(1)
                for bl in range(NBL):
                    normalise(bl)
                    if bl % 2:
                        y_lo(bl // 2)
                    if bl + 2 < NBL:
                        maxima(bl + 2)
                    if bl % 2:
                        residual(bl // 2)
                f_finish()

            steps(dve, phase1, phase2)

        @block.gpsimd
        def _(pool):
            pool.memset(ones_f[:], 1.0).then_inc(ones_set, 1)
            pool.memset(mhalf[:], -0.5).then_inc(ones_set, 1)
            pool.memset(gains[:, H:], 1.0).then_inc(ones_set, 1)
            pool.memset(a_v[:, :, :, HD:HV], 1.0).then_inc(ones_set, 1)
            pool.memset(b_v[:, :, :, HD:HV], 1.0)
            pool.memset(b_vm[:, :, :, HD:HV], 1.0).then_inc(ones_set, 1)
            pool.wait_ge(prepared, N_PREPARED)

            def root(tmp, exponent, chain, start, dst, ready):
                v, y, u = tmp[:, 0, :], tmp[:, 1, :], tmp[:, 2, :]
                pool.wait_ge(chain, start + 1)
                pool.tensor_tensor(y, v, exponent, ALU.pow).then_inc(chain, 1)
                pool.wait_ge(chain, start + 2)
                pool.tensor_tensor(u, y, y, ALU.mult).then_inc(chain, 1)
                pool.wait_ge(chain, start + 3)
                pool.tensor_tensor(u, u, v, ALU.mult).then_inc(chain, 1)
                pool.wait_ge(chain, start + 4)
                pool.sem_inc(pool_gate)
                pool.tensor_scalar(u, u, -0.5, 1.5, ALU.mult, ALU.add).then_inc(chain, 1)
                pool.wait_ge(chain, start + 5)
                last = pool.tensor_tensor(dst, y, u, ALU.mult)
                last.then_inc(ready, 1)

            def norm_rstd(n, turn):
                pool.wait_ge(n.stats, (turn + 1) * NT)
                if needed(turn * NT):
                    pool.wait_ge(n.normed, turn * NT)
                pool.sem_inc(pool_gate)
                pool.tensor_scalar(n.tmp[:, 0, :], n.mv[:, :, 1], 1.0, LN_EPS, ALU.mult, ALU.add).then_inc(n.chain, 1)
                root(n.tmp, mhalf[:, 0:NT], n.chain, turn * 5, n.rstd[:], n.ready)

            def f_lo_part(turn, fb):
                pool.wait_ge(f_act, turn * FB + fb + 1)
                if needed(turn * FB + fb - 1):
                    pool.wait_ge(f_w2, turn * FB + fb - 1)
                pool.tensor_tensor(f_hl[:, fb % 2, :], f_r[:, fb % 2, :], f_hh[:, fb % 2, :], ALU.subtract).then_inc(f_lo, 1)

            def phase1(a, n, c, fn, b_done):
                def lo(fb):
                    if fn is not None:
                        f_lo_part(fn, fb)

                def cap_k(t):
                    pool.wait_ge(a_ek_s, a * (NT - 1) + t + 1)
                    pool.sem_inc(pool_gate)
                    pool.tensor_scalar(a_ek[:, t % 2, :], a_ek[:, t % 2, :], 1.0, 0.0, ALU.min, ALU.max).then_inc(a_mk, 1)

                def cap_q(m):
                    pool.wait_ge(a_eq_s, a * 4 + m + 1)
                    pool.sem_inc(pool_gate)
                    pool.tensor_scalar(a_eq[:, m % 2, :], a_eq[:, m % 2, :], 1.0, 0.0, ALU.min, ALU.max).then_inc(a_mq, 1)

                if a is None:
                    norm_rstd(ff, fn)
                    for k in range(FB):
                        lo(k)
                    return
                norm_rstd(at, n)
                cap_k(0)
                if fn is not None:
                    norm_rstd(ff, fn)
                cap_k(1)
                cap_k(2)
                lo(0)
                cap_q(0)
                cap_q(1)
                cap_q(2)
                lo(1)
                cap_q(3)
                for k in range(2, FB):
                    lo(k)

            def phase2(b, n, f, fn, a_done):
                def lo(fb):
                    if fn is not None:
                        f_lo_part(fn, fb)

                def rstd(t):
                    j = b * NT + t
                    pool.wait_ge(b_ss_s, j + 1)
                    pool.sem_inc(pool_gate)
                    pool.tensor_scalar(b_tmp[:, 0, :], b_ss[:], 1.0 / HD, RMS_EPS, ALU.mult, ALU.add).then_inc(b_ch, 1)
                    if needed(j):
                        pool.wait_ge(b_qn_s, j)
                    root(b_tmp, mhalf[:], b_ch, j * 6, b_rs[:], b_ch)
                    pool.wait_ge(b_ch, j * 6 + 6)
                    pool.tensor_tensor(b_rs[:], b_rs[:], gains[:], ALU.mult).then_inc(b_rs_s, 1)

                def rotate(t):
                    j = b * NT + t
                    qn = b_qn[:, t % 2]
                    table = lambda name, lo, hi: C[name].rearrange("p (t d) -> p t d", t=NT)[:, t, lo:hi].unsqueeze(1) \
                        .broadcast_to([P, H + KVH, hi - lo])
                    pool.wait_ge(b_qn_s, j + 1)
                    pool.tensor_tensor(b_rc[:], qn, table("cos", 0, HD), ALU.mult)
                    pool.tensor_tensor(b_rsn[:, :, 0:HD // 2], qn[:, :, HD // 2:], table("sin", 0, HD // 2), ALU.mult)
                    pool.tensor_tensor(b_rsn[:, :, HD // 2:], qn[:, :, 0:HD // 2], table("sin", HD // 2, HD),
                                       ALU.mult).then_inc(b_ro, 1)
                    pool.wait_ge(b_ro, j + 1)
                    if needed(j - 1):
                        pool.wait_ge(b_lo, j - 1)
                    pool.tensor_tensor(b_qr[:, t % 2], b_rc[:], b_rsn[:], ALU.add).then_inc(b_qr_s, 1)

                if b is None:
                    norm_rstd(ff, fn)
                    for k in range(FB):
                        lo(k)
                    return
                norm_rstd(at, n)
                rstd(0)
                if fn is not None:
                    norm_rstd(ff, fn)
                rotate(0)
                rstd(1)
                rotate(1)
                lo(0)
                rstd(2)
                rotate(2)
                lo(1)
                rstd(3)
                rotate(3)
                for k in range(2, FB):
                    lo(k)

            steps(pool, phase1, phase2)


def arrays_of(x, W_qkv, W_out, Wq, Wk, Wv, Wo, q_gain, pair_mix, W1, b1, W2, b2):
    wq = Wq.T.reshape(D, 2, 2, REP, HD).transpose(0, 1, 3, 2, 4).reshape(D, D)
    return {
        "x": x,
        "w_qkv": W_qkv,
        "w_out": W_out,
        "w_b": np.concatenate([wq, Wk.T, Wv.T], 1),
        "wo_b": Wo.T.reshape(H // 2, 2, HD, D).transpose(1, 0, 2, 3).reshape(2, P, D),
        "gain": q_gain.reshape(2, 2, REP).transpose(0, 2, 1).reshape(H),
        "mix": np.repeat(pair_mix.reshape(H // 2, 4), HD, axis=0),
        "w1": W1.T,
        "b1": b1.reshape(FB, P).T,
        "w2": W2.T,
        "b2": b2.reshape(1, D),
        "const": constants(),
    }


def kernel(**inputs):
    import concourse.bacc as bacc
    from concourse.bass_utils import run_bass_kernel_spmd

    g = {k: np.asarray(v) for k, v in inputs.items()}
    laid = arrays_of(g["L0_attn_a_x"], g["L0_attn_a_W_qkv"], g["L0_attn_a_W_out"], g["L0_attn_b_Wq"], g["L0_attn_b_Wk"],
                     g["L0_attn_b_Wv"], g["L0_attn_b_Wo"], g["L0_attn_b_q_gain"], g["L0_attn_b_pair_mix"],
                     g["L0_ffn_W1"], g["L0_ffn_b1"], g["L0_ffn_W2"], g["L0_ffn_b2"])
    nc = bacc.Bacc("TRN2", target_bir_lowering=False, num_devices=1)
    arrays = {f"in_{n}": np.ascontiguousarray(a) for n, a in laid.items()}
    aps = [nc.dram_tensor(n, a.shape, F32, kind="ExternalInput").ap() for n, a in arrays.items()]
    out = nc.dram_tensor("out", (NSEQ, S, D), F32, kind="ExternalOutput").ap()
    build(nc, *aps, out)
    r = run_bass_kernel_spmd(nc, [arrays], core_ids=[0])
    return r.results[0]["out"]
```

```python
from contextlib import ExitStack

import numpy as np

import concourse.bass as bass
from concourse import mybir

ALU = mybir.AluOpType
ACT = mybir.ActivationFunctionType
X = mybir.AxisListType.X
F32 = mybir.dt.float32
F32R = mybir.dt.float32r
BF16 = mybir.dt.bfloat16

P = 128
NSEQ, S, D = 32, 512, 256
NT = S // P
KB = D // P
H, HD = 16, 16
HB = H // KB
HV = HD + 1
FF = 4 * D
FB = FF // P
KVH = 4
REP = H // KVH
W = 64
NBL = S // W
QK = (H + KVH) * HD
NB = QK + KVH * HD
SLOT = 4 * HD
LN_EPS, A_EPS, RMS_EPS, Q_EPS = 1e-5, 1e-6, 1e-6, 1e-5
MASKED = -1e30
SAFE_SCORE = 40.0

_WIDTHS = dict(ident=P, causal=P, heads=HB * HV, parity=2, kodd=W, keven=W, qodd=P, qeven=P,
               cos=NT * HD, sin=NT * HD)
COL, _at = {}, 0
for _name, _w in _WIDTHS.items():
    COL[_name] = (_at, _at + _w)
    _at += _w
NCONST = _at


def constants():
    c = np.zeros((P, NCONST), np.float32)

    def put(name, value):
        c[:, COL[name][0]:COL[name][1]] = np.asarray(value, np.float32).reshape(P, -1)

    p, q = np.arange(P)[:, None], np.arange(P)[None, :]
    put("ident", p == q)
    put("causal", p <= q)
    head = np.repeat(np.arange(HB), HV)[None, :]
    put("heads", p // HD == head)
    put("parity", (p // HD) % 2 == np.arange(2)[None, :])
    k, qq = np.arange(P)[:, None], np.arange(W)[None, :]
    odd = np.where(k < W, qq < k, k - W <= qq)
    even = np.where(k < W, k <= qq, qq < k - W)
    put("kodd", np.where(odd, 0.0, MASKED))
    put("keven", np.where(even, 0.0, MASKED))
    put("qodd", np.where(np.tile(odd.T, (2, 1)), 0.0, MASKED))
    put("qeven", np.where(np.tile(even.T, (2, 1)), 0.0, MASKED))
    inv = (1.0 / np.float32(10000.0) ** (np.arange(0, HD, 2, dtype=np.float32) / HD)).astype(np.float32)
    ang = np.outer(np.arange(S, dtype=np.float32), inv)
    cos, sin = np.cos(ang).astype(np.float32), np.sin(ang).astype(np.float32)
    table = lambda a, b: np.concatenate([a, b], 1).reshape(NT, P, HD).transpose(1, 0, 2)
    put("cos", table(cos, cos))
    put("sin", table(sin, -sin))
    return c


def needed(value):
    return not isinstance(value, int) or value > 0


def build(nc, x, w_qkv, w_out, w_b, wo_b, gain, mix, w1, b1, w2, b2, const, out):
    with ExitStack() as ctx:
        def sb(name, shape, dt=F32):
            return ctx.enter_context(nc.sbuf_tensor(name, shape, dt))

        def sem(name):
            return ctx.enter_context(nc.semaphore(name))

        cst = sb("cst", [P, NCONST])
        C = {n: cst[:, a:b] for n, (a, b) in COL.items()}
        ident, causal = C["ident"], C["causal"]
        ident_b = sb("ident_b", [P, P], BF16)
        neg_ident = sb("neg_ident", [P, P], F32R)
        ident_r = sb("ident_r", [P, P], F32R)
        kmask = sb("kmask", [P, 2, W], BF16)
        qmask = sb("qmask", [P, 2, P], BF16)
        wqkv_h, wqkv_l = (sb(f"wqkv_{n}", [P, KB, 3 * D], F32R) for n in "hl")
        wout_h, wout_l = (sb(f"wout_{n}", [P, KB, D], F32R) for n in "hl")
        wb_h, wb_l = (sb(f"wb_{n}", [P, KB, NB], F32R) for n in "hl")
        wob_h, wob_l = (sb(f"wob_{n}", [P, 2, D], F32R) for n in "hl")
        w1t = sb("w1t", [P, KB, FF], F32R)
        w2t = sb("w2t", [P, FB, D], F32R)
        b1c = sb("b1c", [P, FB])
        b2f = sb("b2f", [1, D])
        b2_h, b2_l = sb("b2_h", [1, D], F32R), sb("b2_l", [1, D], F32R)
        ones_f = sb("ones_f", [P, P])
        ones_r = sb("ones_r", [1, P], F32R)
        gains = sb("gains", [P, H + KVH])
        mixc = sb("mixc", [P, 4])
        mhalf = sb("mhalf", [P, H + KVH])
        gsum = sb("gsum", [P, 2])
        thr = sb("thr", [P, 4])
        wide_f, wide_i = sb("wide_f", [P, 2]), sb("wide_i", [P, 1], mybir.dt.int32)

        x0, x1, x2, x3 = (sb(f"x{n}", [P, NT, D]) for n in range(4))

        class Norm:
            def __init__(self, n):
                self.st = sb(n + "st", [P, NT, 6])
                self.mv = sb(n + "mv", [P, NT, 2])
                self.tmp = sb(n + "tmp", [P, 3, NT])
                self.rstd = sb(n + "rstd", [P, NT])
                self.xn = sb(n + "xn", [P, NT, D])
                self.xh = sb(n + "xh", [P, KB, S], F32R)
                self.xl = sb(n + "xl", [P, KB, S], F32R)
                self.bn = sem(n + "bn_stats_done")
                self.stats = sem(n + "mean_var_ready")
                self.chain = sem(n + "rstd_steps")
                self.ready = sem(n + "rstd_ready")
                self.normed = sem(n + "normed")
                self.turned = sem(n + "transposed")
                self.hi = sem(n + "hi_ready")
                self.lo = sem(n + "lo_ready")

        at, ff = Norm("at_"), Norm("ff_")

        f_r = sb("f_r", [P, 2, S])
        f_hh = sb("f_hh", [P, 2, S], F32R)
        f_hl = sb("f_hl", [P, 2, S], F32R)

        a_ek = sb("a_ek", [P, 2, D])
        a_eq = sb("a_eq", [P, 2, S])
        a_kt = sb("a_kt", [P, NT - 1, D])
        a_v = sb("a_v", [P, NT, H, HV])
        a_qT = sb("a_qT", [P, KB, S])
        a_kT = sb("a_kT", [P, KB, S])
        a_qz = sb("a_qz", [P, KB, 2, S])
        a_s = sb("a_s", [P, 2, 4, S])
        a_state = sb("a_state", [P, 2, KB * HB * HV])
        a_den = sb("a_den", [P, 2, H])
        a_y = sb("a_y", [P, D])
        a_yh, a_yl = sb("a_yh", [P, KB, P], F32R), sb("a_yl", [P, KB, P], F32R)

        b_sq = sb("b_sq", [P, QK])
        b_ss = sb("b_ss", [P, H + KVH])
        b_tmp = sb("b_tmp", [P, 3, H + KVH])
        b_rs = sb("b_rs", [P, H + KVH])
        b_qn = sb("b_qn", [P, 2, H + KVH, HD])
        b_rc = sb("b_rc", [P, H + KVH, HD])
        b_rsn = sb("b_rsn", [P, H + KVH, HD])
        b_qr = sb("b_qr", [P, 2, H + KVH, HD])
        b_qs = sb("b_qs", [P, H, 4, HD], F32R)
        b_ks = sb("b_ks", [P, KVH, 4, HD], F32R)
        b_qT = sb("b_qT", [P, 2, NBL, REP * W], F32R)
        b_kT = sb("b_kT", [P, 2, S], F32R)
        b_kTm = sb("b_kTm", [P, 2, NT, P], F32R)
        b_v = sb("b_v", [P, NT, KVH, HV])
        b_vm = sb("b_vm", [P, NT, KVH, HV])
        b_m = sb("b_m", [P, 2, 2 * 4], F32R)
        b_p = sb("b_p", [P, 2, 2, S])
        b_den = sb("b_den", [P, 2, 2 * KVH])
        b_y = sb("b_y", [P, 2, P])
        b_yh, b_yl = sb("b_yh", [P, 2, P], F32R), sb("b_yl", [P, 2, P], F32R)

        Q = [ctx.enter_context(nc.psum_tensor(f"Q{n}", [P, S], F32)) for n in range(4)]
        HID = [ctx.enter_context(nc.psum_tensor(f"HID{n}", [P, S], F32)) for n in range(2)]
        Y = [ctx.enter_context(nc.psum_tensor(f"Y{n}", [P, S], F32)) for n in range(2)]

        st_a = a_s[:, 0].rearrange("p a n -> p (a n)")
        st_w1 = a_s[:, 1].rearrange("p a n -> p (a n)")
        st_w2 = a_qz[:, :].rearrange("p a b n -> p (a b n)")
        st_b = b_p[:, :].rearrange("p a b n -> p (a b n)")

        loaded, setup, setup_pe, prepared, ones_set = (sem(n) for n in (
            "weights_loaded", "setup_steps", "abs_sum_ready", "weights_prepared", "constants_set"))
        pool_gate, dve_gate = sem("pool_gate"), sem("dve_gate")
        x_in, stored = sem("x_loaded"), sem("x_stored")
        f_h, f_rr, f_act, f_lo, f_w2, f_out = (sem(n) for n in (
            "f_hidden_ready", "f_relu_ready", "f_hi_ready", "f_lo_ready", "f_down_done", "f_added"))
        (a_kv, a_ek_s, a_v_s, a_mk, a_kt_s, a_qk, a_eq_s, a_mq, a_ph, a_qz_s, a_sc, a_sm, a_u, a_st, a_o, a_dn,
         a_yn, a_t, a_h, a_l, a_p, a_out) = (sem("a_" + n) for n in (
             "kv_projected", "k_exp", "v_ready", "k_exp_capped", "k_ready", "qk_projected", "q_exp", "q_exp_capped",
             "phi_ready", "q_split_by_parity", "scores", "scores_masked", "state_summed", "state_ready", "numerators",
             "denominator_steps", "normalised", "y_transposed", "y_hi", "y_lo", "projected", "added"))
        (b_qkv, b_sq_s, b_v_s, b_ss_s, b_ch, b_rs_s, b_vm_s, b_qn_s, b_ro, b_qr_s, b_hi, b_lo, b_t, b_te, b_km, b_mm,
         b_mx, b_s, b_ex, b_o, b_dn, b_yn, b_t2, b_h2, b_l2, b_pp, b_out) = (sem("b_" + n) for n in (
             "projected", "squares", "v_ready", "sums_of_squares", "rstd_steps", "rstd_ready", "even_v_ready",
             "qk_normed", "rotary_steps", "rotated", "stack_hi", "stack_lo", "qk_transposed", "qk_evacuated", "even_keys_ready",
             "scores_for_max", "max_ready", "scores", "exp_ready", "numerators", "denominators", "normalised",
             "y_transposed", "y_hi", "y_lo", "out_projected", "added"))

        block = ctx.enter_context(nc.Block())
        N_LOADS = 11
        N_PREPARED = 24

        class Step:
            def __init__(self, i):
                def there(j):
                    return j if not isinstance(j, int) or 0 <= j < NSEQ else None
                self.a, self.b, self.c, self.next_a = there(i), there(i - 1), there(i - 2), there(i + 1)
                self.last = isinstance(i, int) and i == NSEQ + 1

        def first_turn(s):
            return None if s is None else 0 if isinstance(s, int) and s == 0 else s * 2 - 1

        def second_turn(s):
            return None if s is None else 2 * NSEQ - 1 if isinstance(s, int) and s == NSEQ - 1 else s * 2 + 2

        def steps(engine, phase1, phase2):
            for i in (0, 1):
                phase1(Step(i))
                phase2(Step(i))
            with engine.Fori(2, NSEQ - 1) as i:
                phase1(Step(i))
                phase2(Step(i))
            for i in (NSEQ - 1, NSEQ):
                phase1(Step(i))
                phase2(Step(i))
            phase1(Step(NSEQ + 1))

        def both_ways(engine, program):
            engine.wait_ge(prepared, N_PREPARED)
            wide = engine.value_load(wide_i[0:1, 0:1], min_val=0, max_val=1)
            with engine.If(wide):
                program(True)
            with engine.Else():
                program(False)

        @block.sync
        def _(sp):
            sp.dma_start(st_a[:, 0:KB * 3 * D].rearrange("p (k n) -> p k n", k=KB),
                         w_qkv.rearrange("(k p) n -> p k n", p=P)).then_inc(loaded, 16)
            sp.dma_start(st_a[:, KB * 3 * D:KB * 4 * D].rearrange("p (k n) -> p k n", k=KB),
                         w_out.rearrange("(k p) n -> p k n", p=P)).then_inc(loaded, 16)
            sp.dma_start(cst[:], const).then_inc(loaded, 16)
            sp.dma_start(st_b[:, 0:KB * NB].rearrange("p (k n) -> p k n", k=KB),
                         w_b.rearrange("(k p) n -> p k n", p=P)).then_inc(loaded, 16)
            sp.dma_start(st_b[:, KB * NB:KB * NB + 2 * D].rearrange("p (k n) -> p k n", k=2),
                         wo_b.rearrange("o p n -> p o n")).then_inc(loaded, 16)
            sp.dma_start(st_w1.rearrange("p (k n) -> p k n", k=KB),
                         w1.rearrange("(k p) n -> p k n", p=P)).then_inc(loaded, 16)
            sp.dma_start(st_w2.rearrange("p (k n) -> p k n", k=FB),
                         w2.rearrange("(k p) n -> p k n", p=P)).then_inc(loaded, 16)
            sp.dma_start(b1c[:], b1).then_inc(loaded, 16)
            sp.dma_start(b2f[:], b2).then_inc(loaded, 16)
            sp.dma_start(gains[:, 0:H], gain.partition_broadcast(P)).then_inc(loaded, 16)
            sp.dma_start(mixc[:], mix).then_inc(loaded, 16)

            def load(a):
                if needed(a * NT):
                    sp.wait_ge(a_out, a * NT)
                src = x[a] if isinstance(a, int) else x[bass.ds(a, 1)].rearrange("o s d -> (o s) d")
                sp.dma_start(x0[:], src.rearrange("(t p) d -> p t d", p=P)).then_inc(x_in, 16)

            def store(c):
                sp.wait_ge(f_out, (second_turn(c) + 1) * 2)
                dst = out[c] if isinstance(c, int) else out[bass.ds(c, 1)].rearrange("o s d -> (o s) d")
                sp.dma_start(dst.rearrange("(t p) d -> p t d", p=P), x3[:]).then_inc(stored, 16)

            def phase1(s):
                if s.last:
                    store(s.c)

            def phase2(s):
                if s.c is not None:
                    store(s.c)
                if s.next_a is not None:
                    load(s.next_a)

            load(0)
            steps(sp, phase1, phase2)
            sp.wait_ge(stored, 16 * NSEQ)

        @block.tensor
        def _(pe):
            pe.wait_ge(ones_set, 5)
            pe.wait_ge(setup, 2)
            pe.matmul(Q[0][:, 0:2], ones_f[:], gsum[:], start=True, stop=True).then_inc(setup_pe, 1)
            def three(dst, lhs, rhs, n, start=True, last=True):
                mm = None
                for k in range(n):
                    (lh, ll), (rh, rl) = lhs(k), rhs(k)
                    for j, (a, b) in enumerate(((lh, rh), (lh, rl), (ll, rh))):
                        mm = pe.matmul(dst, a, b, start=(start and k == 0 and j == 0), stop=(last and k == n - 1 and j == 2))
                return mm

            def norm_transpose(n, turn, banks):
                for hf in range(2):
                    pe.wait_ge(n.normed, turn * NT + 2 * hf + 2)
                    for k in range(KB):
                        for t in range(2):
                            mm = pe.transpose(banks[hf][:, k * D + t * P:k * D + (t + 1) * P],
                                              n.xn[:, 2 * hf + t, k * P:(k + 1) * P], ident)
                    mm.then_inc(n.turned, 1)

            def f_norm(turn):
                if needed(turn * FB):
                    pe.wait_ge(f_act, turn * FB)
                norm_transpose(ff, turn, HID)

            def f_up(turn, fb):
                if fb == 0:
                    pe.wait_ge(ff.lo, turn * 2 + 2)
                if fb >= 2:
                    pe.wait_ge(f_act, turn * FB + fb - 1)
                for k in range(KB):
                    for j, src in enumerate((ff.xh, ff.xl)):
                        mm = pe.matmul(HID[fb % 2][:], w1t[:, k, fb * P:(fb + 1) * P], src[:, k, :],
                                       start=(k == 0 and j == 0), stop=(k == KB - 1 and j == 1))
                mm.then_inc(f_h, 1)

            def f_down(turn, fb):
                pe.wait_ge(f_lo, turn * FB + fb + 1)
                if fb == 0:
                    if needed(turn * 2):
                        pe.wait_ge(f_out, turn * 2)
                    for t in range(NT):
                        for j, b in enumerate((b2_h, b2_l)):
                            pe.matmul(Y[t // 2][:, (t % 2) * D:(t % 2 + 1) * D], ones_r[:], b[:],
                                      start=(t % 2 == 0 and j == 0), stop=False, skip_group_check=True)
                for t in range(NT):
                    for j, h in enumerate((f_hh, f_hl)):
                        mm = pe.matmul(Y[t // 2][:, (t % 2) * D:(t % 2 + 1) * D], h[:, fb % 2, t * P:(t + 1) * P],
                                       w2t[:, fb, :], start=False, stop=(fb == FB - 1 and j == 1), skip_group_check=True)
                mm.then_inc(f_w2, 1)

            def f_unit(turn, k):
                if turn is not None:
                    if k + 1 < FB:
                        f_up(turn, k + 1)
                    if k >= 0:
                        f_down(turn, k)

            def carried(turn, k):
                f_unit(turn, FB - 2 + k)

            def alone(own, carry, last):
                carried(carry, 0)
                carried(carry, 1)
                if own is not None:
                    f_norm(own)
                    for k in range(-1, FB if last else FB - 2):
                        f_unit(own, k)

            def norm_for_b(s):
                if s.a is not None:
                    pe.wait_ge(a_sm, (s.a + 1) * 16)
                elif s.b > 0:
                    pe.wait_ge(b_ex, s.b * 2 * NBL)
                norm_transpose(at, second_turn(s.b), Q)

            def norm_for_a(s):
                if s.b is not None:
                    pe.wait_ge(b_ex, (s.b + 1) * 2 * NBL)
                else:
                    pe.wait_ge(a_sm, (s.a + 1) * 16)
                norm_transpose(at, first_turn(s.next_a), Q)

            def program(guarded):
                def phase1(s):
                    a, n, own, carry = s.a, first_turn(s.a), second_turn(s.c), first_turn(s.b)
                    b_done = a - 1 if s.b is not None and a is not None else 0

                    def unit(k):
                        f_unit(own, k)

                    def kv(t):
                        pe.wait_ge(at.lo, n * 2 + t // 2 + 1)
                        if t < 2 and needed(b_done * NT):
                            pe.wait_ge(b_out, b_done * NT)
                            pe.wait_ge(b_yn, b_done * NBL)
                        if t >= 2:
                            pe.wait_ge(a_kt_s, a * (NT - 1) + t - 1)
                        lo, width = (D, 2 * D) if t < NT - 1 else (2 * D, D)
                        three(Q[2 + t % 2][:, 0:width],
                              lambda k: (at.xh[:, k, t * P:(t + 1) * P], at.xl[:, k, t * P:(t + 1) * P]),
                              lambda k: (wqkv_h[:, k, lo:lo + width], wqkv_l[:, k, lo:lo + width]), KB).then_inc(a_kv, 1)

                    def qk(m):
                        if m == 0:
                            pe.wait_ge(at.lo, n * 2 + 2)
                        if m >= 2:
                            pe.wait_ge(a_ph, a * 4 + m - 1)
                        three(Q[m % 2][:], lambda k: (wqkv_h[:, k, m * P:(m + 1) * P], wqkv_l[:, k, m * P:(m + 1) * P]),
                              lambda k: (at.xh[:, k, :], at.xl[:, k, :]), KB).then_inc(a_qk, 1)

                    def scores(ch):
                        if ch == 0:
                            pe.wait_ge(a_qz_s, (a + 1) * 4)
                            pe.wait_ge(a_ph, (a + 1) * 4)
                        for r in range(4):
                            if 4 * ch + r >= 2:
                                pe.wait_ge(a_sm, a * 16 + 4 * ch + r - 1)
                            rows = slice(32 * r, 32 * r + 32)
                            for k in range(KB):
                                mm = pe.matmul(Q[r % 2][:, k * 2 * P:(k + 1) * 2 * P].rearrange("p (e q) -> p e q", e=2),
                                               a_kT[rows, k, ch * P:(ch + 1) * P], a_qz[rows, k, :, ch * P:(ch + 1) * P],
                                               start=(k == 0), stop=(k == KB - 1), skip_group_check=True)
                            mm.then_inc(a_sc, 1)

                    def state(ch):
                        pe.wait_ge(a_v_s, a * NT + (NT if ch == 0 else ch + 1))
                        pe.wait_ge(a_kt_s, a * (NT - 1) + ch + 1)
                        if ch:
                            pe.wait_ge(a_st, a * 3 + ch)
                        for k in range(KB):
                            mm = pe.matmul(Q[3][:, k * HB * HV:(k + 1) * HB * HV].rearrange("p (h j) -> p h j", h=HB),
                                           a_kt[:, ch, k * P:(k + 1) * P], a_v[:, ch, k * HB:(k + 1) * HB, :],
                                           start=(ch == 0 and k == 0), stop=True, skip_group_check=True)
                        mm.then_inc(a_u, 1)

                    def numer(ch):
                        pe.wait_ge(a_sm, a * 16 + 4 * ch + 4)
                        pe.wait_ge(a_v_s, a * NT + ch + 1)
                        if ch:
                            pe.wait_ge(a_st, a * 3 + ch)
                            pe.wait_ge(a_out, a * NT + ch)
                        else:
                            pe.wait_ge(a_kt_s, (a + 1) * (NT - 1))
                        first = True
                        if ch:
                            for k in range(KB):
                                pe.matmul(Q[2][:, k * HB * HV:(k + 1) * HB * HV], a_qT[:, k, ch * P:(ch + 1) * P],
                                          a_state[:, (ch - 1) % 2, k * HB * HV:(k + 1) * HB * HV],
                                          start=first, stop=False, skip_group_check=True)
                                first = False
                        for r in range(4):
                            for j in range(4):
                                k, e = divmod(j, 2)
                                h = k * HB + 2 * r + e
                                mm = pe.matmul(Q[2][:, h * HV:(h + 1) * HV], a_s[:, ch % 2, r, j * P:(j + 1) * P],
                                               a_v[:, ch, h, :], start=first, stop=True, skip_group_check=True)
                                first = False
                        mm.then_inc(a_o, 1)

                    def turn_y(ch):
                        pe.wait_ge(a_yn, a * NT + ch + 1)
                        for k in range(KB):
                            mm = pe.transpose(Q[2][:, k * P:(k + 1) * P], a_y[:, k * P:(k + 1) * P], ident)
                        mm.then_inc(a_t, 1)

                    def project(ch):
                        pe.wait_ge(a_l, a * NT + ch + 1)
                        three(Q[2][:, 0:D], lambda k: (a_yh[:, k, :], a_yl[:, k, :]),
                              lambda k: (wout_h[:, k, :], wout_l[:, k, :]), KB).then_inc(a_p, 1)

                    if a is None:
                        alone(own, carry, s.last)
                        if s.b is not None:
                            norm_for_b(s)
                        return
                    kv(0)
                    kv(1)
                    carried(carry, 0)
                    kv(2)
                    kv(3)
                    carried(carry, 1)
                    qk(0)
                    qk(1)
                    if own is not None:
                        f_norm(own)
                    qk(2)
                    unit(-1)
                    qk(3)
                    unit(0)
                    scores(0)
                    state(0)
                    numer(0)
                    unit(1)
                    for ch in range(NT):
                        if ch + 1 < NT:
                            scores(ch + 1)
                        elif s.b is not None:
                            norm_for_b(s)
                        turn_y(ch)
                        unit(2 + ch)
                        project(ch)
                        if ch + 1 < NT:
                            if ch + 1 < NT - 1:
                                state(ch + 1)
                            numer(ch + 1)

                def phase2(s):
                    b, n, own, carry = s.b, second_turn(s.b), first_turn(s.a), second_turn(s.c)
                    a_done = NSEQ if s.a is None else s.a + 1

                    def unit(k):
                        f_unit(own, k)

                    def qkv(t):
                        pe.wait_ge(at.lo, n * 2 + t // 2 + 1)
                        if t == 0:
                            pe.wait_ge(a_out, a_done * NT)
                            pe.wait_ge(a_st, a_done * 3)
                        if t >= 2:
                            pe.wait_ge(b_qn_s, b * NT + t - 1)
                        three(Q[2 + t % 2][:, 0:NB],
                              lambda k: (at.xh[:, k, t * P:(t + 1) * P], at.xl[:, k, t * P:(t + 1) * P]),
                              lambda k: (wb_h[:, k, :], wb_l[:, k, :]), KB).then_inc(b_qkv, 1)

                    def turn_qk(t):
                        pe.wait_ge(b_lo, b * NT + t + 1)
                        for j in range(3):
                            free = b * 12 + 3 * t + (0, 0, 1)[j]
                            if (t or j == 2) and needed(free):
                                pe.wait_ge(b_te, free)
                            src = b_ks[:] if j == 2 else b_qs[:, 8 * j:8 * j + 8]
                            src = src.rearrange("p h s d -> p (h s d)")
                            for r in range(2 if j == 2 else REP):
                                mm = pe.transpose(Q[j % 2][:, r * P:(r + 1) * P].bitcast(F32R),
                                                  src[:, r * P:(r + 1) * P], ident_r[:])
                            mm.then_inc(b_t, 1)

                    def keys(bl, g2, gp):
                        rows = slice(64 * g2, 64 * g2 + 64)
                        if bl % 2:
                            return b_kT[rows, gp, (bl - 1) * W:(bl + 1) * W]
                        return b_kTm[rows, gp, bl // 2, 0:(P if bl else W)]

                    def for_max(bl, g2, nk):
                        dst = Q[g2][:, 0:4 * nk].rearrange("p (u k) -> p u k", u=4)
                        pe.matmul(dst, ident_b[:], qmask[:, 1 - bl % 2, 0:nk].unsqueeze(1).broadcast_to([P, 4, nk]),
                                  start=True, stop=False, skip_group_check=True)
                        for gp in range(2):
                            for rp in range(2):
                                mm = pe.matmul(dst[:, 2 * gp + rp, :],
                                               b_qT[64 * g2:64 * g2 + 64, gp, bl, rp * P:(rp + 1) * P],
                                               keys(bl, g2, gp), start=False, stop=True, skip_group_check=True)
                        mm.then_inc(b_mm, 1)

                    def scores(bl):
                        nk = W if bl == 0 else P
                        j = b * NBL + bl
                        if bl == 0:
                            pe.wait_ge(b_te, (b + 1) * 12)
                            pe.wait_ge(b_km, (b + 1) * 7)
                        for g2 in range(2):
                            if bl:
                                pe.wait_ge(b_ex, j * 2 - 1 + g2)
                            if guarded:
                                for_max(bl, g2, nk)
                                pe.wait_ge(b_mx, j * 2 + g2 + 1)
                            dst = Q[g2][0:nk, :]
                            pe.matmul(dst.rearrange("p (u q) -> p u q", u=8), ident_b[:, 0:nk],
                                      kmask[:, 1 - bl % 2, :].unsqueeze(1).broadcast_to([P, 8, W]),
                                      start=True, stop=False, skip_group_check=True)
                            for gp in range(2):
                                mm = pe.matmul(dst[:, gp * REP * W:(gp + 1) * REP * W], keys(bl, g2, gp),
                                               b_qT[64 * g2:64 * g2 + 64, gp, bl, :],
                                               start=False, stop=not guarded, skip_group_check=True)
                            if guarded:
                                for u in range(4):
                                    mm = pe.matmul(dst[:, u * P:(u + 1) * P],
                                                   b_m[:, bl % 2, 4 * g2 + u:4 * g2 + u + 1].broadcast_to([P, nk]),
                                                   neg_ident[:], start=False, stop=True, skip_group_check=True)
                            mm.then_inc(b_s, 1)

                    def numer(bl):
                        nk = W if bl == 0 else P
                        pe.wait_ge(b_ex, (b * NBL + bl + 1) * 2)
                        if bl == 0:
                            pe.wait_ge(b_vm_s, (b + 1) * 7)
                        if bl == 0:
                            pe.wait_ge(b_qn_s, (b + 1) * NT)
                        elif bl % 2:
                            if bl > 1:
                                pe.wait_ge(b_yn, b * NBL + bl - 1)
                        else:
                            pe.wait_ge(b_out, b * NT + bl // 2)
                        v = (b_v[:, (bl - 1) // 2] if bl % 2 else b_vm[:, bl // 2])
                        first = True
                        for g in range(KVH):
                            gp, g2 = divmod(g, 2)
                            for rp in range(2):
                                u = 2 * g + rp
                                mm = pe.matmul(Q[2 + bl % 2][:, u * HV:(u + 1) * HV],
                                               b_p[0:nk, bl % 2, g2, gp * 256 + rp * P:gp * 256 + (rp + 1) * P],
                                               v[0:nk, g, :], start=first, stop=True, skip_group_check=True)
                                first = False
                        mm.then_inc(b_o, 1)

                    def turn_y(t):
                        pe.wait_ge(b_yn, b * NBL + 2 * t + 2)
                        for e in range(2):
                            mm = pe.transpose(Q[2][:, e * P:(e + 1) * P], b_y[:, e, :], ident)
                        mm.then_inc(b_t2, 1)

                    def project(t):
                        pe.wait_ge(b_l2, b * NT + t + 1)
                        three(Q[2][:, 0:D], lambda k: (b_yh[:, k, :], b_yl[:, k, :]),
                              lambda k: (wob_h[:, k, :], wob_l[:, k, :]), 2).then_inc(b_pp, 1)

                    if b is None:
                        alone(own, carry, False)
                        norm_for_a(s)
                        return
                    qkv(0)
                    qkv(1)
                    carried(carry, 0)
                    qkv(2)
                    carried(carry, 1)
                    qkv(3)
                    turn_qk(0)
                    if own is not None:
                        f_norm(own)
                    turn_qk(1)
                    unit(-1)
                    turn_qk(2)
                    unit(0)
                    turn_qk(3)
                    scores(0)
                    unit(1)
                    for t in range(NT):
                        scores(2 * t + 1)
                        numer(2 * t)
                        if 2 * t + 2 < NBL:
                            scores(2 * t + 2)
                        numer(2 * t + 1)
                        if t == NT - 1 and s.next_a is not None:
                            norm_for_a(s)
                        if own is not None:
                            f_up(own, 3 + t)
                        turn_y(t)
                        if own is not None:
                            f_down(own, 2 + t)
                        project(t)

                norm_transpose(at, 0, Q)
                steps(pe, phase1, phase2)

            both_ways(pe, program)


        @block.scalar
        def _(act):
            def norm_hi(n, turn, banks):
                for hf in range(2):
                    act.wait_ge(n.turned, turn * 2 + hf + 1)
                    act.activation(n.xh[:, :, hf * D:(hf + 1) * D],
                                   banks[hf][:, :].rearrange("p (k n) -> p k n", k=KB), ACT.Copy).then_inc(n.hi, 1)

            def f_norm(turn):
                if needed(turn * FB):
                    act.wait_ge(f_h, turn * FB)
                norm_hi(ff, turn, HID)

            def f_relu(turn, fb):
                act.wait_ge(f_h, turn * FB + fb + 1)
                if needed(turn * FB + fb - 1):
                    act.wait_ge(f_lo, turn * FB + fb - 1)
                    act.wait_ge(f_w2, turn * FB + fb - 1)
                act.activation(f_r[:, fb % 2, :], HID[fb % 2][:], ACT.Relu, bias=b1c[:, fb:fb + 1]).then_inc(f_rr, 1)
                act.activation(f_hh[:, fb % 2, :], HID[fb % 2][:], ACT.Relu, bias=b1c[:, fb:fb + 1]).then_inc(f_act, 1)

            def alone(own, carry, last):
                if carry is not None:
                    f_relu(carry, FB - 1)
                if own is not None:
                    f_norm(own)
                    for k in range(FB if last else FB - 1):
                        f_relu(own, k)

            def norm_for_b(s):
                done = (NSEQ if s.a is None else s.a + 1) * 4
                act.wait_ge(a_qk, done)
                act.wait_ge(a_kv, done)
                norm_hi(at, second_turn(s.b), Q)

            def norm_for_a(s):
                if s.b is not None:
                    act.wait_ge(b_qkv, (s.b + 1) * NT)
                else:
                    act.wait_ge(a_qk, (s.a + 1) * 4)
                    act.wait_ge(a_kv, (s.a + 1) * NT)
                norm_hi(at, first_turn(s.next_a), Q)

            def program(guarded):
                def phase1(s):
                    a, own, carry = s.a, second_turn(s.c), first_turn(s.b)

                    def relu(fb, turn=own):
                        if turn is not None:
                            f_relu(turn, fb)

                    def kv(t):
                        act.wait_ge(a_kv, a * NT + t + 1)
                        src, v_at = Q[2 + t % 2], D
                        if t < NT - 1:
                            if needed(a * (NT - 1) + t - 1):
                                act.wait_ge(a_kt_s, a * (NT - 1) + t - 1)
                            act.activation(a_ek[:, t % 2, :], src[:, 0:D], ACT.Exp).then_inc(a_ek_s, 1)
                        else:
                            v_at = 0
                        if t == 0 and needed(a * NT):
                            act.wait_ge(a_o, a * NT)
                        act.activation(a_v[:, t, :, 0:HD], src[:, v_at:v_at + D].rearrange("p (h j) -> p h j", h=H),
                                       ACT.Copy).then_inc(a_v_s, 1)

                    def q_exp(m):
                        act.wait_ge(a_qk, a * 4 + m + 1)
                        if needed(a * 4 + m - 1):
                            act.wait_ge(a_ph, a * 4 + m - 1)
                        act.activation(a_eq[:, m % 2, :], Q[m % 2][:], ACT.Exp).then_inc(a_eq_s, 1)

                    def y_hi(ch):
                        act.wait_ge(a_t, a * NT + ch + 1)
                        if needed(a * NT + ch):
                            act.wait_ge(a_p, a * NT + ch)
                        act.activation(a_yh[:], Q[2][:, 0:D].rearrange("p (k n) -> p k n", k=KB), ACT.Copy).then_inc(a_h, 1)

                    if a is None:
                        alone(own, carry, s.last)
                        if s.b is not None:
                            norm_for_b(s)
                        return
                    kv(0)
                    kv(1)
                    relu(FB - 1, carry)
                    kv(2)
                    kv(3)
                    q_exp(0)
                    q_exp(1)
                    if own is not None:
                        f_norm(own)
                    q_exp(2)
                    relu(0)
                    q_exp(3)
                    relu(1)
                    relu(2)
                    for ch in range(NT):
                        if ch == NT - 1 and s.b is not None:
                            norm_for_b(s)
                        y_hi(ch)
                        relu(3 + ch)

                def phase2(s):
                    b, own, carry = s.b, first_turn(s.a), second_turn(s.c)

                    def relu(fb, turn=own):
                        if turn is not None:
                            f_relu(turn, fb)

                    def squares(t):
                        act.wait_ge(b_qkv, b * NT + t + 1)
                        if needed(b * NT + t):
                            act.wait_ge(b_ss_s, b * NT + t)
                        act.activation(b_sq[:], Q[2 + t % 2][:, 0:QK], ACT.Square).then_inc(b_sq_s, 1)
                        if t == 0 and needed(b * NBL):
                            act.wait_ge(b_o, b * NBL)
                        act.activation(b_v[:, t, :, 0:HD], Q[2 + t % 2][:, QK:NB].rearrange("p (h j) -> p h j", h=KVH),
                                       ACT.Copy).then_inc(b_v_s, 1)

                    def stack_hi(t):
                        act.wait_ge(b_qr_s, b * NT + t + 1)
                        if needed(b * 12 + 3 * t):
                            act.wait_ge(b_t, b * 12 + 3 * t)
                        act.activation(b_qs[:, :, 0:2, :], b_qr[:, t % 2, 0:H, :].unsqueeze(2).broadcast_to([P, H, 2, HD]),
                                       ACT.Copy).then_inc(b_hi, 1)
                        act.activation(b_ks[:, :, 0::2, :], b_qr[:, t % 2, H:, :].unsqueeze(2).broadcast_to([P, KVH, 2, HD]),
                                       ACT.Copy).then_inc(b_hi, 1)

                    def evacuate(t):
                        if t == 0 and needed(b * 2 * NBL):
                            act.wait_ge(b_s, b * 2 * NBL)
                        for j in range(3):
                            act.wait_ge(b_t, b * 12 + 3 * t + j + 1)
                            if j < 2:
                                act.activation(b_qT[:, j, 2 * t:2 * t + 2, :].rearrange("p e (r q) -> p r e q", r=REP),
                                               Q[j][:, :].rearrange("p (r e q) -> p r e q", r=REP, e=2), ACT.Copy).then_inc(b_te, 1)
                            else:
                                act.activation(b_kT[:, :, t * P:(t + 1) * P],
                                               Q[0][:, 0:2 * P].rearrange("p (r n) -> p r n", r=2), ACT.Copy).then_inc(b_te, 1)

                    def exps(bl):
                        nk = W if bl == 0 else P
                        j = b * NBL + bl
                        if needed(j - 1):
                            act.wait_ge(b_o, j - 1)
                        for g2 in range(2):
                            act.wait_ge(b_s, j * 2 + g2 + 1)
                            act.activation(b_p[0:nk, bl % 2, g2, :], Q[g2][0:nk, :], ACT.Exp).then_inc(b_ex, 1)

                    def y_hi(t):
                        act.wait_ge(b_t2, b * NT + t + 1)
                        if needed(b * NT + t):
                            act.wait_ge(b_pp, b * NT + t)
                        act.activation(b_yh[:].rearrange("p r (e q) -> p r e q", e=2),
                                       Q[2][:, 0:D].rearrange("p (e r q) -> p r e q", e=2, r=2), ACT.Copy).then_inc(b_h2, 1)

                    if b is None:
                        alone(own, carry, False)
                        norm_for_a(s)
                        return
                    squares(0)
                    squares(1)
                    relu(FB - 1, carry)
                    squares(2)
                    squares(3)
                    stack_hi(0)
                    evacuate(0)
                    if own is not None:
                        f_norm(own)
                    stack_hi(1)
                    evacuate(1)
                    relu(0)
                    stack_hi(2)
                    evacuate(2)
                    relu(1)
                    stack_hi(3)
                    evacuate(3)
                    exps(0)
                    relu(2)
                    for t in range(NT):
                        exps(2 * t + 1)
                        if 2 * t + 2 < NBL:
                            exps(2 * t + 2)
                        elif s.next_a is not None:
                            norm_for_a(s)
                        y_hi(t)
                        relu(3 + t)

                norm_hi(at, 0, Q)
                steps(act, phase1, phase2)

            both_ways(act, program)


        @block.vector
        def _(dve):
            dve.wait_ge(loaded, 16 * N_LOADS)
            dve.tensor_reduce(gsum[:, 0:1], st_w1, X, ALU.add, apply_absolute_value=True).then_inc(setup, 1)
            dve.tensor_reduce(gsum[:, 1:2], st_w2, X, ALU.add, apply_absolute_value=True).then_inc(setup, 1)
            n = 0
            pairs = [(wqkv_h, wqkv_l, st_a[:, 0:KB * 3 * D], KB), (wout_h, wout_l, st_a[:, KB * 3 * D:KB * 4 * D], KB),
                     (wb_h, wb_l, st_b[:, 0:KB * NB], KB)]
            for hi, _, src, k in pairs:
                dve.tensor_copy(hi[:], src.rearrange("p (k n) -> p k n", k=k)).then_inc(prepared, 1)
                n += 1
            dve.tensor_copy(b2_h[:], b2f[:]).then_inc(prepared, 1)
            n += 1
            dve.wait_ge(prepared, n)
            for hi, lo, src, k in pairs:
                dve.tensor_tensor(lo[:], src.rearrange("p (k n) -> p k n", k=k), hi[:], ALU.subtract).then_inc(prepared, 1)
                n += 1
            dve.tensor_tensor(b2_l[:], b2f[:], b2_h[:], ALU.subtract).then_inc(prepared, 1)
            n += 1
            wo = st_b[:, KB * NB:KB * NB + 2 * D].rearrange("p (o n) -> p o n", o=2)
            mixed = x3[:, 0:2, :]
            for i in range(2):
                dve.tensor_scalar(mixed[:, i, :], wo[:, 0, :], mixc[:, i:i + 1], None, ALU.mult).then_inc(setup, 1)
            dve.wait_ge(setup, 4)
            for i in range(2):
                dve.scalar_tensor_tensor(out=mixed[:, i, :], in0=wo[:, 1, :], scalar=mixc[:, 2 + i:3 + i],
                                         in1=mixed[:, i, :], op0=ALU.mult, op1=ALU.add).then_inc(setup, 1)
            dve.wait_ge(setup, 6)
            dve.tensor_copy(wob_h[:], mixed).then_inc(prepared, 1)
            n += 1
            dve.wait_ge(prepared, n)
            dve.tensor_tensor(wob_l[:], mixed, wob_h[:], ALU.subtract).then_inc(prepared, 1)
            n += 1
            dve.wait_ge(setup_pe, 1)
            dve.tensor_scalar(thr[:, 0:2], Q[0][:, 0:2], 1.0 / (FF * D), Q_EPS, ALU.mult, ALU.add).then_inc(setup, 1)
            dve.wait_ge(setup, 7)
            dve.tensor_scalar(thr[:, 2:4], thr[:, 0:2], -0.5, None, ALU.mult).then_inc(setup, 1)
            dve.wait_ge(setup, 8)
            dve.tensor_scalar(thr[:, 0:2], thr[:, 0:2], 0.5, None, ALU.mult).then_inc(setup, 1)
            dve.wait_ge(setup, 9)
            below = [t[:].rearrange("p k n -> p (k n)") for t in (x1, x2, at.xn, ff.xn)]
            m = 9
            for j, (dst, src, k) in enumerate(((w1t, st_w1, KB), (w2t, st_w2, FB))):
                for half in range(2):
                    part = slice(half * 1024, (half + 1) * 1024)
                    dve.tensor_scalar(below[2 * j + half], src[:, part], thr[:, 2 + j:3 + j], None, ALU.is_lt).then_inc(setup, 1)
                m += 2
                dve.wait_ge(setup, m)
                flat = dst[:].rearrange("p k n -> p (k n)")
                for half in range(2):
                    part = slice(half * 1024, (half + 1) * 1024)
                    dve.scalar_tensor_tensor(out=flat[:, part], in0=src[:, part], scalar=thr[:, j:j + 1], in1=below[2 * j + half],
                                             op0=ALU.is_gt, op1=ALU.subtract).then_inc(prepared, 1)
                    n += 1
            dve.tensor_copy(ident_b[:], ident).then_inc(prepared, 1)
            dve.tensor_copy(ident_r[:], ident).then_inc(prepared, 1)
            dve.tensor_scalar(neg_ident[:], ident, -1.0, None, ALU.mult).then_inc(prepared, 1)
            dve.tensor_copy(kmask[:, 0, :], C["kodd"]).then_inc(prepared, 1)
            dve.tensor_copy(kmask[:, 1, :], C["keven"]).then_inc(prepared, 1)
            dve.tensor_copy(qmask[:, 0, :], C["qodd"]).then_inc(prepared, 1)
            dve.wait_ge(ones_set, 5)
            dve.tensor_copy(qmask[:, 1, :], C["qeven"]).then_inc(prepared, 1)
            dve.tensor_copy(ones_r[:], ones_f[0:1, :]).then_inc(prepared, 1)
            dve.tensor_reduce(wide_f[:, 0:1], gains[:, 0:H], X, ALU.max, apply_absolute_value=True).then_inc(setup, 1)
            dve.wait_ge(setup, m + 1)
            dve.tensor_scalar(wide_f[:, 1:2], wide_f[:, 0:1], SAFE_SCORE / HD ** 0.5, None, ALU.is_le).then_inc(setup, 1)
            dve.wait_ge(setup, m + 2)
            dve.tensor_scalar(wide_i[:], wide_f[:, 1:2], -1.0, 1.0, ALU.mult, ALU.add).then_inc(prepared, 1)
            dve.tensor_scalar(gains[:, 0:H], gains[:, 0:H], HD ** -0.5, None, ALU.mult).then_inc(prepared, 1)
            assert n + 10 == N_PREPARED

            def norm_stats(n, turn, src, tiles):
                if tiles[0] == 0 and needed(turn * NT):
                    dve.wait_ge(n.stats, turn * NT)
                    dve.wait_ge(n.ready, turn)
                    dve.wait_ge(n.normed, turn * NT)
                for t in tiles:
                    dve.bn_stats(n.st[:, t, :], src[:, t, :]).then_inc(n.bn, 1)
                for t in tiles:
                    dve.wait_ge(n.bn, turn * NT + t + 1)
                    dve.sem_inc(dve_gate)
                    dve.bn_aggr(n.mv[:, t, :], n.st[:, t, :]).then_inc(n.stats, 1)

            def norm_apply(n, turn, src):
                dve.wait_ge(n.ready, turn + 1)
                if needed(turn * 2):
                    dve.wait_ge(n.turned, turn * 2)
                for t in range(NT):
                    dve.tensor_scalar(n.xn[:, t, :], src[:, t, :], n.mv[:, t, 0:1], n.rstd[:, t:t + 1],
                                      ALU.subtract, ALU.mult).then_inc(n.normed, 1)

            def norm_lo(n, turn, banks):
                for hf in range(2):
                    dve.wait_ge(n.hi, turn * 2 + hf + 1)
                    dve.tensor_tensor(n.xl[:, :, hf * D:(hf + 1) * D], banks[hf][:, :].rearrange("p (k n) -> p k n", k=KB),
                                      n.xh[:, :, hf * D:(hf + 1) * D], ALU.subtract).then_inc(n.lo, 1)

            def f_lo_part(turn, fb):
                if turn is not None:
                    dve.wait_ge(f_act, turn * FB + fb + 1)
                    if needed(turn * FB + fb - 1):
                        dve.wait_ge(f_w2, turn * FB + fb - 1)
                    dve.tensor_tensor(f_hl[:, fb % 2, :], f_r[:, fb % 2, :], f_hh[:, fb % 2, :], ALU.subtract).then_inc(f_lo, 1)

            def f_apply(turn, src):
                if turn is not None:
                    norm_apply(ff, turn, src)

            def f_norm_lo(turn):
                if turn is not None:
                    norm_lo(ff, turn, HID)

            def f_finish(turn, src, dst):
                if turn is not None:
                    dve.wait_ge(f_w2, (turn + 1) * FB)
                    for y in range(2):
                        dve.tensor_tensor(dst[:, 2 * y:2 * y + 2, :], Y[y][:, :].rearrange("p (t n) -> p t n", t=2),
                                          src[:, 2 * y:2 * y + 2, :], ALU.add).then_inc(f_out, 1)

            def finish_first(s):
                if s.b is not None:
                    if needed(s.b * NT):
                        dve.wait_ge(b_out, s.b * NT)
                    f_finish(first_turn(s.b), x1, x2)

            def finish_second(s):
                if s.c is not None:
                    f_finish(second_turn(s.c), x3, x3)

            def stats_for_b(s):
                dve.wait_ge(f_out, 2 * (first_turn(s.b) + 1))
                norm_stats(at, second_turn(s.b), x2, range(NT))

            def stats_for_a(s):
                dve.wait_ge(x_in, (s.next_a + 1) * 16)
                norm_stats(at, first_turn(s.next_a), x0, range(NT))

            def alone(own, src, carry, finish, stats, apply, lo, last):
                f_lo_part(carry, FB - 2)
                f_apply(own, src)
                f_lo_part(carry, FB - 1)
                if carry is not None:
                    finish()
                if stats is not None:
                    stats()
                    apply()
                f_norm_lo(own)
                if own is not None:
                    for k in range(FB if last else FB - 2):
                        f_lo_part(own, k)
                if lo is not None:
                    lo()

            def program(guarded):
                def phase1(s):
                    a, own, carry = s.a, second_turn(s.c), first_turn(s.b)
                    turn_b = second_turn(s.b)

                    def k_phi(t):
                        dve.wait_ge(a_mk, a * (NT - 1) + t + 1)
                        dve.wait_ge(a_v_s, a * NT + t + 1)
                        if t == 0 and needed(a * 3):
                            dve.wait_ge(a_u, a * 3)
                        dve.scalar_tensor_tensor(out=a_kt[:, t, :], in0=Q[2 + t % 2][:, 0:D], scalar=1.0, in1=a_ek[:, t % 2, :],
                                                 op0=ALU.add, op1=ALU.max).then_inc(a_kt_s, 1)

                    def phi(m):
                        dve.wait_ge(a_mq, a * 4 + m + 1)
                        if m == 0 and needed(a * NT):
                            dve.wait_ge(a_o, a * NT)
                        dst = (a_qT if m < 2 else a_kT)[:, m % 2, :]
                        dve.scalar_tensor_tensor(out=dst, in0=Q[m % 2][:], scalar=1.0, in1=a_eq[:, m % 2, :],
                                                 op0=ALU.add, op1=ALU.max).then_inc(a_ph, 1)
                        if m < 2:
                            dve.wait_ge(a_ph, a * 4 + m + 1)
                            for e in range(2):
                                dve.tensor_scalar(a_qz[:, m, e, :], a_qT[:, m, :], C["parity"][:, e:e + 1], None,
                                                  ALU.mult).then_inc(a_qz_s, 1)

                    def mask(ch):
                        if needed(a * NT + ch - 1):
                            dve.wait_ge(a_o, a * NT + ch - 1)
                        for r in range(4):
                            dve.wait_ge(a_sc, a * 16 + 4 * ch + r + 1)
                            dve.tensor_tensor(a_s[:, ch % 2, r, :].rearrange("p (h q) -> p h q", h=4),
                                              Q[r % 2][:, :].rearrange("p (h q) -> p h q", h=4),
                                              causal.unsqueeze(1).broadcast_to([P, 4, P]), ALU.mult).then_inc(a_sm, 1)

                    def state(ch):
                        dve.wait_ge(a_u, a * 3 + ch + 1)
                        if needed(a * NT + ch):
                            dve.wait_ge(a_o, a * NT + ch)
                        dve.tensor_tensor(a_state[:, ch % 2, :].rearrange("p (k n) -> p k n", k=KB),
                                          Q[3][:, 0:KB * HB * HV].rearrange("p (k n) -> p k n", k=KB),
                                          C["heads"].unsqueeze(1).broadcast_to([P, KB, HB * HV]), ALU.mult).then_inc(a_st, 1)

                    def normalise(ch):
                        o = Q[2][:, 0:H * HV].rearrange("p (h j) -> p h j", h=H)
                        steps_before = a * 2 * NT + 2 * ch
                        dve.wait_ge(a_o, a * NT + ch + 1)
                        dve.tensor_scalar(a_den[:, 0, :], o[:, :, HD], A_EPS, None, ALU.add).then_inc(a_dn, 1)
                        dve.wait_ge(a_dn, steps_before + 1)
                        dve.reciprocal(a_den[:, 1, :], a_den[:, 0, :]).then_inc(a_dn, 1)
                        dve.wait_ge(a_dn, steps_before + 2)
                        if needed(a * NT + ch):
                            dve.wait_ge(a_t, a * NT + ch)
                        dve.tensor_tensor(a_y[:].rearrange("p (h j) -> p h j", h=H), o[:, :, 0:HD],
                                          a_den[:, 1, :].unsqueeze(2).broadcast_to([P, H, HD]), ALU.mult).then_inc(a_yn, 1)

                    def y_lo(ch):
                        dve.wait_ge(a_h, a * NT + ch + 1)
                        dve.tensor_tensor(a_yl[:], Q[2][:, 0:D].rearrange("p (k n) -> p k n", k=KB), a_yh[:],
                                          ALU.subtract).then_inc(a_l, 1)

                    def residual(ch):
                        dve.wait_ge(a_p, a * NT + ch + 1)
                        if ch == 0 and carry is not None:
                            dve.wait_ge(f_out, (carry + 1) * 2)
                        dve.tensor_tensor(x1[:, ch, :], Q[2][:, 0:D], x0[:, ch, :], ALU.add).then_inc(a_out, 1)

                    def f1_stats(ch):
                        dve.wait_ge(a_out, a * NT + ch + 1)
                        norm_stats(ff, first_turn(a), x1, [ch])

                    if a is None:
                        if s.last:
                            alone(own, x3, None, None, None, None, None, True)
                            finish_second(s)
                        else:
                            alone(own, x3, carry, lambda: finish_first(s), lambda: stats_for_b(s),
                                  lambda: norm_apply(at, turn_b, x2), lambda: norm_lo(at, turn_b, Q), False)
                        return
                    f_lo_part(carry, FB - 2)
                    k_phi(0)
                    k_phi(1)
                    f_apply(own, x3)
                    f_lo_part(carry, FB - 1)
                    k_phi(2)
                    finish_first(s)
                    phi(0)
                    phi(1)
                    f_norm_lo(own)
                    phi(2)
                    phi(3)
                    f_lo_part(own, 0)
                    mask(0)
                    f_lo_part(own, 1)
                    state(0)
                    normalise(0)
                    for ch in range(NT):
                        f_lo_part(own, 2 + ch)
                        if ch + 1 < NT:
                            mask(ch + 1)
                        y_lo(ch)
                        if ch == NT - 1 and s.b is not None:
                            norm_lo(at, turn_b, Q)
                        residual(ch)
                        f1_stats(ch)
                        if ch + 1 < NT:
                            if ch + 1 < NT - 1:
                                state(ch + 1)
                            normalise(ch + 1)
                        if s.b is not None:
                            if ch == 1:
                                stats_for_b(s)
                            if ch == 2:
                                norm_apply(at, turn_b, x2)

                def phase2(s):
                    b, own, carry = s.b, first_turn(s.a), second_turn(s.c)
                    turn_a = first_turn(s.next_a)

                    def sums(t):
                        dve.wait_ge(b_sq_s, b * NT + t + 1)
                        if needed(b * NT + t):
                            dve.wait_ge(b_rs_s, b * NT + t)
                        dve.tensor_reduce(b_ss[:], b_sq[:].rearrange("p (h j) -> p h j", j=HD), X, ALU.add).then_inc(b_ss_s, 1)

                    def norm_qk(t):
                        dve.wait_ge(b_rs_s, b * NT + t + 1)
                        dve.wait_ge(b_v_s, b * NT + t + 1)
                        if needed(b * NT + t - 1):
                            dve.wait_ge(b_qr_s, b * NT + t - 1)
                        dve.tensor_tensor(b_qn[:, t % 2], Q[2 + t % 2][:, 0:QK].rearrange("p (h j) -> p h j", j=HD),
                                          b_rs[:].unsqueeze(2).broadcast_to([P, H + KVH, HD]), ALU.mult).then_inc(b_qn_s, 1)

                    def even_v(t):
                        dve.tensor_copy(b_vm[0:W, t, :, 0:HD], b_v[0:W, t, :, 0:HD]).then_inc(b_vm_s, 1)
                        if t + 1 < NT:
                            dve.tensor_copy(b_vm[W:P, t + 1, :, 0:HD], b_v[W:P, t, :, 0:HD]).then_inc(b_vm_s, 1)

                    def stack_lo(t):
                        dve.wait_ge(b_hi, (b * NT + t + 1) * 2)
                        dve.tensor_tensor(b_qs[:, :, 2:4, :], b_qr[:, t % 2, 0:H, :].unsqueeze(2).broadcast_to([P, H, 2, HD]),
                                          b_qs[:, :, 0:2, :], ALU.subtract)
                        dve.tensor_tensor(b_ks[:, :, 1::2, :], b_qr[:, t % 2, H:, :].unsqueeze(2).broadcast_to([P, KVH, 2, HD]),
                                          b_ks[:, :, 0::2, :], ALU.subtract).then_inc(b_lo, 1)

                    def even_keys(t):
                        dve.wait_ge(b_te, b * 12 + 3 * t + 3)
                        if t == 0 and needed(b * 2 * NBL):
                            dve.wait_ge(b_s, b * 2 * NBL)
                        dve.tensor_copy(b_kTm[:, :, t, 0:W], b_kT[:, :, t * P:t * P + W]).then_inc(b_km, 1)
                        if t + 1 < NT:
                            dve.tensor_copy(b_kTm[:, :, t + 1, W:P], b_kT[:, :, t * P + W:(t + 1) * P]).then_inc(b_km, 1)

                    def maxima(bl):
                        nk = W if bl == 0 else P
                        j = b * NBL + bl
                        if needed(j * 2 - 2):
                            dve.wait_ge(b_s, j * 2 - 2)
                        for g2 in range(2):
                            dve.wait_ge(b_mm, j * 2 + g2 + 1)
                            dve.tensor_reduce(b_m[:, bl % 2, 4 * g2:4 * g2 + 4],
                                              Q[g2][:, 0:4 * nk].rearrange("p (u k) -> p u k", u=4), X, ALU.max).then_inc(b_mx, 1)

                    def normalise(bl):
                        j = b * NBL + bl
                        o = Q[2 + bl % 2][:, 0:2 * KVH * HV].rearrange("p (h j) -> p h j", j=HV)
                        dve.wait_ge(b_o, j + 1)
                        dve.reciprocal(b_den[:, bl % 2, :], o[:, :, HD]).then_inc(b_dn, 1)
                        dve.wait_ge(b_dn, j + 1)
                        if needed(b * NT + bl // 2):
                            dve.wait_ge(b_t2, b * NT + bl // 2)
                        dve.tensor_tensor(b_y[:, bl % 2, :].rearrange("p (h j) -> p h j", j=HD), o[:, :, 0:HD],
                                          b_den[:, bl % 2, :].unsqueeze(2).broadcast_to([P, 2 * KVH, HD]), ALU.mult).then_inc(b_yn, 1)

                    def y_lo(t):
                        dve.wait_ge(b_h2, b * NT + t + 1)
                        dve.tensor_tensor(b_yl[:].rearrange("p r (e q) -> p r e q", e=2),
                                          Q[2][:, 0:D].rearrange("p (e r q) -> p r e q", e=2, r=2),
                                          b_yh[:].rearrange("p r (e q) -> p r e q", e=2), ALU.subtract).then_inc(b_l2, 1)

                    def residual(t):
                        dve.wait_ge(b_pp, b * NT + t + 1)
                        if t == 0 and needed(b * 16):
                            dve.wait_ge(stored, b * 16)
                        dve.tensor_tensor(x3[:, t, :], Q[2][:, 0:D], x2[:, t, :], ALU.add).then_inc(b_out, 1)

                    def f2_stats(t):
                        dve.wait_ge(b_out, b * NT + t + 1)
                        norm_stats(ff, second_turn(b), x3, [t])

                    if b is None:
                        alone(own, x1, None, None, lambda: stats_for_a(s), lambda: norm_apply(at, turn_a, x0),
                              lambda: norm_lo(at, turn_a, Q), False)
                        return
                    f_lo_part(carry, FB - 2)
                    sums(0)
                    norm_qk(0)
                    even_v(0)
                    sums(1)
                    f_apply(own, x1)
                    norm_qk(1)
                    even_v(1)
                    f_lo_part(carry, FB - 1)
                    sums(2)
                    norm_qk(2)
                    even_v(2)
                    finish_second(s)
                    sums(3)
                    stack_lo(0)
                    norm_qk(3)
                    even_v(3)
                    f_norm_lo(own)
                    stack_lo(1)
                    stack_lo(2)
                    f_lo_part(own, 0)
                    stack_lo(3)
                    for t in range(NT):
                        even_keys(t)
                    if guarded:
                        maxima(0)
                    f_lo_part(own, 1)
                    for t in range(NT):
                        if guarded:
                            maxima(2 * t + 1)
                        f_lo_part(own, 2 + t)
                        normalise(2 * t)
                        if guarded and 2 * t + 2 < NBL:
                            maxima(2 * t + 2)
                        normalise(2 * t + 1)
                        y_lo(t)
                        if t == NT - 1 and s.next_a is not None:
                            norm_lo(at, turn_a, Q)
                        residual(t)
                        f2_stats(t)
                        if s.next_a is not None:
                            if t == 1:
                                stats_for_a(s)
                            if t == 2:
                                norm_apply(at, turn_a, x0)

                dve.wait_ge(x_in, 16)
                norm_stats(at, 0, x0, range(NT))
                norm_apply(at, 0, x0)
                norm_lo(at, 0, Q)
                steps(dve, phase1, phase2)

            both_ways(dve, program)


        @block.gpsimd
        def _(pool):
            pool.memset(ones_f[:], 1.0).then_inc(ones_set, 1)
            pool.memset(mhalf[:], -0.5).then_inc(ones_set, 1)
            pool.memset(gains[:, H:], 1.0).then_inc(ones_set, 1)
            pool.memset(a_v[:, :, :, HD:HV], 1.0).then_inc(ones_set, 1)
            pool.memset(b_v[:, :, :, HD:HV], 1.0)
            pool.memset(b_vm[:, :, :, HD:HV], 1.0).then_inc(ones_set, 1)
            def root(tmp, exponent, chain, start, dst, ready):
                v, y, u = tmp[:, 0, :], tmp[:, 1, :], tmp[:, 2, :]
                pool.wait_ge(chain, start + 1)
                pool.tensor_tensor(y, v, exponent, ALU.pow).then_inc(chain, 1)
                pool.wait_ge(chain, start + 2)
                pool.tensor_tensor(u, y, y, ALU.mult).then_inc(chain, 1)
                pool.wait_ge(chain, start + 3)
                pool.tensor_tensor(u, u, v, ALU.mult).then_inc(chain, 1)
                pool.wait_ge(chain, start + 4)
                pool.sem_inc(pool_gate)
                pool.tensor_scalar(u, u, -0.5, 1.5, ALU.mult, ALU.add).then_inc(chain, 1)
                pool.wait_ge(chain, start + 5)
                last = pool.tensor_tensor(dst, y, u, ALU.mult)
                last.then_inc(ready, 1)

            def norm_rstd(n, turn):
                pool.wait_ge(n.stats, (turn + 1) * NT)
                if needed(turn * NT):
                    pool.wait_ge(n.normed, turn * NT)
                pool.sem_inc(pool_gate)
                pool.tensor_scalar(n.tmp[:, 0, :], n.mv[:, :, 1], 1.0, LN_EPS, ALU.mult, ALU.add).then_inc(n.chain, 1)
                root(n.tmp, mhalf[:, 0:NT], n.chain, turn * 5, n.rstd[:], n.ready)

            def program(guarded):
                def phase1(s):
                    a = s.a

                    def cap_k(t):
                        pool.wait_ge(a_ek_s, a * (NT - 1) + t + 1)
                        pool.sem_inc(pool_gate)
                        pool.tensor_scalar(a_ek[:, t % 2, :], a_ek[:, t % 2, :], 1.0, 0.0, ALU.min, ALU.max).then_inc(a_mk, 1)

                    def cap_q(m):
                        pool.wait_ge(a_eq_s, a * 4 + m + 1)
                        pool.sem_inc(pool_gate)
                        pool.tensor_scalar(a_eq[:, m % 2, :], a_eq[:, m % 2, :], 1.0, 0.0, ALU.min, ALU.max).then_inc(a_mq, 1)

                    if a is not None:
                        for t in range(NT - 1):
                            cap_k(t)
                        for m in range(4):
                            cap_q(m)
                    if s.b is not None:
                        norm_rstd(at, second_turn(s.b))
                    if a is not None:
                        norm_rstd(ff, first_turn(a))

                def phase2(s):
                    b = s.b

                    def rstd(t):
                        j = b * NT + t
                        pool.wait_ge(b_ss_s, j + 1)
                        pool.sem_inc(pool_gate)
                        pool.tensor_scalar(b_tmp[:, 0, :], b_ss[:], 1.0 / HD, RMS_EPS, ALU.mult, ALU.add).then_inc(b_ch, 1)
                        if needed(j):
                            pool.wait_ge(b_qn_s, j)
                        root(b_tmp, mhalf[:], b_ch, j * 6, b_rs[:], b_ch)
                        pool.wait_ge(b_ch, j * 6 + 6)
                        pool.tensor_tensor(b_rs[:], b_rs[:], gains[:], ALU.mult).then_inc(b_rs_s, 1)

                    def rotate(t):
                        j = b * NT + t
                        qn = b_qn[:, t % 2]
                        table = lambda name, lo, hi: C[name].rearrange("p (t d) -> p t d", t=NT)[:, t, lo:hi].unsqueeze(1) \
                            .broadcast_to([P, H + KVH, hi - lo])
                        pool.wait_ge(b_qn_s, j + 1)
                        if needed(j):
                            pool.wait_ge(b_qr_s, j)
                        pool.tensor_tensor(b_rc[:], qn, table("cos", 0, HD), ALU.mult)
                        pool.tensor_tensor(b_rsn[:, :, 0:HD // 2], qn[:, :, HD // 2:], table("sin", 0, HD // 2), ALU.mult)
                        pool.tensor_tensor(b_rsn[:, :, HD // 2:], qn[:, :, 0:HD // 2], table("sin", HD // 2, HD),
                                           ALU.mult).then_inc(b_ro, 1)
                        pool.wait_ge(b_ro, j + 1)
                        if needed(j - 1):
                            pool.wait_ge(b_lo, j - 1)
                        pool.tensor_tensor(b_qr[:, t % 2], b_rc[:], b_rsn[:], ALU.add).then_inc(b_qr_s, 1)

                    if b is not None:
                        for t in range(NT):
                            rstd(t)
                            if t:
                                rotate(t - 1)
                        rotate(NT - 1)
                    if s.next_a is not None:
                        norm_rstd(at, first_turn(s.next_a))
                    if b is not None:
                        norm_rstd(ff, second_turn(b))

                norm_rstd(at, 0)
                steps(pool, phase1, phase2)

            both_ways(pool, program)



def arrays_of(x, W_qkv, W_out, Wq, Wk, Wv, Wo, q_gain, pair_mix, W1, b1, W2, b2):
    wq = Wq.T.reshape(D, 2, 2, REP, HD).transpose(0, 1, 3, 2, 4).reshape(D, D)
    return {
        "x": x,
        "w_qkv": W_qkv,
        "w_out": W_out,
        "w_b": np.concatenate([wq, Wk.T, Wv.T], 1),
        "wo_b": Wo.T.reshape(H // 2, 2, HD, D).transpose(1, 0, 2, 3).reshape(2, P, D),
        "gain": q_gain.reshape(2, 2, REP).transpose(0, 2, 1).reshape(H),
        "mix": np.repeat(pair_mix.reshape(H // 2, 4), HD, axis=0),
        "w1": W1.T,
        "b1": b1.reshape(FB, P).T,
        "w2": W2.T,
        "b2": b2.reshape(1, D),
        "const": constants(),
    }


def kernel(**inputs):
    import concourse.bacc as bacc
    from concourse.bass_utils import run_bass_kernel_spmd

    g = {k: np.asarray(v) for k, v in inputs.items()}
    laid = arrays_of(g["L0_attn_a_x"], g["L0_attn_a_W_qkv"], g["L0_attn_a_W_out"], g["L0_attn_b_Wq"], g["L0_attn_b_Wk"],
                     g["L0_attn_b_Wv"], g["L0_attn_b_Wo"], g["L0_attn_b_q_gain"], g["L0_attn_b_pair_mix"],
                     g["L0_ffn_W1"], g["L0_ffn_b1"], g["L0_ffn_W2"], g["L0_ffn_b2"])
    nc = bacc.Bacc("TRN2", target_bir_lowering=False, num_devices=1)
    arrays = {f"in_{n}": np.ascontiguousarray(a) for n, a in laid.items()}
    aps = [nc.dram_tensor(n, a.shape, F32, kind="ExternalInput").ap() for n, a in arrays.items()]
    out = nc.dram_tensor("out", (NSEQ, S, D), F32, kind="ExternalOutput").ap()
    build(nc, *aps, out)
    r = run_bass_kernel_spmd(nc, [arrays], core_ids=[0])
    return r.results[0]["out"]
```

```python
from contextlib import ExitStack

import numpy as np

import concourse.bass as bass
from concourse import mybir

ALU = mybir.AluOpType
ACT = mybir.ActivationFunctionType
X = mybir.AxisListType.X
F32 = mybir.dt.float32
F32R = mybir.dt.float32r
BF16 = mybir.dt.bfloat16

P = 128
NSEQ, S, D = 32, 512, 256
NT = S // P
KB = D // P
H, HD = 16, 16
HB = H // KB
HV = HD + 1
FF = 4 * D
FB = FF // P
KVH = 4
REP = H // KVH
W = 64
NBL = S // W
QK = (H + KVH) * HD
NB = QK + KVH * HD
SLOT = 4 * HD
LN_EPS, A_EPS, RMS_EPS, Q_EPS = 1e-5, 1e-6, 1e-6, 1e-5
MASKED = -1e30
ROOT_GUESS = 0x5F3759DF
SAFE_SCORE = 40.0

_WIDTHS = dict(ident=P, causal=P, heads=HB * HV, parity=2, kodd=W, keven=W, qodd=P, qeven=P,
               cos=NT * HD, sin=NT * HD)
COL, _at = {}, 0
for _name, _w in _WIDTHS.items():
    COL[_name] = (_at, _at + _w)
    _at += _w
NCONST = _at


def constants():
    c = np.zeros((P, NCONST), np.float32)

    def put(name, value):
        c[:, COL[name][0]:COL[name][1]] = np.asarray(value, np.float32).reshape(P, -1)

    p, q = np.arange(P)[:, None], np.arange(P)[None, :]
    put("ident", p == q)
    put("causal", p <= q)
    head = np.repeat(np.arange(HB), HV)[None, :]
    put("heads", p // HD == head)
    put("parity", (p // HD) % 2 == np.arange(2)[None, :])
    k, qq = np.arange(P)[:, None], np.arange(W)[None, :]
    odd = np.where(k < W, qq < k, k - W <= qq)
    even = np.where(k < W, k <= qq, qq < k - W)
    put("kodd", np.where(odd, 0.0, MASKED))
    put("keven", np.where(even, 0.0, MASKED))
    put("qodd", np.where(np.tile(odd.T, (2, 1)), 0.0, MASKED))
    put("qeven", np.where(np.tile(even.T, (2, 1)), 0.0, MASKED))
    inv = (1.0 / np.float32(10000.0) ** (np.arange(0, HD, 2, dtype=np.float32) / HD)).astype(np.float32)
    ang = np.outer(np.arange(S, dtype=np.float32), inv)
    cos, sin = np.cos(ang).astype(np.float32), np.sin(ang).astype(np.float32)
    table = lambda a, b: np.concatenate([a, b], 1).reshape(NT, P, HD).transpose(1, 0, 2)
    put("cos", table(cos, cos))
    put("sin", table(sin, -sin))
    return c


def needed(value):
    return not isinstance(value, int) or value > 0


def build(nc, x, w_qkv, w_out, w_b, wo_b, gain, mix, w1, b1, w2, b2, const, out):
    with ExitStack() as ctx:
        def sb(name, shape, dt=F32):
            return ctx.enter_context(nc.sbuf_tensor(name, shape, dt))

        def sem(name):
            return ctx.enter_context(nc.semaphore(name))

        cst = sb("cst", [P, NCONST])
        C = {n: cst[:, a:b] for n, (a, b) in COL.items()}
        ident, causal = C["ident"], C["causal"]
        ident_b = sb("ident_b", [P, P], BF16)
        neg_ident = sb("neg_ident", [P, P], F32R)
        ident_r = sb("ident_r", [P, P], F32R)
        kmask = sb("kmask", [P, 2, W], BF16)
        qmask = sb("qmask", [P, 2, P], BF16)
        wqkv_h, wqkv_l = (sb(f"wqkv_{n}", [P, KB, 3 * D], F32R) for n in "hl")
        wout_h, wout_l = (sb(f"wout_{n}", [P, KB, D], F32R) for n in "hl")
        wb_h, wb_l = (sb(f"wb_{n}", [P, KB, NB], F32R) for n in "hl")
        wob_h, wob_l = (sb(f"wob_{n}", [P, 2, D], F32R) for n in "hl")
        w1t = sb("w1t", [P, KB, FF], F32R)
        w2t = sb("w2t", [P, FB, D], F32R)
        b1c = sb("b1c", [P, FB])
        b2f = sb("b2f", [1, D])
        b2_h, b2_l = sb("b2_h", [1, D], F32R), sb("b2_l", [1, D], F32R)
        ones_f = sb("ones_f", [P, P])
        ones_r = sb("ones_r", [1, P], F32R)
        gains = sb("gains", [P, H + KVH])
        mixc = sb("mixc", [P, 4])
        mhalf = sb("mhalf", [P, NT])
        gsum = sb("gsum", [P, 2])
        thr = sb("thr", [P, 4])
        wide_f, wide_i = sb("wide_f", [P, 2]), sb("wide_i", [P, 1], mybir.dt.int32)

        x0, x1, x2, x3 = (sb(f"x{n}", [P, NT, D]) for n in range(4))

        class Norm:
            def __init__(self, n):
                self.st = sb(n + "st", [P, NT, 6])
                self.mv = sb(n + "mv", [P, NT, 2])
                self.tmp = sb(n + "tmp", [P, 3, NT])
                self.rstd = sb(n + "rstd", [P, NT])
                self.xn = sb(n + "xn", [P, NT, D])
                self.xh = sb(n + "xh", [P, KB, S], F32R)
                self.xl = sb(n + "xl", [P, KB, S], F32R)
                self.bn = sem(n + "bn_stats_done")
                self.stats = sem(n + "mean_var_ready")
                self.chain = sem(n + "rstd_steps")
                self.ready = sem(n + "rstd_ready")
                self.normed = sem(n + "normed")
                self.turned = sem(n + "transposed")
                self.hi = sem(n + "hi_ready")
                self.lo = sem(n + "lo_ready")

        at, ff = Norm("at_"), Norm("ff_")

        f_r = sb("f_r", [P, 2, S])
        f_hh = sb("f_hh", [P, 2, S], F32R)
        f_hl = sb("f_hl", [P, 2, S], F32R)

        a_ek = sb("a_ek", [P, 2, D])
        a_eq = sb("a_eq", [P, 2, S])
        a_kt = sb("a_kt", [P, NT - 1, D])
        a_v = sb("a_v", [P, NT, H, HV])
        a_relu = sb("a_relu", [P, 2, S])
        a_qT = sb("a_qT", [P, KB, S])
        a_kT = sb("a_kT", [P, KB, S])
        a_qz = sb("a_qz", [P, KB, 2, S])
        a_s = sb("a_s", [P, 2, 4, S])
        a_state = sb("a_state", [P, 2, KB * HB * HV])
        a_den = sb("a_den", [P, 2, H])
        a_y = sb("a_y", [P, D])
        a_yh, a_yl = sb("a_yh", [P, KB, P], F32R), sb("a_yl", [P, KB, P], F32R)

        b_ss = sb("b_ss", [P, NT, H + KVH])
        b_var = sb("b_var", [P, NT, H + KVH])
        b_half = sb("b_half", [P, NT, H + KVH])
        b_root = sb("b_root", [P, NT, H + KVH])
        b_step = sb("b_step", [P, NT, H + KVH])
        b_rs = sb("b_rs", [P, NT, H + KVH])
        b_sq = a_eq[:, :, 0:QK]
        b_qn, b_rsn, b_qr = (a_s[:, 0].rearrange("p a n -> p (a n)")[:, n * 2 * QK:(n + 1) * 2 * QK].rearrange(
            "p (u h d) -> p u h d", u=2, h=H + KVH) for n in range(3))
        b_p = a_qz
        b_qs = sb("b_qs", [P, 2, H, 4, HD], F32R)
        b_ks = sb("b_ks", [P, 2, KVH, 4, HD], F32R)
        b_qT = sb("b_qT", [P, 2, NBL, REP * W], F32R)
        b_kT = sb("b_kT", [P, 2, S], F32R)
        b_kTm = sb("b_kTm", [P, 2, NT, P], F32R)
        b_v = sb("b_v", [P, NT, KVH, HV])
        b_vm = sb("b_vm", [P, NT, KVH, HV])
        b_m = sb("b_m", [P, 2, 2 * 4], F32R)
        b_den = sb("b_den", [P, 2, 2 * KVH])
        b_y = sb("b_y", [P, 2, P])
        b_yh, b_yl = sb("b_yh", [P, 2, P], F32R), sb("b_yl", [P, 2, P], F32R)

        Q = [ctx.enter_context(nc.psum_tensor(f"Q{n}", [P, S], F32)) for n in range(4)]
        HID = [ctx.enter_context(nc.psum_tensor(f"HID{n}", [P, S], F32)) for n in range(2)]
        Y = [ctx.enter_context(nc.psum_tensor(f"Y{n}", [P, S], F32)) for n in range(2)]

        st_a = a_s[:, 0].rearrange("p a n -> p (a n)")
        st_w1 = a_s[:, 1].rearrange("p a n -> p (a n)")
        st_w2 = a_qz[:, :].rearrange("p a b n -> p (a b n)")
        st_wb = a_qT[:, :].rearrange("p k n -> p (k n)")[:, 0:KB * NB]
        st_wo = x3[:, 2:4, :]

        loaded, setup, setup_pe, prepared, ones_set = (sem(n) for n in (
            "weights_loaded", "setup_steps", "abs_sum_ready", "weights_prepared", "constants_set"))
        pool_gate, dve_gate = sem("pool_gate"), sem("dve_gate")
        x_in, stored = sem("x_loaded"), sem("x_stored")
        f_h, f_rr, f_act, f_lo, f_w2, f_out = (sem(n) for n in (
            "f_hidden_ready", "f_relu_ready", "f_hi_ready", "f_lo_ready", "f_down_done", "f_added"))
        (a_kv, a_ek_s, a_v_s, a_rk_s, a_kt_s, a_qk, a_eq_s, a_rq_s, a_ph, a_qz_s, a_sc, a_sm, a_u, a_st, a_o, a_dn,
         a_yn, a_t, a_h, a_l, a_p, a_out) = (sem("a_" + n) for n in (
             "kv_projected", "k_exp", "v_ready", "k_relu", "k_ready", "qk_projected", "q_exp", "q_relu",
             "phi_ready", "q_split_by_parity", "scores", "scores_masked", "state_summed", "state_ready", "numerators",
             "denominator_steps", "normalised", "y_transposed", "y_hi", "y_lo", "projected", "added"))
        (b_qkv, b_sq_s, b_v_s, b_ss_s, b_ch, b_rs_s, b_vm_s, b_qn_s, b_ro, b_rc_s, b_qr_s, b_hi, b_lo, b_t, b_te, b_km, b_mm,
         b_mx, b_s, b_ex, b_o, b_dn, b_yn, b_t2, b_h2, b_l2, b_pp, b_out) = (sem("b_" + n) for n in (
             "projected", "squares", "v_ready", "sums_of_squares", "rstd_steps", "rstd_ready", "even_v_ready",
             "qk_normed", "sine_products", "cosine_products", "rotated", "stack_hi", "stack_lo", "qk_transposed", "qk_evacuated", "even_keys_ready",
             "scores_for_max", "max_ready", "scores", "exp_ready", "numerators", "denominators", "normalised",
             "y_transposed", "y_hi", "y_lo", "out_projected", "added"))

        QKV_BANK = (2, 3, 0, 1)
        TURN_BANK = (2, 3, 0, 1)

        def table(name, t, lo, hi):
            return C[name].rearrange("p (t d) -> p t d", t=NT)[:, t, lo:hi].unsqueeze(1).broadcast_to([P, H + KVH, hi - lo])

        block = ctx.enter_context(nc.Block())
        N_LOADS = 11
        N_PREPARED = 24

        class Step:
            def __init__(self, i):
                def there(j):
                    return j if not isinstance(j, int) or 0 <= j < NSEQ else None
                self.a, self.b, self.c, self.next_a = there(i), there(i - 1), there(i - 2), there(i + 1)
                self.last = isinstance(i, int) and i == NSEQ + 1

        def first_turn(s):
            return None if s is None else 0 if isinstance(s, int) and s == 0 else s * 2 - 1

        def second_turn(s):
            return None if s is None else 2 * NSEQ - 1 if isinstance(s, int) and s == NSEQ - 1 else s * 2 + 2

        def steps(engine, phase1, phase2):
            for i in (0, 1):
                phase1(Step(i))
                phase2(Step(i))
            with engine.Fori(2, NSEQ - 1) as i:
                phase1(Step(i))
                phase2(Step(i))
            for i in (NSEQ - 1, NSEQ):
                phase1(Step(i))
                phase2(Step(i))
            phase1(Step(NSEQ + 1))

        def both_ways(engine, program):
            engine.wait_ge(prepared, N_PREPARED)
            wide = engine.value_load(wide_i[0:1, 0:1], min_val=0, max_val=1)
            with engine.If(wide):
                program(True)
            with engine.Else():
                program(False)

        @block.sync
        def _(sp):
            sp.dma_start(st_a[:, 0:KB * 3 * D].rearrange("p (k n) -> p k n", k=KB),
                         w_qkv.rearrange("(k p) n -> p k n", p=P)).then_inc(loaded, 16)
            sp.dma_start(st_a[:, KB * 3 * D:KB * 4 * D].rearrange("p (k n) -> p k n", k=KB),
                         w_out.rearrange("(k p) n -> p k n", p=P)).then_inc(loaded, 16)
            sp.dma_start(cst[:], const).then_inc(loaded, 16)
            sp.dma_start(st_wb.rearrange("p (k n) -> p k n", k=KB),
                         w_b.rearrange("(k p) n -> p k n", p=P)).then_inc(loaded, 16)
            sp.dma_start(st_wo, wo_b.rearrange("o p n -> p o n")).then_inc(loaded, 16)
            sp.dma_start(st_w1.rearrange("p (k n) -> p k n", k=KB),
                         w1.rearrange("(k p) n -> p k n", p=P)).then_inc(loaded, 16)
            sp.dma_start(st_w2.rearrange("p (k n) -> p k n", k=FB),
                         w2.rearrange("(k p) n -> p k n", p=P)).then_inc(loaded, 16)
            sp.dma_start(b1c[:], b1).then_inc(loaded, 16)
            sp.dma_start(b2f[:], b2).then_inc(loaded, 16)
            sp.dma_start(gains[:, 0:H], gain.partition_broadcast(P)).then_inc(loaded, 16)
            sp.dma_start(mixc[:], mix).then_inc(loaded, 16)

            def load(a):
                if needed(a * NT):
                    sp.wait_ge(a_out, a * NT)
                src = x[a] if isinstance(a, int) else x[bass.ds(a, 1)].rearrange("o s d -> (o s) d")
                sp.dma_start(x0[:], src.rearrange("(t p) d -> p t d", p=P)).then_inc(x_in, 16)

            def store(c):
                sp.wait_ge(f_out, (second_turn(c) + 1) * 2)
                dst = out[c] if isinstance(c, int) else out[bass.ds(c, 1)].rearrange("o s d -> (o s) d")
                sp.dma_start(dst.rearrange("(t p) d -> p t d", p=P), x3[:]).then_inc(stored, 16)

            def phase1(s):
                if s.last:
                    store(s.c)

            def phase2(s):
                if s.c is not None:
                    store(s.c)
                if s.next_a is not None:
                    load(s.next_a)

            load(0)
            steps(sp, phase1, phase2)
            sp.wait_ge(stored, 16 * NSEQ)

        @block.tensor
        def _(pe):
            pe.wait_ge(ones_set, 5)
            pe.wait_ge(setup, 2)
            pe.matmul(Q[0][:, 0:2], ones_f[:], gsum[:], start=True, stop=True).then_inc(setup_pe, 1)
            def three(dst, lhs, rhs, n, start=True, last=True):
                mm = None
                for k in range(n):
                    (lh, ll), (rh, rl) = lhs(k), rhs(k)
                    for j, (a, b) in enumerate(((lh, rh), (lh, rl), (ll, rh))):
                        mm = pe.matmul(dst, a, b, start=(start and k == 0 and j == 0), stop=(last and k == n - 1 and j == 2))
                return mm

            def norm_transpose(n, turn, banks):
                for hf in range(2):
                    pe.wait_ge(n.normed, turn * NT + 2 * hf + 2)
                    for k in range(KB):
                        for t in range(2):
                            mm = pe.transpose(banks[hf][:, k * D + t * P:k * D + (t + 1) * P],
                                              n.xn[:, 2 * hf + t, k * P:(k + 1) * P], ident)
                    mm.then_inc(n.turned, 1)

            def f_norm(turn):
                if needed(turn * FB):
                    pe.wait_ge(f_act, turn * FB)
                norm_transpose(ff, turn, HID)

            def f_up(turn, fb, blocks=range(KB)):
                if turn is None:
                    return
                if fb == 0:
                    pe.wait_ge(ff.lo, turn * 2 + 2)
                if fb >= 2:
                    pe.wait_ge(f_act, turn * FB + fb - 1)
                for k in blocks:
                    for j, src in enumerate((ff.xh, ff.xl)):
                        mm = pe.matmul(HID[fb % 2][:], w1t[:, k, fb * P:(fb + 1) * P], src[:, k, :],
                                       start=(k == 0 and j == 0), stop=(k == KB - 1 and j == 1))
                if KB - 1 in blocks:
                    mm.then_inc(f_h, 1)

            def f_down(turn, fb, tiles=range(NT)):
                if turn is None:
                    return
                pe.wait_ge(f_lo, turn * FB + fb + 1)
                if fb == 0:
                    if needed(turn * 2):
                        pe.wait_ge(f_out, turn * 2)
                    for t in range(NT):
                        for j, b in enumerate((b2_h, b2_l)):
                            pe.matmul(Y[t // 2][:, (t % 2) * D:(t % 2 + 1) * D], ones_r[:], b[:],
                                      start=(t % 2 == 0 and j == 0), stop=False, skip_group_check=True)
                for t in tiles:
                    for j, h in enumerate((f_hh, f_hl)):
                        mm = pe.matmul(Y[t // 2][:, (t % 2) * D:(t % 2 + 1) * D], h[:, fb % 2, t * P:(t + 1) * P],
                                       w2t[:, fb, :], start=False, stop=(fb == FB - 1 and j == 1), skip_group_check=True)
                if NT - 1 in tiles:
                    mm.then_inc(f_w2, 1)

            def f_unit(turn, k):
                if turn is not None:
                    if k + 1 < FB:
                        f_up(turn, k + 1)
                    if k >= 0:
                        f_down(turn, k)

            def carried(turn, k):
                f_unit(turn, FB - 2 + k)

            def alone(own, carry, last):
                carried(carry, 0)
                carried(carry, 1)
                if own is not None:
                    f_norm(own)
                    for k in range(-1, FB if last else FB - 2):
                        f_unit(own, k)

            def norm_for_b(s):
                if s.a is not None:
                    pe.wait_ge(a_sm, (s.a + 1) * 16)
                elif s.b > 0:
                    pe.wait_ge(b_ex, s.b * 2 * NBL)
                norm_transpose(at, second_turn(s.b), Q)

            def norm_for_a(s):
                if s.b is not None:
                    pe.wait_ge(b_ex, (s.b + 1) * 2 * NBL)
                else:
                    pe.wait_ge(a_sm, (s.a + 1) * 16)
                norm_transpose(at, first_turn(s.next_a), Q)

            def program(guarded):
                def phase1(s):
                    a, n, own, carry = s.a, first_turn(s.a), second_turn(s.c), first_turn(s.b)
                    b_done = a - 1 if s.b is not None and a is not None else 0

                    def unit(k):
                        f_unit(own, k)

                    def kv(t):
                        pe.wait_ge(at.lo, n * 2 + t // 2 + 1)
                        if t < 2 and needed(b_done * NT):
                            pe.wait_ge(b_out, b_done * NT)
                            pe.wait_ge(b_yn, b_done * NBL)
                        if t >= 2:
                            pe.wait_ge(a_v_s, a * NT + t - 1)
                        lo, width = (D, 2 * D) if t < NT - 1 else (2 * D, D)
                        three(Q[2 + t % 2][:, 0:width],
                              lambda k: (at.xh[:, k, t * P:(t + 1) * P], at.xl[:, k, t * P:(t + 1) * P]),
                              lambda k: (wqkv_h[:, k, lo:lo + width], wqkv_l[:, k, lo:lo + width]), KB).then_inc(a_kv, 1)

                    def qk(m):
                        if m == 0:
                            pe.wait_ge(at.lo, n * 2 + 2)
                        if m >= 2:
                            pe.wait_ge(a_rq_s, a * 4 + m - 1)
                        three(Q[m % 2][:], lambda k: (wqkv_h[:, k, m * P:(m + 1) * P], wqkv_l[:, k, m * P:(m + 1) * P]),
                              lambda k: (at.xh[:, k, :], at.xl[:, k, :]), KB).then_inc(a_qk, 1)

                    def scores(ch, r):
                        if ch == 0 and r == 0:
                            pe.wait_ge(a_qz_s, (a + 1) * 4)
                            pe.wait_ge(a_ph, (a + 1) * 4)
                        if 4 * ch + r >= 2:
                            pe.wait_ge(a_sm, a * 16 + 4 * ch + r - 1)
                        rows = slice(32 * r, 32 * r + 32)
                        for k in range(KB):
                            mm = pe.matmul(Q[r % 2][:, k * 2 * P:(k + 1) * 2 * P].rearrange("p (e q) -> p e q", e=2),
                                           a_kT[rows, k, ch * P:(ch + 1) * P], a_qz[rows, k, :, ch * P:(ch + 1) * P],
                                           start=(k == 0), stop=(k == KB - 1), skip_group_check=True)
                        mm.then_inc(a_sc, 1)

                    def state(ch):
                        pe.wait_ge(a_v_s, a * NT + (NT if ch == 0 else ch + 1))
                        pe.wait_ge(a_kt_s, a * (NT - 1) + ch + 1)
                        if ch:
                            pe.wait_ge(a_st, a * 3 + ch)
                        for k in range(KB):
                            mm = pe.matmul(Q[3][:, k * HB * HV:(k + 1) * HB * HV].rearrange("p (h j) -> p h j", h=HB),
                                           a_kt[:, ch, k * P:(k + 1) * P], a_v[:, ch, k * HB:(k + 1) * HB, :],
                                           start=(ch == 0 and k == 0), stop=True, skip_group_check=True)
                        mm.then_inc(a_u, 1)

                    def numer(ch, r):
                        if r == 0:
                            pe.wait_ge(a_v_s, a * NT + ch + 1)
                            if ch:
                                pe.wait_ge(a_st, a * 3 + ch)
                                pe.wait_ge(a_out, a * NT + ch)
                                for k in range(KB):
                                    pe.matmul(Q[2][:, k * HB * HV:(k + 1) * HB * HV], a_qT[:, k, ch * P:(ch + 1) * P],
                                              a_state[:, (ch - 1) % 2, k * HB * HV:(k + 1) * HB * HV],
                                              start=(k == 0), stop=False, skip_group_check=True)
                            else:
                                pe.wait_ge(a_kt_s, (a + 1) * (NT - 1))
                        pe.wait_ge(a_sm, a * 16 + 4 * ch + r + 1)
                        for j in range(4):
                            k, e = divmod(j, 2)
                            h = k * HB + 2 * r + e
                            mm = pe.matmul(Q[2][:, h * HV:(h + 1) * HV], a_s[:, ch % 2, r, j * P:(j + 1) * P],
                                           a_v[:, ch, h, :], start=(ch == 0 and r == 0 and j == 0), stop=True,
                                           skip_group_check=True)
                        if r == 3:
                            mm.then_inc(a_o, 1)

                    def turn_y(ch):
                        pe.wait_ge(a_yn, a * NT + ch + 1)
                        for k in range(KB):
                            mm = pe.transpose(Q[2][:, k * P:(k + 1) * P], a_y[:, k * P:(k + 1) * P], ident)
                        mm.then_inc(a_t, 1)

                    def project(ch):
                        pe.wait_ge(a_l, a * NT + ch + 1)
                        three(Q[2][:, 0:D], lambda k: (a_yh[:, k, :], a_yl[:, k, :]),
                              lambda k: (wout_h[:, k, :], wout_l[:, k, :]), KB).then_inc(a_p, 1)

                    if a is None:
                        alone(own, carry, s.last)
                        if s.b is not None:
                            norm_for_b(s)
                        return
                    kv(0)
                    kv(1)
                    carried(carry, 0)
                    kv(2)
                    if own is not None:
                        f_norm(own)
                    kv(3)
                    carried(carry, 1)
                    qk(0)
                    qk(1)
                    unit(-1)
                    qk(2)
                    qk(3)
                    unit(0)
                    for r in range(4):
                        scores(0, r)
                    state(0)
                    unit(1)
                    for ch in range(NT):
                        for r in range(4):
                            if ch + 1 < NT:
                                scores(ch + 1, r)
                            elif r == 2 and s.b is not None:
                                norm_for_b(s)
                            numer(ch, r)
                        if own is not None:
                            f_up(own, 3 + ch)
                        turn_y(ch)
                        if own is not None:
                            f_down(own, 2 + ch)
                        project(ch)
                        if ch + 1 < NT - 1:
                            state(ch + 1)

                def phase2(s):
                    b, n, own, carry = s.b, second_turn(s.b), first_turn(s.a), second_turn(s.c)
                    a_done = NSEQ if s.a is None else s.a + 1

                    def unit(k):
                        f_unit(own, k)

                    def qkv(t):
                        pe.wait_ge(at.lo, n * 2 + t // 2 + 1)
                        if t == 0:
                            pe.wait_ge(a_out, a_done * NT)
                            pe.wait_ge(a_st, a_done * 3)
                        if t == 2:
                            pe.wait_ge(at.lo, n * 2 + 2)
                        three(Q[QKV_BANK[t]][:, 0:NB],
                              lambda k: (at.xh[:, k, t * P:(t + 1) * P], at.xl[:, k, t * P:(t + 1) * P]),
                              lambda k: (wb_h[:, k, :], wb_l[:, k, :]), KB).then_inc(b_qkv, 1)

                    def turn_qk(t):
                        pe.wait_ge(b_lo, b * NT + t + 1)
                        for j in range(3):
                            turn = 3 * t + j
                            if turn < 4:
                                pe.wait_ge(b_qn_s, b * NT + turn + 1)
                            else:
                                pe.wait_ge(b_te, b * 12 + turn - 3)
                            src = b_ks[:, t % 2] if j == 2 else b_qs[:, t % 2, 8 * j:8 * j + 8]
                            src = src.rearrange("p h s d -> p (h s d)")
                            for r in range(2 if j == 2 else REP):
                                mm = pe.transpose(Q[TURN_BANK[turn % 4]][:, r * P:(r + 1) * P].bitcast(F32R),
                                                  src[:, r * P:(r + 1) * P], ident_r[:])
                            mm.then_inc(b_t, 1)

                    def keys(bl, g2, gp):
                        rows = slice(64 * g2, 64 * g2 + 64)
                        if bl % 2:
                            return b_kT[rows, gp, (bl - 1) * W:(bl + 1) * W]
                        return b_kTm[rows, gp, bl // 2, 0:(P if bl else W)]

                    def for_max(bl, g2, nk):
                        dst = Q[g2][:, 0:4 * nk].rearrange("p (u k) -> p u k", u=4)
                        pe.matmul(dst, ident_b[:], qmask[:, 1 - bl % 2, 0:nk].unsqueeze(1).broadcast_to([P, 4, nk]),
                                  start=True, stop=False, skip_group_check=True)
                        for gp in range(2):
                            for rp in range(2):
                                mm = pe.matmul(dst[:, 2 * gp + rp, :],
                                               b_qT[64 * g2:64 * g2 + 64, gp, bl, rp * P:(rp + 1) * P],
                                               keys(bl, g2, gp), start=False, stop=True, skip_group_check=True)
                        mm.then_inc(b_mm, 1)

                    def scores(bl, g2):
                        if bl < NBL:
                            nk = W if bl == 0 else P
                            j = b * NBL + bl
                            if bl == 0 and g2 == 0:
                                pe.wait_ge(b_te, (b + 1) * 12)
                                pe.wait_ge(b_km, (b + 1) * 7)
                            if bl:
                                pe.wait_ge(b_ex, j * 2 - 1 + g2)
                            if guarded:
                                for_max(bl, g2, nk)
                                pe.wait_ge(b_mx, j * 2 + g2 + 1)
                            dst = Q[g2][0:nk, :]
                            pe.matmul(dst.rearrange("p (u q) -> p u q", u=8), ident_b[:, 0:nk],
                                      kmask[:, 1 - bl % 2, :].unsqueeze(1).broadcast_to([P, 8, W]),
                                      start=True, stop=False, skip_group_check=True)
                            for gp in range(2):
                                mm = pe.matmul(dst[:, gp * REP * W:(gp + 1) * REP * W], keys(bl, g2, gp),
                                               b_qT[64 * g2:64 * g2 + 64, gp, bl, :],
                                               start=False, stop=not guarded, skip_group_check=True)
                            if guarded:
                                for u in range(4):
                                    mm = pe.matmul(dst[:, u * P:(u + 1) * P],
                                                   b_m[:, bl % 2, 4 * g2 + u:4 * g2 + u + 1].broadcast_to([P, nk]),
                                                   neg_ident[:], start=False, stop=True, skip_group_check=True)
                            mm.then_inc(b_s, 1)

                    def numer(bl, g2):
                        nk = W if bl == 0 else P
                        if g2 == 0:
                            if bl == 0:
                                pe.wait_ge(b_vm_s, (b + 1) * 7)
                            elif bl % 2:
                                if bl > 1:
                                    pe.wait_ge(b_yn, b * NBL + bl - 1)
                            else:
                                pe.wait_ge(b_out, b * NT + bl // 2)
                        pe.wait_ge(b_ex, (b * NBL + bl) * 2 + g2 + 1)
                        v = (b_v[:, (bl - 1) // 2] if bl % 2 else b_vm[:, bl // 2])
                        for gp in range(2):
                            g = 2 * gp + g2
                            for rp in range(2):
                                u = 2 * g + rp
                                mm = pe.matmul(Q[2 + bl % 2][:, u * HV:(u + 1) * HV],
                                               b_p[0:nk, bl % 2, g2, gp * 256 + rp * P:gp * 256 + (rp + 1) * P],
                                               v[0:nk, g, :], start=(g == 0 and rp == 0), stop=True, skip_group_check=True)
                        if g2:
                            mm.then_inc(b_o, 1)

                    def turn_y(t):
                        pe.wait_ge(b_yn, b * NBL + 2 * t + 2)
                        for e in range(2):
                            mm = pe.transpose(Q[2][:, e * P:(e + 1) * P], b_y[:, e, :], ident)
                        mm.then_inc(b_t2, 1)

                    def project(t):
                        pe.wait_ge(b_l2, b * NT + t + 1)
                        three(Q[2][:, 0:D], lambda k: (b_yh[:, k, :], b_yl[:, k, :]),
                              lambda k: (wob_h[:, k, :], wob_l[:, k, :]), 2).then_inc(b_pp, 1)

                    if b is None:
                        alone(own, carry, False)
                        norm_for_a(s)
                        return
                    qkv(0)
                    qkv(1)
                    qkv(2)
                    qkv(3)
                    carried(carry, 0)
                    if own is not None:
                        f_norm(own)
                    carried(carry, 1)
                    unit(-1)
                    turn_qk(0)
                    unit(0)
                    turn_qk(1)
                    turn_qk(2)
                    unit(1)
                    turn_qk(3)
                    scores(0, 0)
                    scores(0, 1)
                    for t in range(NT):
                        for bl in (2 * t, 2 * t + 1):
                            for g2 in range(2):
                                scores(bl + 1, g2)
                                numer(bl, g2)
                        if t == NT - 1 and s.next_a is not None:
                            norm_for_a(s)
                        if own is not None:
                            f_up(own, 3 + t)
                        turn_y(t)
                        if own is not None:
                            f_down(own, 2 + t)
                        project(t)

                norm_transpose(at, 0, Q)
                steps(pe, phase1, phase2)

            both_ways(pe, program)


        @block.scalar
        def _(act):
            def norm_hi(n, turn, banks):
                for hf in range(2):
                    act.wait_ge(n.turned, turn * 2 + hf + 1)
                    act.activation(n.xh[:, :, hf * D:(hf + 1) * D],
                                   banks[hf][:, :].rearrange("p (k n) -> p k n", k=KB), ACT.Copy).then_inc(n.hi, 1)

            def f_norm(turn):
                if needed(turn * FB):
                    act.wait_ge(f_h, turn * FB)
                norm_hi(ff, turn, HID)

            def f_relu(turn, fb):
                act.wait_ge(f_h, turn * FB + fb + 1)
                if needed(turn * FB + fb - 1):
                    act.wait_ge(f_lo, turn * FB + fb - 1)
                    act.wait_ge(f_w2, turn * FB + fb - 1)
                act.activation(f_r[:, fb % 2, :], HID[fb % 2][:], ACT.Relu, bias=b1c[:, fb:fb + 1]).then_inc(f_rr, 1)
                act.activation(f_hh[:, fb % 2, :], HID[fb % 2][:], ACT.Relu, bias=b1c[:, fb:fb + 1]).then_inc(f_act, 1)

            def alone(own, carry, last):
                if carry is not None:
                    f_relu(carry, FB - 1)
                if own is not None:
                    f_norm(own)
                    for k in range(FB if last else FB - 1):
                        f_relu(own, k)

            def norm_for_b(s):
                done = (NSEQ if s.a is None else s.a + 1) * 4
                act.wait_ge(a_qk, done)
                act.wait_ge(a_kv, done)
                norm_hi(at, second_turn(s.b), Q)

            def norm_for_a(s):
                if s.b is not None:
                    act.wait_ge(b_qkv, (s.b + 1) * NT)
                else:
                    act.wait_ge(a_qk, (s.a + 1) * 4)
                    act.wait_ge(a_kv, (s.a + 1) * NT)
                norm_hi(at, first_turn(s.next_a), Q)

            def program(guarded):
                def phase1(s):
                    a, own, carry = s.a, second_turn(s.c), first_turn(s.b)

                    def relu(fb, turn=own):
                        if turn is not None:
                            f_relu(turn, fb)

                    def kv(t):
                        act.wait_ge(a_kv, a * NT + t + 1)
                        src, v_at = Q[2 + t % 2], D
                        if t < NT - 1:
                            if needed(a * (NT - 1) + t - 1):
                                act.wait_ge(a_kt_s, a * (NT - 1) + t - 1)
                            if t == 0 and needed(a * 4):
                                act.wait_ge(a_ph, a * 4)
                            act.activation(a_ek[:, t % 2, :], src[:, 0:D], ACT.Exp).then_inc(a_ek_s, 1)
                            act.activation(a_relu[:, t % 2, 0:D], src[:, 0:D], ACT.Relu).then_inc(a_rk_s, 1)
                        else:
                            v_at = 0
                        if t == 0 and needed(a * NT):
                            act.wait_ge(a_o, a * NT)
                        act.activation(a_v[:, t, :, 0:HD], src[:, v_at:v_at + D].rearrange("p (h j) -> p h j", h=H),
                                       ACT.Copy).then_inc(a_v_s, 1)

                    def q_exp(m):
                        act.wait_ge(a_qk, a * 4 + m + 1)
                        if m == 0:
                            act.wait_ge(a_kt_s, (a + 1) * (NT - 1))
                        if needed(a * 4 + m - 1):
                            act.wait_ge(a_ph, a * 4 + m - 1)
                        act.activation(a_eq[:, m % 2, :], Q[m % 2][:], ACT.Exp).then_inc(a_eq_s, 1)
                        act.activation(a_relu[:, m % 2, :], Q[m % 2][:], ACT.Relu).then_inc(a_rq_s, 1)

                    def y_hi(ch):
                        act.wait_ge(a_t, a * NT + ch + 1)
                        if needed(a * NT + ch):
                            act.wait_ge(a_p, a * NT + ch)
                        act.activation(a_yh[:], Q[2][:, 0:D].rearrange("p (k n) -> p k n", k=KB), ACT.Copy).then_inc(a_h, 1)

                    if a is None:
                        alone(own, carry, s.last)
                        if s.b is not None:
                            norm_for_b(s)
                        return
                    kv(0)
                    kv(1)
                    relu(FB - 1, carry)
                    kv(2)
                    if own is not None:
                        f_norm(own)
                    kv(3)
                    q_exp(0)
                    q_exp(1)
                    relu(0)
                    q_exp(2)
                    q_exp(3)
                    relu(1)
                    relu(2)
                    for ch in range(NT):
                        if ch == NT - 1 and s.b is not None:
                            norm_for_b(s)
                        y_hi(ch)
                        relu(3 + ch)

                def phase2(s):
                    b, own, carry = s.b, first_turn(s.a), second_turn(s.c)

                    def relu(fb, turn=own):
                        if turn is not None:
                            f_relu(turn, fb)

                    def squares(t):
                        act.wait_ge(b_qkv, b * NT + t + 1)
                        if needed(b * NT + t - 1):
                            act.wait_ge(b_ss_s, b * NT + t - 1)
                        act.activation(b_sq[:, t % 2], Q[QKV_BANK[t]][:, 0:QK], ACT.Square).then_inc(b_sq_s, 1)
                        if t == 0 and needed(b * NBL):
                            act.wait_ge(b_o, b * NBL)
                        act.activation(b_v[:, t, :, 0:HD], Q[QKV_BANK[t]][:, QK:NB].rearrange("p (h j) -> p h j", h=KVH),
                                       ACT.Copy).then_inc(b_v_s, 1)

                    def stack_hi(t):
                        act.wait_ge(b_qr_s, b * NT + t + 1)
                        if needed(b * 12 + 3 * t - 3):
                            act.wait_ge(b_t, b * 12 + 3 * t - 3)
                        act.activation(b_qs[:, t % 2, :, 0:2, :], b_qr[:, t % 2, 0:H, :].unsqueeze(2).broadcast_to([P, H, 2, HD]),
                                       ACT.Copy).then_inc(b_hi, 1)
                        act.activation(b_ks[:, t % 2, :, 0::2, :], b_qr[:, t % 2, H:, :].unsqueeze(2).broadcast_to([P, KVH, 2, HD]),
                                       ACT.Copy).then_inc(b_hi, 1)

                    def evacuate(t):
                        if t == 0 and needed(b * 2 * NBL):
                            act.wait_ge(b_s, b * 2 * NBL)
                        for j in range(3):
                            act.wait_ge(b_t, b * 12 + 3 * t + j + 1)
                            if j < 2:
                                act.activation(b_qT[:, j, 2 * t:2 * t + 2, :].rearrange("p e (r q) -> p r e q", r=REP),
                                               Q[TURN_BANK[(3 * t + j) % 4]][:, :].rearrange("p (r e q) -> p r e q", r=REP, e=2), ACT.Copy).then_inc(b_te, 1)
                            else:
                                act.activation(b_kT[:, :, t * P:(t + 1) * P],
                                               Q[TURN_BANK[(3 * t + j) % 4]][:, 0:2 * P].rearrange("p (r n) -> p r n", r=2), ACT.Copy).then_inc(b_te, 1)

                    def exps(bl):
                        nk = W if bl == 0 else P
                        j = b * NBL + bl
                        if needed(j - 1):
                            act.wait_ge(b_o, j - 1)
                        for g2 in range(2):
                            act.wait_ge(b_s, j * 2 + g2 + 1)
                            act.activation(b_p[0:nk, bl % 2, g2, :], Q[g2][0:nk, :], ACT.Exp).then_inc(b_ex, 1)

                    def y_hi(t):
                        act.wait_ge(b_t2, b * NT + t + 1)
                        if needed(b * NT + t):
                            act.wait_ge(b_pp, b * NT + t)
                        act.activation(b_yh[:].rearrange("p r (e q) -> p r e q", e=2),
                                       Q[2][:, 0:D].rearrange("p (e r q) -> p r e q", e=2, r=2), ACT.Copy).then_inc(b_h2, 1)

                    if b is None:
                        alone(own, carry, False)
                        norm_for_a(s)
                        return
                    squares(0)
                    squares(1)
                    squares(2)
                    squares(3)
                    relu(FB - 1, carry)
                    if own is not None:
                        f_norm(own)
                    stack_hi(0)
                    relu(0)
                    stack_hi(1)
                    evacuate(0)
                    stack_hi(2)
                    evacuate(1)
                    relu(1)
                    stack_hi(3)
                    evacuate(2)
                    evacuate(3)
                    exps(0)
                    relu(2)
                    for t in range(NT):
                        exps(2 * t + 1)
                        if 2 * t + 2 < NBL:
                            exps(2 * t + 2)
                        elif s.next_a is not None:
                            norm_for_a(s)
                        y_hi(t)
                        relu(3 + t)

                norm_hi(at, 0, Q)
                steps(act, phase1, phase2)

            both_ways(act, program)


        @block.vector
        def _(dve):
            dve.wait_ge(loaded, 16 * N_LOADS)
            dve.tensor_reduce(gsum[:, 0:1], st_w1, X, ALU.add, apply_absolute_value=True).then_inc(setup, 1)
            dve.tensor_reduce(gsum[:, 1:2], st_w2, X, ALU.add, apply_absolute_value=True).then_inc(setup, 1)
            n = 0
            pairs = [(wqkv_h, wqkv_l, st_a[:, 0:KB * 3 * D], KB), (wout_h, wout_l, st_a[:, KB * 3 * D:KB * 4 * D], KB),
                     (wb_h, wb_l, st_wb, KB)]
            for hi, _, src, k in pairs:
                dve.tensor_copy(hi[:], src.rearrange("p (k n) -> p k n", k=k)).then_inc(prepared, 1)
                n += 1
            dve.tensor_copy(b2_h[:], b2f[:]).then_inc(prepared, 1)
            n += 1
            dve.wait_ge(prepared, n)
            for hi, lo, src, k in pairs:
                dve.tensor_tensor(lo[:], src.rearrange("p (k n) -> p k n", k=k), hi[:], ALU.subtract).then_inc(prepared, 1)
                n += 1
            dve.tensor_tensor(b2_l[:], b2f[:], b2_h[:], ALU.subtract).then_inc(prepared, 1)
            n += 1
            wo = st_wo
            mixed = x3[:, 0:2, :]
            for i in range(2):
                dve.tensor_scalar(mixed[:, i, :], wo[:, 0, :], mixc[:, i:i + 1], None, ALU.mult).then_inc(setup, 1)
            dve.wait_ge(setup, 4)
            for i in range(2):
                dve.scalar_tensor_tensor(out=mixed[:, i, :], in0=wo[:, 1, :], scalar=mixc[:, 2 + i:3 + i],
                                         in1=mixed[:, i, :], op0=ALU.mult, op1=ALU.add).then_inc(setup, 1)
            dve.wait_ge(setup, 6)
            dve.tensor_copy(wob_h[:], mixed).then_inc(prepared, 1)
            n += 1
            dve.wait_ge(prepared, n)
            dve.tensor_tensor(wob_l[:], mixed, wob_h[:], ALU.subtract).then_inc(prepared, 1)
            n += 1
            dve.wait_ge(setup_pe, 1)
            dve.tensor_scalar(thr[:, 0:2], Q[0][:, 0:2], 1.0 / (FF * D), Q_EPS, ALU.mult, ALU.add).then_inc(setup, 1)
            dve.wait_ge(setup, 7)
            dve.tensor_scalar(thr[:, 2:4], thr[:, 0:2], -0.5, None, ALU.mult).then_inc(setup, 1)
            dve.wait_ge(setup, 8)
            dve.tensor_scalar(thr[:, 0:2], thr[:, 0:2], 0.5, None, ALU.mult).then_inc(setup, 1)
            dve.wait_ge(setup, 9)
            below = [t[:].rearrange("p k n -> p (k n)") for t in (x1, x2, at.xn, ff.xn)]
            m = 9
            for j, (dst, src, k) in enumerate(((w1t, st_w1, KB), (w2t, st_w2, FB))):
                for half in range(2):
                    part = slice(half * 1024, (half + 1) * 1024)
                    dve.tensor_scalar(below[2 * j + half], src[:, part], thr[:, 2 + j:3 + j], None, ALU.is_lt).then_inc(setup, 1)
                m += 2
                dve.wait_ge(setup, m)
                flat = dst[:].rearrange("p k n -> p (k n)")
                for half in range(2):
                    part = slice(half * 1024, (half + 1) * 1024)
                    dve.scalar_tensor_tensor(out=flat[:, part], in0=src[:, part], scalar=thr[:, j:j + 1], in1=below[2 * j + half],
                                             op0=ALU.is_gt, op1=ALU.subtract).then_inc(prepared, 1)
                    n += 1
            dve.tensor_copy(ident_b[:], ident).then_inc(prepared, 1)
            dve.tensor_copy(ident_r[:], ident).then_inc(prepared, 1)
            dve.tensor_scalar(neg_ident[:], ident, -1.0, None, ALU.mult).then_inc(prepared, 1)
            dve.tensor_copy(kmask[:, 0, :], C["kodd"]).then_inc(prepared, 1)
            dve.tensor_copy(kmask[:, 1, :], C["keven"]).then_inc(prepared, 1)
            dve.tensor_copy(qmask[:, 0, :], C["qodd"]).then_inc(prepared, 1)
            dve.wait_ge(ones_set, 5)
            dve.tensor_copy(qmask[:, 1, :], C["qeven"]).then_inc(prepared, 1)
            dve.tensor_copy(ones_r[:], ones_f[0:1, :]).then_inc(prepared, 1)
            dve.tensor_reduce(wide_f[:, 0:1], gains[:, 0:H], X, ALU.max, apply_absolute_value=True).then_inc(setup, 1)
            dve.wait_ge(setup, m + 1)
            dve.tensor_scalar(wide_f[:, 1:2], wide_f[:, 0:1], SAFE_SCORE / HD ** 0.5, None, ALU.is_le).then_inc(setup, 1)
            dve.wait_ge(setup, m + 2)
            dve.tensor_scalar(wide_i[:], wide_f[:, 1:2], -1.0, 1.0, ALU.mult, ALU.add).then_inc(prepared, 1)
            dve.tensor_scalar(gains[:, 0:H], gains[:, 0:H], HD ** -0.5, None, ALU.mult).then_inc(prepared, 1)
            assert n + 10 == N_PREPARED

            def norm_stats(n, turn, src, tiles):
                if tiles[0] == 0 and needed(turn * NT):
                    dve.wait_ge(n.stats, turn * NT)
                    dve.wait_ge(n.ready, turn)
                    dve.wait_ge(n.normed, turn * NT)
                for t in tiles:
                    dve.bn_stats(n.st[:, t, :], src[:, t, :]).then_inc(n.bn, 1)
                for t in tiles:
                    dve.wait_ge(n.bn, turn * NT + t + 1)
                    dve.sem_inc(dve_gate)
                    dve.bn_aggr(n.mv[:, t, :], n.st[:, t, :]).then_inc(n.stats, 1)

            def norm_apply(n, turn, src):
                dve.wait_ge(n.ready, turn + 1)
                if needed(turn * 2):
                    dve.wait_ge(n.turned, turn * 2)
                for t in range(NT):
                    dve.tensor_scalar(n.xn[:, t, :], src[:, t, :], n.mv[:, t, 0:1], n.rstd[:, t:t + 1],
                                      ALU.subtract, ALU.mult).then_inc(n.normed, 1)

            def norm_lo(n, turn, banks):
                for hf in range(2):
                    dve.wait_ge(n.hi, turn * 2 + hf + 1)
                    dve.tensor_tensor(n.xl[:, :, hf * D:(hf + 1) * D], banks[hf][:, :].rearrange("p (k n) -> p k n", k=KB),
                                      n.xh[:, :, hf * D:(hf + 1) * D], ALU.subtract).then_inc(n.lo, 1)

            def f_lo_part(turn, fb):
                if turn is not None:
                    dve.wait_ge(f_act, turn * FB + fb + 1)
                    if needed(turn * FB + fb - 1):
                        dve.wait_ge(f_w2, turn * FB + fb - 1)
                    dve.tensor_tensor(f_hl[:, fb % 2, :], f_r[:, fb % 2, :], f_hh[:, fb % 2, :], ALU.subtract).then_inc(f_lo, 1)

            def f_apply(turn, src):
                if turn is not None:
                    norm_apply(ff, turn, src)

            def f_norm_lo(turn):
                if turn is not None:
                    norm_lo(ff, turn, HID)

            def f_finish(turn, src, dst):
                if turn is not None:
                    dve.wait_ge(f_w2, (turn + 1) * FB)
                    for y in range(2):
                        dve.tensor_tensor(dst[:, 2 * y:2 * y + 2, :], Y[y][:, :].rearrange("p (t n) -> p t n", t=2),
                                          src[:, 2 * y:2 * y + 2, :], ALU.add).then_inc(f_out, 1)

            def finish_first(s):
                if s.b is not None:
                    if needed(s.b * NT):
                        dve.wait_ge(b_out, s.b * NT)
                    f_finish(first_turn(s.b), x1, x2)

            def finish_second(s):
                if s.c is not None:
                    f_finish(second_turn(s.c), x3, x3)

            def stats_for_b(s):
                dve.wait_ge(f_out, 2 * (first_turn(s.b) + 1))
                norm_stats(at, second_turn(s.b), x2, range(NT))

            def stats_for_a(s):
                dve.wait_ge(x_in, (s.next_a + 1) * 16)
                norm_stats(at, first_turn(s.next_a), x0, range(NT))

            def alone(own, src, carry, finish, stats, apply, lo, last):
                f_lo_part(carry, FB - 2)
                f_apply(own, src)
                f_lo_part(carry, FB - 1)
                if carry is not None:
                    finish()
                if stats is not None:
                    stats()
                    apply()
                f_norm_lo(own)
                if own is not None:
                    for k in range(FB if last else FB - 2):
                        f_lo_part(own, k)
                if lo is not None:
                    lo()

            def program(guarded):
                def phase1(s):
                    a, own, carry = s.a, second_turn(s.c), first_turn(s.b)
                    turn_b = second_turn(s.b)

                    def k_phi(t):
                        dve.wait_ge(a_rk_s, a * (NT - 1) + t + 1)
                        if t == 0 and needed(a * 3):
                            dve.wait_ge(a_u, a * 3)
                        dve.scalar_tensor_tensor(out=a_kt[:, t, :], in0=a_ek[:, t % 2, :], scalar=1.0, in1=a_relu[:, t % 2, 0:D],
                                                 op0=ALU.min, op1=ALU.add).then_inc(a_kt_s, 1)

                    def phi(m):
                        dve.wait_ge(a_rq_s, a * 4 + m + 1)
                        if m == 0 and needed(a * NT):
                            dve.wait_ge(a_o, a * NT)
                        dst = (a_qT if m < 2 else a_kT)[:, m % 2, :]
                        dve.scalar_tensor_tensor(out=dst, in0=a_eq[:, m % 2, :], scalar=1.0, in1=a_relu[:, m % 2, :],
                                                 op0=ALU.min, op1=ALU.add).then_inc(a_ph, 1)

                    def by_parity(m):
                        dve.wait_ge(a_ph, a * 4 + m + 1)
                        for e in range(2):
                            dve.tensor_scalar(a_qz[:, m, e, :], a_qT[:, m, :], C["parity"][:, e:e + 1], None,
                                              ALU.mult).then_inc(a_qz_s, 1)

                    def mask(ch, tiles=range(4)):
                        if tiles[0] == 0 and needed(a * NT + ch - 1):
                            dve.wait_ge(a_o, a * NT + ch - 1)
                        for r in tiles:
                            dve.wait_ge(a_sc, a * 16 + 4 * ch + r + 1)
                            dve.tensor_tensor(a_s[:, ch % 2, r, :].rearrange("p (h q) -> p h q", h=4),
                                              Q[r % 2][:, :].rearrange("p (h q) -> p h q", h=4),
                                              causal.unsqueeze(1).broadcast_to([P, 4, P]), ALU.mult).then_inc(a_sm, 1)

                    def state(ch):
                        dve.wait_ge(a_u, a * 3 + ch + 1)
                        if needed(a * NT + ch):
                            dve.wait_ge(a_o, a * NT + ch)
                        dve.tensor_tensor(a_state[:, ch % 2, :].rearrange("p (k n) -> p k n", k=KB),
                                          Q[3][:, 0:KB * HB * HV].rearrange("p (k n) -> p k n", k=KB),
                                          C["heads"].unsqueeze(1).broadcast_to([P, KB, HB * HV]), ALU.mult).then_inc(a_st, 1)

                    def normalise(ch):
                        o = Q[2][:, 0:H * HV].rearrange("p (h j) -> p h j", h=H)
                        steps_before = a * 2 * NT + 2 * ch
                        dve.wait_ge(a_o, a * NT + ch + 1)
                        dve.tensor_scalar(a_den[:, 0, :], o[:, :, HD], A_EPS, None, ALU.add).then_inc(a_dn, 1)
                        dve.wait_ge(a_dn, steps_before + 1)
                        dve.reciprocal(a_den[:, 1, :], a_den[:, 0, :]).then_inc(a_dn, 1)
                        dve.wait_ge(a_dn, steps_before + 2)
                        if needed(a * NT + ch):
                            dve.wait_ge(a_t, a * NT + ch)
                        dve.tensor_tensor(a_y[:].rearrange("p (h j) -> p h j", h=H), o[:, :, 0:HD],
                                          a_den[:, 1, :].unsqueeze(2).broadcast_to([P, H, HD]), ALU.mult).then_inc(a_yn, 1)

                    def y_lo(ch):
                        dve.wait_ge(a_h, a * NT + ch + 1)
                        dve.tensor_tensor(a_yl[:], Q[2][:, 0:D].rearrange("p (k n) -> p k n", k=KB), a_yh[:],
                                          ALU.subtract).then_inc(a_l, 1)

                    def residual(ch):
                        dve.wait_ge(a_p, a * NT + ch + 1)
                        if ch == 0 and carry is not None:
                            dve.wait_ge(f_out, (carry + 1) * 2)
                        dve.tensor_tensor(x1[:, ch, :], Q[2][:, 0:D], x0[:, ch, :], ALU.add).then_inc(a_out, 1)

                    def f1_stats(ch):
                        dve.wait_ge(a_out, a * NT + ch + 1)
                        norm_stats(ff, first_turn(a), x1, [ch])

                    if a is None:
                        if s.last:
                            alone(own, x3, None, None, None, None, None, True)
                            finish_second(s)
                        else:
                            alone(own, x3, carry, lambda: finish_first(s), lambda: stats_for_b(s),
                                  lambda: norm_apply(at, turn_b, x2), lambda: norm_lo(at, turn_b, Q), False)
                        return
                    f_lo_part(carry, FB - 2)
                    f_apply(own, x3)
                    k_phi(0)
                    k_phi(1)
                    f_lo_part(carry, FB - 1)
                    k_phi(2)
                    f_norm_lo(own)
                    phi(0)
                    phi(1)
                    by_parity(1)
                    finish_first(s)
                    f_lo_part(own, 0)
                    phi(2)
                    phi(3)
                    mask(0)
                    state(0)
                    f_lo_part(own, 1)
                    for ch in range(NT):
                        if ch + 1 < NT:
                            mask(ch + 1, (0, 1))
                        f_lo_part(own, 2 + ch)
                        if ch + 1 < NT:
                            mask(ch + 1, (2, 3))
                        normalise(ch)
                        y_lo(ch)
                        if ch == NT - 1 and s.b is not None:
                            norm_lo(at, turn_b, Q)
                        residual(ch)
                        f1_stats(ch)
                        if ch + 1 < NT - 1:
                            state(ch + 1)
                        if s.b is not None:
                            if ch == 1:
                                stats_for_b(s)
                            if ch == 2:
                                norm_apply(at, turn_b, x2)

                def phase2(s):
                    b, own, carry = s.b, first_turn(s.a), second_turn(s.c)
                    turn_a = first_turn(s.next_a)

                    def sums(t):
                        dve.wait_ge(b_sq_s, b * NT + t + 1)
                        if t == 0 and needed(b):
                            dve.wait_ge(b_rs_s, b)
                        dve.tensor_reduce(b_ss[:, t, :], b_sq[:, t % 2].rearrange("p (h j) -> p h j", j=HD), X,
                                          ALU.add).then_inc(b_ss_s, 1)

                    def roots():
                        step = b * 12
                        dve.wait_ge(b_ss_s, (b + 1) * NT)
                        dve.tensor_scalar(b_var[:], b_ss[:], 1.0 / HD, RMS_EPS, ALU.mult, ALU.add).then_inc(b_ch, 1)
                        dve.wait_ge(b_ch, step + 1)
                        dve.tensor_scalar(b_root[:].bitcast(mybir.dt.int32), b_var[:].bitcast(mybir.dt.int32),
                                          -0.5, float(ROOT_GUESS), ALU.mult, ALU.add).then_inc(b_ch, 1)
                        dve.tensor_scalar(b_half[:], b_var[:], -0.5, None, ALU.mult).then_inc(b_ch, 1)
                        for n in range(3):
                            dve.wait_ge(b_ch, step + 3 * n + 3)
                            dve.tensor_tensor(b_step[:], b_root[:], b_root[:], ALU.mult).then_inc(b_ch, 1)
                            dve.wait_ge(b_ch, step + 3 * n + 4)
                            dve.tensor_tensor(b_step[:], b_step[:], b_half[:], ALU.mult).then_inc(b_ch, 1)
                            dve.wait_ge(b_ch, step + 3 * n + 5)
                            dve.scalar_tensor_tensor(out=b_root[:], in0=b_step[:], scalar=1.5, in1=b_root[:],
                                                     op0=ALU.add, op1=ALU.mult).then_inc(b_ch, 1)
                        dve.wait_ge(b_ch, step + 12)
                        if needed(b * NT):
                            dve.wait_ge(b_qn_s, b * NT)
                        dve.tensor_tensor(b_rs[:], b_root[:], gains[:].unsqueeze(1).broadcast_to([P, NT, H + KVH]),
                                          ALU.mult).then_inc(b_rs_s, 1)

                    def norm_qk(t):
                        dve.wait_ge(b_rs_s, b + 1)
                        dve.wait_ge(b_v_s, b * NT + t + 1)
                        if needed(b * NT + t - 1):
                            dve.wait_ge(b_ro, b * NT + t - 1)
                            dve.wait_ge(b_rc_s, b * NT + t - 1)
                        dve.tensor_tensor(b_qn[:, t % 2], Q[QKV_BANK[t]][:, 0:QK].rearrange("p (h j) -> p h j", j=HD),
                                          b_rs[:, t, :].unsqueeze(2).broadcast_to([P, H + KVH, HD]), ALU.mult).then_inc(b_qn_s, 1)

                    def cosines(t):
                        j = b * NT + t
                        dve.wait_ge(b_qn_s, j + 1)
                        if needed(j - 1):
                            dve.wait_ge(b_lo, j - 1)
                        dve.tensor_tensor(b_qr[:, t % 2], b_qn[:, t % 2], table("cos", t, 0, HD), ALU.mult).then_inc(b_rc_s, 1)

                    def rotate(t):
                        j = b * NT + t
                        dve.wait_ge(b_rc_s, j + 1)
                        dve.wait_ge(b_ro, j + 1)
                        dve.tensor_tensor(b_qr[:, t % 2], b_qr[:, t % 2], b_rsn[:, t % 2], ALU.add).then_inc(b_qr_s, 1)

                    def even_v(t):
                        dve.tensor_copy(b_vm[0:W, t, :, 0:HD], b_v[0:W, t, :, 0:HD]).then_inc(b_vm_s, 1)
                        if t + 1 < NT:
                            dve.tensor_copy(b_vm[W:P, t + 1, :, 0:HD], b_v[W:P, t, :, 0:HD]).then_inc(b_vm_s, 1)

                    def stack_lo(t):
                        dve.wait_ge(b_hi, (b * NT + t + 1) * 2)
                        dve.tensor_tensor(b_qs[:, t % 2, :, 2:4, :], b_qr[:, t % 2, 0:H, :].unsqueeze(2).broadcast_to([P, H, 2, HD]),
                                          b_qs[:, t % 2, :, 0:2, :], ALU.subtract)
                        dve.tensor_tensor(b_ks[:, t % 2, :, 1::2, :], b_qr[:, t % 2, H:, :].unsqueeze(2).broadcast_to([P, KVH, 2, HD]),
                                          b_ks[:, t % 2, :, 0::2, :], ALU.subtract).then_inc(b_lo, 1)

                    def even_keys(t):
                        dve.wait_ge(b_te, b * 12 + 3 * t + 3)
                        if t == 0 and needed(b * 2 * NBL):
                            dve.wait_ge(b_s, b * 2 * NBL)
                        dve.tensor_copy(b_kTm[:, :, t, 0:W], b_kT[:, :, t * P:t * P + W]).then_inc(b_km, 1)
                        if t + 1 < NT:
                            dve.tensor_copy(b_kTm[:, :, t + 1, W:P], b_kT[:, :, t * P + W:(t + 1) * P]).then_inc(b_km, 1)

                    def maxima(bl):
                        nk = W if bl == 0 else P
                        j = b * NBL + bl
                        if needed(j * 2 - 2):
                            dve.wait_ge(b_s, j * 2 - 2)
                        for g2 in range(2):
                            dve.wait_ge(b_mm, j * 2 + g2 + 1)
                            dve.tensor_reduce(b_m[:, bl % 2, 4 * g2:4 * g2 + 4],
                                              Q[g2][:, 0:4 * nk].rearrange("p (u k) -> p u k", u=4), X, ALU.max).then_inc(b_mx, 1)

                    def normalise(bl):
                        j = b * NBL + bl
                        o = Q[2 + bl % 2][:, 0:2 * KVH * HV].rearrange("p (h j) -> p h j", j=HV)
                        dve.wait_ge(b_o, j + 1)
                        dve.reciprocal(b_den[:, bl % 2, :], o[:, :, HD]).then_inc(b_dn, 1)
                        dve.wait_ge(b_dn, j + 1)
                        if needed(b * NT + bl // 2):
                            dve.wait_ge(b_t2, b * NT + bl // 2)
                        dve.tensor_tensor(b_y[:, bl % 2, :].rearrange("p (h j) -> p h j", j=HD), o[:, :, 0:HD],
                                          b_den[:, bl % 2, :].unsqueeze(2).broadcast_to([P, 2 * KVH, HD]), ALU.mult).then_inc(b_yn, 1)

                    def y_lo(t):
                        dve.wait_ge(b_h2, b * NT + t + 1)
                        dve.tensor_tensor(b_yl[:].rearrange("p r (e q) -> p r e q", e=2),
                                          Q[2][:, 0:D].rearrange("p (e r q) -> p r e q", e=2, r=2),
                                          b_yh[:].rearrange("p r (e q) -> p r e q", e=2), ALU.subtract).then_inc(b_l2, 1)

                    def residual(t):
                        dve.wait_ge(b_pp, b * NT + t + 1)
                        if t == 0 and needed(b * 16):
                            dve.wait_ge(stored, b * 16)
                        dve.tensor_tensor(x3[:, t, :], Q[2][:, 0:D], x2[:, t, :], ALU.add).then_inc(b_out, 1)

                    def f2_stats(t):
                        dve.wait_ge(b_out, b * NT + t + 1)
                        norm_stats(ff, second_turn(b), x3, [t])

                    if b is None:
                        alone(own, x1, None, None, lambda: stats_for_a(s), lambda: norm_apply(at, turn_a, x0),
                              lambda: norm_lo(at, turn_a, Q), False)
                        return
                    f_lo_part(carry, FB - 2)
                    sums(0)
                    sums(1)
                    f_apply(own, x1)
                    sums(2)
                    sums(3)
                    roots()
                    norm_qk(0)
                    cosines(0)
                    norm_qk(1)
                    f_lo_part(carry, FB - 1)
                    rotate(0)
                    norm_qk(2)
                    f_norm_lo(own)
                    stack_lo(0)
                    cosines(1)
                    rotate(1)
                    norm_qk(3)
                    finish_second(s)
                    f_lo_part(own, 0)
                    cosines(2)
                    stack_lo(1)
                    rotate(2)
                    cosines(3)
                    rotate(3)
                    stack_lo(2)
                    f_lo_part(own, 1)
                    stack_lo(3)
                    for t in range(NT):
                        even_v(t)
                        even_keys(t)
                    if guarded:
                        maxima(0)
                    for t in range(NT):
                        if guarded:
                            maxima(2 * t + 1)
                        f_lo_part(own, 2 + t)
                        normalise(2 * t)
                        if guarded and 2 * t + 2 < NBL:
                            maxima(2 * t + 2)
                        normalise(2 * t + 1)
                        y_lo(t)
                        if t == NT - 1 and s.next_a is not None:
                            norm_lo(at, turn_a, Q)
                        residual(t)
                        f2_stats(t)
                        if s.next_a is not None:
                            if t == 1:
                                stats_for_a(s)
                            if t == 2:
                                norm_apply(at, turn_a, x0)

                dve.wait_ge(x_in, 16)
                norm_stats(at, 0, x0, range(NT))
                norm_apply(at, 0, x0)
                norm_lo(at, 0, Q)
                steps(dve, phase1, phase2)

            both_ways(dve, program)


        @block.gpsimd
        def _(pool):
            pool.memset(ones_f[:], 1.0).then_inc(ones_set, 1)
            pool.memset(mhalf[:], -0.5).then_inc(ones_set, 1)
            pool.memset(gains[:, H:], 1.0).then_inc(ones_set, 1)
            pool.memset(a_v[:, :, :, HD:HV], 1.0).then_inc(ones_set, 1)
            pool.memset(b_v[:, :, :, HD:HV], 1.0)
            pool.memset(b_vm[:, :, :, HD:HV], 1.0).then_inc(ones_set, 1)
            def root(tmp, chain, start, dst, ready):
                v, y, u = tmp[:, 0, :], tmp[:, 1, :], tmp[:, 2, :]
                pool.wait_ge(chain, start + 1)
                pool.tensor_tensor(y, v, mhalf[:], ALU.pow).then_inc(chain, 1)
                pool.wait_ge(chain, start + 2)
                pool.tensor_tensor(u, y, y, ALU.mult).then_inc(chain, 1)
                pool.wait_ge(chain, start + 3)
                pool.tensor_tensor(u, u, v, ALU.mult).then_inc(chain, 1)
                pool.wait_ge(chain, start + 4)
                pool.sem_inc(pool_gate)
                pool.tensor_scalar(u, u, -0.5, 1.5, ALU.mult, ALU.add).then_inc(chain, 1)
                pool.wait_ge(chain, start + 5)
                last = pool.tensor_tensor(dst, y, u, ALU.mult)
                last.then_inc(ready, 1)

            def norm_rstd(n, turn):
                pool.wait_ge(n.stats, (turn + 1) * NT)
                if needed(turn * NT):
                    pool.wait_ge(n.normed, turn * NT)
                pool.sem_inc(pool_gate)
                pool.tensor_scalar(n.tmp[:, 0, :], n.mv[:, :, 1], 1.0, LN_EPS, ALU.mult, ALU.add).then_inc(n.chain, 1)
                root(n.tmp, n.chain, turn * 5, n.rstd[:], n.ready)

            def program(guarded):
                def phase1(s):
                    a = s.a

                    def by_parity(m):
                        for e in range(2):
                            pool.wait_ge(a_ph, a * 4 + m + 1)
                            pool.sem_inc(pool_gate)
                            pool.tensor_scalar(a_qz[:, m, e, :], a_qT[:, m, :], C["parity"][:, e:e + 1], None,
                                               ALU.mult).then_inc(a_qz_s, 1)

                    if a is not None:
                        by_parity(0)
                    if s.b is not None:
                        norm_rstd(at, second_turn(s.b))
                    if a is not None:
                        norm_rstd(ff, first_turn(a))

                def phase2(s):
                    b = s.b

                    def sines(t):
                        j = b * NT + t
                        qn, dst = b_qn[:, t % 2], b_rsn[:, t % 2]
                        pool.wait_ge(b_qn_s, j + 1)
                        if needed(j - 1):
                            pool.wait_ge(b_qr_s, j - 1)
                        pool.tensor_tensor(dst[:, :, 0:HD // 2], qn[:, :, HD // 2:], table("sin", t, 0, HD // 2), ALU.mult)
                        pool.tensor_tensor(dst[:, :, HD // 2:], qn[:, :, 0:HD // 2], table("sin", t, HD // 2, HD),
                                           ALU.mult).then_inc(b_ro, 1)

                    if b is not None:
                        for t in range(NT):
                            sines(t)
                    if s.next_a is not None:
                        norm_rstd(at, first_turn(s.next_a))
                    if b is not None:
                        norm_rstd(ff, second_turn(b))

                norm_rstd(at, 0)
                steps(pool, phase1, phase2)

            both_ways(pool, program)



def arrays_of(x, W_qkv, W_out, Wq, Wk, Wv, Wo, q_gain, pair_mix, W1, b1, W2, b2):
    wq = Wq.T.reshape(D, 2, 2, REP, HD).transpose(0, 1, 3, 2, 4).reshape(D, D)
    return {
        "x": x,
        "w_qkv": W_qkv,
        "w_out": W_out,
        "w_b": np.concatenate([wq, Wk.T, Wv.T], 1),
        "wo_b": Wo.T.reshape(H // 2, 2, HD, D).transpose(1, 0, 2, 3).reshape(2, P, D),
        "gain": q_gain.reshape(2, 2, REP).transpose(0, 2, 1).reshape(H),
        "mix": np.repeat(pair_mix.reshape(H // 2, 4), HD, axis=0),
        "w1": W1.T,
        "b1": b1.reshape(FB, P).T,
        "w2": W2.T,
        "b2": b2.reshape(1, D),
        "const": constants(),
    }


def kernel(**inputs):
    import concourse.bacc as bacc
    from concourse.bass_utils import run_bass_kernel_spmd

    g = {k: np.asarray(v) for k, v in inputs.items()}
    laid = arrays_of(g["L0_attn_a_x"], g["L0_attn_a_W_qkv"], g["L0_attn_a_W_out"], g["L0_attn_b_Wq"], g["L0_attn_b_Wk"],
                     g["L0_attn_b_Wv"], g["L0_attn_b_Wo"], g["L0_attn_b_q_gain"], g["L0_attn_b_pair_mix"],
                     g["L0_ffn_W1"], g["L0_ffn_b1"], g["L0_ffn_W2"], g["L0_ffn_b2"])
    nc = bacc.Bacc("TRN2", target_bir_lowering=False, num_devices=1)
    arrays = {f"in_{n}": np.ascontiguousarray(a) for n, a in laid.items()}
    aps = [nc.dram_tensor(n, a.shape, F32, kind="ExternalInput").ap() for n, a in arrays.items()]
    out = nc.dram_tensor("out", (NSEQ, S, D), F32, kind="ExternalOutput").ap()
    build(nc, *aps, out)
    r = run_bass_kernel_spmd(nc, [arrays], core_ids=[0])
    return r.results[0]["out"]
```
